# Optimizing a Trainium2 kernel written in Bass

```python
import numpy as np
import jax
import jax.numpy as jnp

def _softmax(x, axis=-1):
    return jax.nn.softmax(x, axis=axis)

def _gelu(x):
    return jax.nn.gelu(x, approximate=True)

def _silu(x):
    return jax.nn.silu(x)

def _sigmoid(x):
    return jax.nn.sigmoid(x)

def _layernorm(x, axis=-1, eps=1e-05):
    m = jnp.mean(x, axis=axis, keepdims=True)
    v = jnp.var(x, axis=axis, keepdims=True)
    return (x - m) / jnp.sqrt(v + eps)

def _scatter_add(tgt, idx, src, axis=0):
    return tgt.at[idx].add(src)

def _segment_sum(src, seg, n):
    return jax.ops.segment_sum(src, seg, n)
kernel_name = 'mk_flamingo_gated_d2_seqx_r8_b7080c'

def setup_inputs(seed: int=0):
    np.random.seed(seed)
    _w = jnp.asarray

    def _rec_inputs():
        import jax
        import jax.numpy as jnp
        _rk = jax.random.key(seed)
        x = 0.000341 + 1 * jax.random.normal(jax.random.fold_in(_rk, 1), (16, 128, 256), jnp.float32)
        _lenS = 128 - jax.random.randint(jax.random.fold_in(_rk, 7), (16,), 0, max(1, 128 // 4) + 1, jnp.int32)
        _lenS2 = 128 - jax.random.randint(jax.random.fold_in(_rk, 8), (16,), 0, max(1, 128 // 4) + 1, jnp.int32)
        _ctx_2048P = jax.random.normal(jax.random.fold_in(_rk, 11), (16, 16, 256), jnp.float32)
        _ctx_2048c = jax.random.dirichlet(jax.random.fold_in(_rk, 511), 0.3 * jnp.ones((16,), jnp.float32), (16, 128))
        _ctx_2048t = jnp.einsum('bsk,bkd->bsd', _ctx_2048c, _ctx_2048P)
        _ctx_2048t = _ctx_2048t * jax.lax.rsqrt(jnp.mean(jnp.square(_ctx_2048t)) + 1e-12) * 0.953939
        ctx_2048 = -1.47943e-05 + 1.00017 * (_ctx_2048t + 0.3 * jax.random.normal(jax.random.fold_in(_rk, 611), (16, 128, 256), jnp.float32))
        _g = jax.random.normal(jax.random.fold_in(_rk, 9001), (2, 2), jnp.float32)
        _g = jnp.sign(_g) * jnp.maximum(jnp.abs(_g), 1.0) + (_g == 0) * 1.0
        g_xattn = _g[0]
        g_ffn = _g[1]
        return (x, ctx_2048, g_xattn, g_ffn)
    x, ctx_2048, g_xattn, g_ffn = _rec_inputs()

    def _L0_xattn_setup():
        import jax, jax.numpy as jnp
        import numpy as np

        def _wkv(time_decay, time_first, k, v):
            w = -jnp.exp(time_decay)
            u = time_first
            B, T, C = k.shape
            aa = jnp.zeros((B, C), dtype=k.dtype)
            bb = jnp.zeros((B, C), dtype=k.dtype)
            pp = jnp.full((B, C), -1e+38, dtype=k.dtype)

            def step(carry, kv_t):
                aa, bb, pp = carry
                kt, vt = kv_t
                ww = u + kt
                q = jnp.maximum(pp, ww)
                e1 = jnp.exp(pp - q)
                e2 = jnp.exp(ww - q)
                y_t = (e1 * aa + e2 * vt) / (e1 * bb + e2)
                ww2 = pp + w
                q2 = jnp.maximum(ww2, kt)
                e1b = jnp.exp(ww2 - q2)
                e2b = jnp.exp(kt - q2)
                new_carry = (e1b * aa + e2b * vt, e1b * bb + e2b, q2)
                return (new_carry, y_t)
            ks = jnp.transpose(k, (1, 0, 2))
            vs = jnp.transpose(v, (1, 0, 2))
            _, ys = jax.lax.scan(step, (aa, bb, pp), (ks, vs))
            return jnp.transpose(ys, (1, 0, 2))
        key = jax.random.key(seed)
        k1, k2, k3, k4 = jax.random.split(key, 4)
        B, T, C = (8, 128, 256)
        return {'batch_size': B, 'seq_len': T, 'embedding_dim': C, 'time_decay': jax.random.normal(k1, (C,), dtype=jnp.float32), 'time_first': jax.random.normal(k2, (C,), dtype=jnp.float32), 'k': jax.random.normal(k3, (B, T, C), dtype=jnp.float32), 'v': jax.random.normal(k4, (B, T, C), dtype=jnp.float32)}
    _L0_xattn_all = _L0_xattn_setup()
    _L0_xattn_in = {k: v for k, v in _L0_xattn_all.items() if k in ('time_decay', 'time_first')}
    del _L0_xattn_all

    def _L0_ffn_setup():
        import jax, jax.numpy as jnp
        import numpy as np
        HIDDEN = 256
        INTER = 1024
        RETRIEVAL = 128
        NUM_EXPERTS = 512
        NUM_KEYS = 64
        TOP_K = 8
        B, S = (4, 256)
        key = jax.random.key(seed)
        ks = jax.random.split(key, 8)
        sc = 0.02
        return {'hidden_states': jax.random.normal(ks[0], (B, S, HIDDEN), jnp.float32), 'W_q': jax.random.normal(ks[1], (HIDDEN, RETRIEVAL), jnp.float32) * sc, 'keys': jax.random.normal(ks[2], (2, RETRIEVAL // 2, NUM_KEYS), jnp.float32) * sc, 'down_embed': jax.random.normal(ks[3], (NUM_EXPERTS, HIDDEN), jnp.float32) * sc, 'up_embed': jax.random.normal(ks[4], (NUM_EXPERTS, HIDDEN), jnp.float32) * sc, 'gate_w': jax.random.normal(ks[5], (HIDDEN, INTER), jnp.float32) * sc, 'up_w': jax.random.normal(ks[6], (HIDDEN, INTER), jnp.float32) * sc, 'down_w': jax.random.normal(ks[7], (INTER, HIDDEN), jnp.float32) * sc}
    _L0_ffn_all = _L0_ffn_setup()
    _L0_ffn_in = {k: v for k, v in _L0_ffn_all.items() if k in ('W_q', 'keys', 'down_embed', 'up_embed', 'gate_w', 'up_w', 'down_w')}
    del _L0_ffn_all

    def _L1_xattn_setup():
        import jax, jax.numpy as jnp
        import numpy as np
        EPS = 1e-06
        NUM_HEADS = 16

        def _feature_map(x):
            return jnp.where(x > 0, x + 1.0, jnp.exp(x))
        key = jax.random.key(seed)
        ks = jax.random.split(key, 7)
        B, L, S, D = (4, 512, 512, 256)
        sc = 1.0 / np.sqrt(D)
        return {'query': jax.random.normal(ks[0], (B, L, D), jnp.float32), 'kv': jax.random.normal(ks[1], (B, S, D), jnp.float32), 'Wq': jax.random.normal(ks[2], (D, D), jnp.float32) * sc, 'Wg': jax.random.normal(ks[3], (D, D), jnp.float32) * sc, 'bg': jnp.ones((D,), jnp.float32), 'Wkv': jax.random.normal(ks[4], (2 * D, D), jnp.float32) * sc, 'Wo': jax.random.normal(ks[5], (D, D), jnp.float32) * sc}
    _L1_xattn_all = _L1_xattn_setup()
    _L1_xattn_in = {k: v for k, v in _L1_xattn_all.items() if k in ('Wq', 'Wg', 'bg', 'Wkv', 'Wo')}
    del _L1_xattn_all

    def _L1_ffn_setup():
        import jax, jax.numpy as jnp
        import numpy as np
        DIM = 256
        HID = 128
        E = 8
        K = 2
        SHID = HID * 1
        INIT = 0.02
        key = jax.random.key(seed)
        ks = jax.random.split(key, 9)
        return {'x': jax.random.normal(ks[0], (2, 128, DIM), jnp.float32), 'expert_bias': jnp.zeros((E,), jnp.float32), 'gate_w': jax.random.normal(ks[1], (E, DIM), jnp.float32) * INIT, 'w1': jax.random.normal(ks[2], (E, HID, DIM), jnp.float32) * INIT, 'w2': jax.random.normal(ks[3], (E, DIM, HID), jnp.float32) * INIT, 'w3': jax.random.normal(ks[4], (E, HID, DIM), jnp.float32) * INIT, 'sw1': jax.random.normal(ks[5], (SHID, DIM), jnp.float32) * INIT, 'sw2': jax.random.normal(ks[6], (DIM, SHID), jnp.float32) * INIT, 'sw3': jax.random.normal(ks[7], (SHID, DIM), jnp.float32) * INIT}
    _L1_ffn_all = _L1_ffn_setup()
    _L1_ffn_in = {k: v for k, v in _L1_ffn_all.items() if k in ('expert_bias', 'gate_w', 'w1', 'w2', 'w3', 'sw1', 'sw2', 'sw3')}
    del _L1_ffn_all
    return {'x': x, 'ctx_2048': ctx_2048, 'g_xattn': g_xattn, 'g_ffn': g_ffn, 'L0_xattn_time_decay': _L0_xattn_in['time_decay'], 'L0_xattn_time_first': _L0_xattn_in['time_first'], 'L0_ffn_W_q': _L0_ffn_in['W_q'], 'L0_ffn_keys': _L0_ffn_in['keys'], 'L0_ffn_down_embed': _L0_ffn_in['down_embed'], 'L0_ffn_up_embed': _L0_ffn_in['up_embed'], 'L0_ffn_gate_w': _L0_ffn_in['gate_w'], 'L0_ffn_up_w': _L0_ffn_in['up_w'], 'L0_ffn_down_w': _L0_ffn_in['down_w'], 'L1_xattn_Wq': _L1_xattn_in['Wq'], 'L1_xattn_Wg': _L1_xattn_in['Wg'], 'L1_xattn_bg': _L1_xattn_in['bg'], 'L1_xattn_Wkv': _L1_xattn_in['Wkv'], 'L1_xattn_Wo': _L1_xattn_in['Wo'], 'L1_ffn_expert_bias': _L1_ffn_in['expert_bias'], 'L1_ffn_gate_w': _L1_ffn_in['gate_w'], 'L1_ffn_w1': _L1_ffn_in['w1'], 'L1_ffn_w2': _L1_ffn_in['w2'], 'L1_ffn_w3': _L1_ffn_in['w3'], 'L1_ffn_sw1': _L1_ffn_in['sw1'], 'L1_ffn_sw2': _L1_ffn_in['sw2'], 'L1_ffn_sw3': _L1_ffn_in['sw3']}

def reference(x, ctx_2048, g_xattn, g_ffn, L0_xattn_time_decay, L0_xattn_time_first, L0_ffn_W_q, L0_ffn_keys, L0_ffn_down_embed, L0_ffn_up_embed, L0_ffn_gate_w, L0_ffn_up_w, L0_ffn_down_w, L1_xattn_Wq, L1_xattn_Wg, L1_xattn_bg, L1_xattn_Wkv, L1_xattn_Wo, L1_ffn_expert_bias, L1_ffn_gate_w, L1_ffn_w1, L1_ffn_w2, L1_ffn_w3, L1_ffn_sw1, L1_ffn_sw2, L1_ffn_sw3):
    import jax
    import jax.numpy as jnp

    def _L0_xattn_ref(batch_size, seq_len, embedding_dim, time_decay, time_first, k, v):
        import jax, jax.numpy as jnp
        import numpy as np

        def _wkv(time_decay, time_first, k, v):
            w = -jnp.exp(time_decay)
            u = time_first
            B, T, C = k.shape
            aa = jnp.zeros((B, C), dtype=k.dtype)
            bb = jnp.zeros((B, C), dtype=k.dtype)
            pp = jnp.full((B, C), -1e+38, dtype=k.dtype)

            def step(carry, kv_t):
                aa, bb, pp = carry
                kt, vt = kv_t
                ww = u + kt
                q = jnp.maximum(pp, ww)
                e1 = jnp.exp(pp - q)
                e2 = jnp.exp(ww - q)
                y_t = (e1 * aa + e2 * vt) / (e1 * bb + e2)
                ww2 = pp + w
                q2 = jnp.maximum(ww2, kt)
                e1b = jnp.exp(ww2 - q2)
                e2b = jnp.exp(kt - q2)
                new_carry = (e1b * aa + e2b * vt, e1b * bb + e2b, q2)
                return (new_carry, y_t)
            ks = jnp.transpose(k, (1, 0, 2))
            vs = jnp.transpose(v, (1, 0, 2))
            _, ys = jax.lax.scan(step, (aa, bb, pp), (ks, vs))
            return jnp.transpose(ys, (1, 0, 2))
        assert seq_len <= 128
        return _wkv(time_decay, time_first, k, v)

    def _L0_ffn_ref(hidden_states, W_q, keys, down_embed, up_embed, gate_w, up_w, down_w):
        import jax, jax.numpy as jnp
        import numpy as np
        HIDDEN = 256
        INTER = 1024
        RETRIEVAL = 128
        NUM_EXPERTS = 512
        NUM_KEYS = 64
        TOP_K = 8
        B, S = (4, 256)
        b, s, h = hidden_states.shape
        n = b * s
        queries = (hidden_states @ W_q).reshape(2, n, RETRIEVAL // 2)
        routing = jnp.einsum('tnd,tdk->tnk', queries, keys)
        scores2, idx2 = jax.lax.top_k(routing, TOP_K)
        sx, sy = (scores2[0], scores2[1])
        ix, iy = (idx2[0], idx2[1])
        all_scores = (sx[:, :, None] + sy[:, None, :]).reshape(n, TOP_K * TOP_K)
        all_idx = (ix[:, :, None] * NUM_KEYS + iy[:, None, :]).reshape(n, TOP_K * TOP_K)
        scores, pk = jax.lax.top_k(all_scores, TOP_K)
        indices = jnp.take_along_axis(all_idx, pk, axis=-1)
        de = down_embed[indices]
        ue = up_embed[indices]
        x = hidden_states.reshape(n, h)
        ew = jnp.einsum('nh,nkh->nk', x, de)
        ew = jax.nn.silu(ew) * jax.nn.softmax(scores, axis=-1)
        experts_states = jnp.einsum('nk,nkh->nh', ew, ue).reshape(b, s, h)
        mlp = jax.nn.silu(x @ gate_w) * (x @ up_w) @ down_w
        return mlp.reshape(b, s, h) + experts_states

    def _L1_xattn_ref(query, kv, Wq, Wg, bg, Wkv, Wo):
        import jax, jax.numpy as jnp
        import numpy as np
        EPS = 1e-06
        NUM_HEADS = 16

        def _feature_map(x):
            return jnp.where(x > 0, x + 1.0, jnp.exp(x))
        B, L, D = query.shape
        S = kv.shape[1]
        H = NUM_HEADS
        hd = D // H
        q = query @ Wq.T
        gate = jax.nn.sigmoid(query @ Wg.T + bg)
        kvp = kv @ Wkv.T
        k, v = jnp.split(kvp, 2, axis=-1)
        q = _feature_map(q.reshape(B, L, H, hd).transpose(0, 2, 1, 3))
        k = _feature_map(k.reshape(B, S, H, hd).transpose(0, 2, 1, 3))
        v = v.reshape(B, S, H, hd).transpose(0, 2, 1, 3)
        kv_summary = jnp.einsum('bhsd,bhse->bhde', k, v)
        k_sum = k.sum(axis=-2)
        z = 1.0 / (jnp.einsum('bhld,bhd->bhl', q, k_sum)[..., None] + EPS)
        attn = jnp.einsum('bhld,bhde->bhle', q, kv_summary) * z
        attn = attn.transpose(0, 2, 1, 3).reshape(B, L, D)
        out = attn * gate @ Wo.T
        return out

    def _L1_ffn_ref(x, expert_bias, gate_w, w1, w2, w3, sw1, sw2, sw3):
        import jax, jax.numpy as jnp
        import numpy as np
        DIM = 256
        HID = 128
        E = 8
        K = 2
        SHID = HID * 1
        INIT = 0.02
        B, S, D = x.shape
        xf = x.reshape(-1, D)
        N = xf.shape[0]
        scores = jax.nn.sigmoid((xf @ gate_w.T).astype(jnp.float32))
        _, sel = jax.lax.top_k(scores + expert_bias[None, :], K)
        top_scores = jnp.take_along_axis(scores, sel, axis=1)
        flat_exp = sel.reshape(-1)
        order = jnp.argsort(flat_exp, stable=True)
        sorted_exp = flat_exp[order]
        tok_idx = order // K
        sc_sorted = top_scores.reshape(-1)[order]
        rin = xf[tok_idx] * sc_sorted[:, None].astype(x.dtype)
        out_sorted = jnp.zeros_like(rin)
        for e in range(E):
            m = (sorted_exp == e)[:, None].astype(rin.dtype)
            h = jax.nn.silu(rin @ w1[e].T) * (rin @ w3[e].T)
            out_sorted = out_sorted + m * (h @ w2[e].T)
        routed = jnp.zeros((N, D), x.dtype).at[tok_idx].add(out_sorted)
        shared = jax.nn.silu(xf @ sw1.T) * (xf @ sw3.T) @ sw2.T
        return (routed + shared).reshape(B, S, D)
    x = x + jnp.tanh(g_xattn[0]) * _L0_xattn_ref(16, 128, 256, L0_xattn_time_decay, L0_xattn_time_first, _layernorm(x, axis=-1), ctx_2048)
    x = x + jnp.tanh(g_ffn[0]) * _L0_ffn_ref(_layernorm(x, axis=-1), L0_ffn_W_q, L0_ffn_keys, L0_ffn_down_embed, L0_ffn_up_embed, L0_ffn_gate_w, L0_ffn_up_w, L0_ffn_down_w)
    x = x + jnp.tanh(g_xattn[1]) * _L1_xattn_ref(_layernorm(x, axis=-1), ctx_2048, L1_xattn_Wq, L1_xattn_Wg, L1_xattn_bg, L1_xattn_Wkv, L1_xattn_Wo)
    x = x + jnp.tanh(g_ffn[1]) * _L1_ffn_ref(_layernorm(x, axis=-1), L1_ffn_expert_bias, L1_ffn_gate_w, L1_ffn_w1, L1_ffn_w2, L1_ffn_w3, L1_ffn_sw1, L1_ffn_sw2, L1_ffn_sw3)
    return x

_drawn_inputs = setup_inputs


def setup_inputs(seed=0):
    import zlib

    import numpy as np

    out = dict(_drawn_inputs(seed))
    spreads = {'g_ffn': (-1.0, 0.6), 'L1_xattn_bg': (1.0, 0.6), 'L1_ffn_expert_bias': (0.0, 0.8)}
    factors = {'L0_ffn_W_q': 8.0,
     'L0_ffn_keys': 8.0,
     'L0_ffn_down_embed': 8.0,
     'L0_ffn_up_embed': 8.0,
     'L0_ffn_gate_w': 2.695,
     'L0_ffn_up_w': 2.67,
     'L1_xattn_Wq': 4.79,
     'L1_ffn_gate_w': 8.0,
     'L1_ffn_w1': 8.0,
     'L1_ffn_w2': 8.0,
     'L1_ffn_w3': 8.0,
     'L1_ffn_sw1': 7.059,
     'L1_ffn_sw2': 6.952,
     'L1_ffn_sw3': 6.979}
    for name, (base, spread) in spreads.items():
        noise = np.random.default_rng([zlib.crc32(name.encode()), seed]).standard_normal(out[name].shape)
        drawn = base * np.exp(spread * noise) if base else spread * noise
        out[name] = jnp.asarray(drawn.astype(out[name].dtype))
    for name, factor in factors.items():
        out[name] = (out[name] * factor).astype(out[name].dtype)
    return out
```

```python
from contextlib import ExitStack

import concourse.bass as bass
from concourse import mybir

ALU = mybir.AluOpType
ACT = mybir.ActivationFunctionType
F32 = mybir.dt.float32
F32R = mybir.dt.float32r
BF16 = mybir.dt.bfloat16
U32 = mybir.dt.uint32
AX_X = mybir.AxisListType.X

P = 128
NSEQ = 16
D = 256
C = D // P
GT = 4
GN = GT * P
NG = NSEQ // GT
NK = 64
TOPK = 8
NEXP = 512
EC = NEXP // P
HEADS = 16
HD = D // HEADS
HC = HEADS // C
KVW = P + HC
INTER = 1024
IC = INTER // P
NE = 8
LN_EPS = 1e-5
Z_EPS = 1e-6
U_LEAST = -60.0
LOWEST = -3.0e38
BANKS = 6
PAD = P + 1

MAIN_FIRST = [0, 8, 4, 12]

SCHED = [
    ("wkv_in", 0), ("kv", 0), ("split", 0), ("wkv_out", 0), ("route_in", 0), ("split", 1), ("route", 0),
    ("wkv_in", 1), ("kv", 1), ("split", 2), ("wkv_out", 1), ("route_in", 1), ("route", 1),
    ("wkv_in", 2), ("kv", 2), ("mlp_in", 0), ("mlp", 0), ("wkv_out", 2), ("route_in", 2), ("mlp_out", 0),
    ("attn_in", 0), ("route", 2), ("attn", 0),
    ("wkv_in", 3), ("moe_in", 0), ("moe", 0),
    ("mlp_in", 1), ("kv", 3), ("wkv_out", 3), ("mlp", 1), ("route_in", 3), ("mlp_out", 1),
    ("attn_in", 1), ("route", 3), ("attn", 1),
    ("moe_in", 1), ("moe", 1),
    ("mlp_in", 2), ("mlp", 2), ("mlp_out", 2), ("attn_in", 2), ("attn", 2), ("moe_in", 2), ("moe", 2),
    ("mlp_in", 3), ("mlp", 3), ("mlp_out", 3), ("attn_in", 3), ("attn", 3), ("moe_in", 3), ("moe", 3),
]
XN_USERS = ("wkv_in", "route_in", "mlp_in", "attn_in", "attn", "moe_in")
XN_ORDER = {step: n for n, step in enumerate(s for s in SCHED if s[0] in XN_USERS)}
SPLIT_ORDER = {s: n for n, s in enumerate(s for s in SCHED if s[0] in ("mlp_in", "attn_in", "moe_in"))}
STATS_ORDER = {s: n for n, s in enumerate(s for s in SCHED if s[0] in ("wkv_in", "route_in", "attn_in", "moe_in"))}

MLP_UNITS = EC + IC
MOE_UNITS = 1 + NE
UNITS = MLP_UNITS + MOE_UNITS


def prep_seqs(g):
    return [2 * g, 2 * g + 1, 2 * g + 8, 2 * g + 9]


def main_seqs(f):
    return [MAIN_FIRST[f] + t for t in range(GT)]


def build(nc, io):
    with ExitStack() as ctx:
        def sb(name, shape, dt=F32):
            return ctx.enter_context(nc.sbuf_tensor(name, shape, dt))

        def sem(name):
            return ctx.enter_context(nc.semaphore(name))

        ring = [ctx.enter_context(nc.psum_tensor(f"ring{k}", [P, GN], F32)) for k in range(BANKS)]
        acc = [ctx.enter_context(nc.psum_tensor(f"acc{k}", [P, 2, D], F32)) for k in range(2)]

        x_nat = sb("x_nat", [P, NSEQ, D])
        kv_sum = sb("kv_sum", [P, NSEQ, C * KVW])
        ident = sb("ident", [P, P])
        identb = sb("identb", [P, P], BF16)
        head_mask = sb("head_mask", [P, C * KVW])
        iota8 = sb("iota8", [P, TOPK, TOPK])
        iota_e = sb("iota_e", [P, NE])
        key_iota = sb("key_iota", [P, NK, TOPK], BF16)
        rank_w = sb("rank_w", [P, TOPK], BF16)
        decay = sb("decay", [P, C, GT * PAD])
        td = sb("td", [P, C])
        tf = sb("tf", [P, C])
        ew = sb("ew", [P, C])
        bias_a = sb("bias_a", [P, C])
        bias_b = sb("bias_b", [P, C])
        gates = sb("gates", [P, 4])
        e_bias = sb("e_bias", [P, NE])
        minus_half = sb("minus_half", [P, GT])
        ones_row = sb("ones_row", [1, P])
        bg = sb("bg", [1, D])
        wq0 = sb("wq0", [P, C, P])
        keys_bd = sb("keys_bd", [P, 2, 2 * NK])
        wkv = sb("wkv", [P, C, 2 * D])
        wo = sb("wo", [P, C, D])
        w_down = sb("w_down", [P, MLP_UNITS, D])
        up_h = sb("up_h", [P, 2, C, INTER], F32R)
        up_l = sb("up_l", [P, 2, C, INTER], F32R)
        exp_h = sb("exp_h", [P, C, NEXP], F32R)
        exp_l = sb("exp_l", [P, C, NEXP], F32R)
        qg_h = sb("qg_h", [P, C, 2 * D], F32R)
        qg_l = sb("qg_l", [P, C, 2 * D], F32R)
        gw_h = sb("gw_h", [P, C * NE], F32R)
        gw_l = sb("gw_l", [P, C * NE], F32R)
        picks = sb("picks", [P, NG, 4, TOPK + NK], BF16)
        exps = sb("exps", [P, NG, 4, TOPK + NK + 1])
        sel_picks = sb("sel_picks", [TOPK + NK, EC, P], BF16)
        sel_exps = sb("sel_exps", [TOPK + NK + 1, EC + 2, P], F32R)
        picks_t = sb("picks_t", [TOPK + NK, GN], BF16)
        mean_rstd = sb("mean_rstd", [P, NSEQ, 2])
        rstd2 = sb("rstd2", [P, NSEQ])

        xn = [sb(f"xn{k}", [P, GT, D]) for k in range(2)]
        stats = sb("stats", [P, GT, 6])
        mv = sb("mv", [P, GT, 2])
        var_eps = sb("var_eps", [P, GT])
        rstd = sb("rstd", [P, GT])
        v_t = sb("v_t", [P, C, GN])
        ee_a = [sb(f"ee_a{c}", [P, 2, GT * PAD]) for c in range(C)]
        ee_b = [sb(f"ee_b{c}", [P, 2, GN]) for c in range(C)]
        logits = sb("logits", [P, 2 * GT, NK])
        q_t = logits[:, :, :].rearrange("p a b -> p (a b)")
        top_v = sb("top_v", [P, 8, TOPK])
        top_i = sb("top_i", [P, 8, TOPK], U32)
        pairs = sb("pairs", [P, 4, TOPK * TOPK])
        pair_top = sb("pair_top", [P, 4, TOPK])
        pair_rep = sb("pair_rep", [P, 4, TOPK * TOPK])
        pair_d = sb("pair_d", [P, 4, TOPK * TOPK])
        ix_f = sb("ix_f", [P, 4, TOPK])
        iy_b = sb("iy_b", [P, 4, TOPK], BF16)
        r_cnt = sb("r_cnt", [P, 4, TOPK])
        r_sum = sb("r_sum", [P, 4, TOPK])
        r_z = sb("r_z", [P, 4])
        onehot = sb("onehot", [P, 2, NK, TOPK], BF16)
        k_e = [sb(f"k_e{k}", [P, D]) for k in range(2)]
        k_r = [sb(f"k_r{k}", [P, D]) for k in range(2)]
        v_x = [sb(f"v_x{k}", [P, C, KVW]) for k in range(2)]
        xt_h = sb("xt_h", [P, C, GN], F32R)
        xt_l = sb("xt_l", [P, C, GN], F32R)
        act_s = [sb(f"act_s{k}", [P, GN]) for k in range(2)]
        hid = [sb(f"hid{k}", [P, GN]) for k in range(2)]
        fs = [sb(f"fs{k}", [P, 2, GN]) for k in range(3)]
        z_den = sb("z_den", [P, HEADS])
        s_e = sb("s_e", [P, GT, NE])
        s_b = sb("s_b", [P, GT, NE])
        s_top = sb("s_top", [P, GT, TOPK])
        s_idx = sb("s_idx", [P, GT, TOPK], U32)
        s_if = sb("s_if", [P, GT, 2])
        s_m = sb("s_m", [P, GT, NE])
        stage = [sb(f"stage{k}", [P, 2 * D]) for k in range(2)]
        ws_h = [sb(f"ws_h{k}", [P, C, 2, P], F32R) for k in range(2)]
        ws_l = [sb(f"ws_l{k}", [P, C, 2, P], F32R) for k in range(2)]
        w2s = [sb(f"w2s{k}", [P, D]) for k in range(2)]

        bank_full = [sem(f"bank_full{k}") for k in range(BANKS)]
        bank_free = [sem(f"bank_free{k}") for k in range(BANKS)]
        consts_loaded = sem("consts_loaded")
        down_loaded = sem("down_loaded")
        x_loaded = [sem(f"x_loaded{g}") for g in range(NG)]
        ctx_loaded = sem("ctx_loaded")
        stage_loaded = [sem(f"stage_loaded{k}") for k in range(2)]
        w2_loaded = [sem(f"w2_loaded{k}") for k in range(2)]
        out_stored = sem("out_stored")
        dve_link = sem("dve_link")
        act_link = sem("act_link")
        identb_ready = sem("identb_ready")
        dve_setup = sem("dve_setup")
        act_setup = sem("act_setup")
        var_ready = sem("var_ready")
        rstd_ready = sem("rstd_ready")
        xn_ready = sem("xn_ready")
        high_ready = sem("high_ready")
        ev_ready = sem("ev_ready")
        y_ready = sem("y_ready")
        k_ready = sem("k_ready")
        diff_ready = sem("diff_ready")
        exp_ready = sem("exp_ready")
        routes_ready = sem("routes_ready")
        exps_high = sem("exps_high")
        h_ready = sem("h_ready")
        down_done = sem("down_done")
        acc_free = sem("acc_free")
        expert_silu = sem("expert_silu")
        scores_ready = sem("scores_ready")
        qf_ready = sem("qf_ready")
        wsplit_h = sem("wsplit_h")
        wsplit_l = sem("wsplit_l")

        jobs = []
        for w, name in enumerate(("gate_up", "up_up")):
            for c in range(C):
                for half in range(2):
                    s = slice(half * GN, (half + 1) * GN)
                    jobs.append((io[name][c * P:(c + 1) * P, s], up_h[:, w, c, s], up_l[:, w, c, s], GN))
        for c in range(C):
            jobs.append((io["down_embed_t"][c * P:(c + 1) * P, :], exp_h[:, c, :], exp_l[:, c, :], NEXP))
        for c in range(C):
            jobs.append((io["wqg_t"][c * P:(c + 1) * P, :], qg_h[:, c, :], qg_l[:, c, :], 2 * D))
        jobs.append((io["gw_t"], gw_h[:, :], gw_l[:, :], C * NE))
        SETUP_JOBS = len(jobs)
        SPLIT_STEPS = [(0, 5), (5, 9), (9, SETUP_JOBS)]
        for f in range(NG):
            for e in range(MOE_UNITS):
                n = len(jobs) - SETUP_JOBS
                h, l = ws_h[n % 2], ws_l[n % 2]
                jobs.append((io["w13_t"][e], h[:, :, :, :].rearrange("p c w m -> p (c w m)"),
                             l[:, :, :, :].rearrange("p c w m -> p (c w m)"), 2 * D))

        def moe_job(f, e):
            return SETUP_JOBS + f * MOE_UNITS + e

        place = {}
        last_xt_read = {}

        def full(eng, key):
            k, n = place[key]
            eng.wait_ge(bank_full[k], n)
            return ring[k]

        def freed(eng, key):
            k, n = place[key]
            eng.wait_ge(bank_free[k], n)

        def free_sem(key):
            return bank_free[place[key][0]]

        def unit_of(f, u):
            return f * UNITS + u

        def xt_wait(eng, n):
            if n > 0:
                k, turn = place[last_xt_read[n - 1]]
                eng.wait_ge(bank_full[k], turn)

        exps_t_h = ws_h[0][0:TOPK + NK + 1, :, :, :].rearrange("p c w m -> p (c w m)")
        exps_t_l = ws_l[0][0:TOPK + NK + 1, :, :, :].rearrange("p c w m -> p (c w m)")

        CONSTS = ["ident", "head_mask", "iota8", "iota_e", "key_iota_f", "rank_w_f", "sel_picks_f", "sel_exps_f", "first_mask", "td", "tf",
                  "gates", "e_bias", "bg", "wq0", "keys_bd", "wkv"]
        key_iota_f = ee_a[0][:, :, :].rearrange("p a b -> p (a b)")[:, 0:NK * TOPK]
        rank_w_f = ee_a[1][:, 0, 0:TOPK]
        sel_picks_f = ee_b[0][:, :, :].rearrange("p a b -> p (a b)")[0:TOPK + NK, 0:EC * P]
        sel_exps_f = ee_b[1][:, :, :].rearrange("p a b -> p (a b)")[0:TOPK + NK + 1, 0:(EC + 2) * P]
        first_mask = xn[1][:, :, :].rearrange("p a b -> p (a b)")[:, 0:GT * PAD]

        block = ctx.enter_context(nc.Block())

        @block.tensor
        def _(pe):
            uses = [0]

            def open_bank(key):
                k, n = uses[0] % BANKS, uses[0] // BANKS + 1
                uses[0] += 1
                place[key] = (k, n)
                if n > 1:
                    pe.wait_ge(bank_free[k], n - 1)
                return ring[k]

            def close_bank(key, last):
                last.then_inc(bank_full[place[key][0]], 1)

            def transpose_xn(step):
                n = XN_ORDER[step]
                pe.wait_ge(xn_ready, n + 1)
                for c in range(C):
                    key = (step, "T", c)
                    bank = open_bank(key)
                    for t in range(GT):
                        last = pe.transpose(bank[:, t * P:(t + 1) * P], xn[n % 2][:, t, c * P:(c + 1) * P], ident[:, :])
                    close_bank(key, last)

            def three_pass(out, wh, wl, xh, xl, first, final):
                pe.matmul(out, wl, xh, start=first, stop=False, skip_group_check=True)
                pe.matmul(out, wh, xl, start=False, stop=False, skip_group_check=True)
                return pe.matmul(out, wh, xh, start=False, stop=final, skip_group_check=True)

            def down(f, u, weights, first, final):
                n = unit_of(f, u)
                pe.wait_ge(h_ready, n + 1)
                for t in range(GT):
                    last = pe.matmul(acc[t // 2][:, t % 2, :], hid[n % 2][:, t * P:(t + 1) * P], weights,
                                     start=first and t % 2 == 0, stop=final, skip_group_check=True)
                last.then_inc(down_done, 1)

            pe.wait_ge(consts_loaded, 16 * len(CONSTS))
            pe.wait_ge(identb_ready, 1)

            for step in SCHED:
                kind, g = step
                if kind == "wkv_in":
                    transpose_xn(step)
                elif kind == "wkv_out":
                    pe.wait_ge(y_ready, C * (g + 1))
                    for p in range(2):
                        key = (step, "Y", p)
                        bank = open_bank(key)
                        for t in range(2):
                            for c in range(C):
                                last = pe.transpose(bank[:, (t * C + c) * P:(t * C + c + 1) * P],
                                                    ee_b[c][:, 0, (2 * p + t) * P:(2 * p + t + 1) * P], ident[:, :])
                        close_bank(key, last)
                elif kind == "kv":
                    pe.wait_ge(ctx_loaded, 16 * (g + 1))
                    for t in range(GT + 1):
                        if t < GT:
                            key = (step, "K", t)
                            bank = open_bank(key)
                            for c in range(C):
                                last = pe.matmul(bank[:, :], v_t[:, c, t * P:(t + 1) * P], wkv[:, c, :],
                                                 start=(c == 0), stop=(c == C - 1))
                            close_bank(key, last)
                        if t >= 1:
                            n = g * GT + t - 1
                            pe.wait_ge(k_ready, n + 1)
                            key = (step, "V", t - 1)
                            bank = open_bank(key)
                            for c in range(C):
                                last = pe.matmul(bank[:, c * KVW:(c + 1) * KVW], k_e[n % 2][:, c * P:(c + 1) * P],
                                                 v_x[n % 2][:, c, :], start=True, stop=True)
                            close_bank(key, last)
                elif kind == "route_in":
                    transpose_xn(step)
                elif kind == "route":
                    key = (step, "Q")
                    for c in range(C):
                        freed(pe, (("route_in", g), "T", c))
                    bank = open_bank(key)
                    for c in range(C):
                        last = pe.matmul(bank[:, :], wq0[:, c, :], ee_b[c][:, 1, :], start=(c == 0), stop=(c == C - 1))
                    close_bank(key, last)
                    freed(pe, key)
                    key = (step, "R")
                    bank = open_bank(key)
                    for t in range(GT):
                        last = pe.matmul(bank[:, t * P:(t + 1) * P], q_t[:, t * P:(t + 1) * P],
                                         keys_bd[:, t // 2, :], start=True, stop=True)
                    close_bank(key, last)
                elif kind == "mlp_in":
                    transpose_xn(step)
                elif kind == "mlp":
                    rg = MAIN_FIRST[g] // GT
                    pe.wait_ge(wsplit_l, SETUP_JOBS)
                    pe.wait_ge(down_loaded, 48)
                    pe.wait_ge(routes_ready, rg + 1)
                    key = (step, "PT")
                    bank = open_bank(key)
                    half_words = bank[0:TOPK + NK, 0:GN // 2].bitcast(BF16)
                    for r in range(4):
                        last = pe.transpose(half_words[:, r * P:(r + 1) * P], picks[:, rg, r, :], identb[:, :])
                    close_bank(key, last)
                    key = (step, "ET")
                    bank = open_bank(key)
                    for r in range(4):
                        last = pe.transpose(bank[0:TOPK + NK + 1, r * P:(r + 1) * P], exps[:, rg, r, :], ident[:, :])
                    close_bank(key, last)
                    freed(pe, (step, "PT"))
                    freed(pe, (step, "ET"))

                    def spread(name, k):
                        key = (step, name)
                        bank = open_bank(key)
                        pe.matmul(bank[:, :], sel_exps[:, k, :], exps_t_l, start=True, stop=False)
                        last = pe.matmul(bank[:, :], sel_exps[:, k, :], exps_t_h, start=False, stop=True)
                        close_bank(key, last)

                    spread("EY", EC)
                    for c in range(C):
                        freed(pe, (("mlp_in", g), "T", c))
                    for u in range(MLP_UNITS + 1):
                        if u < EC:
                            key = (step, "A", u)
                            bank = open_bank(key)
                            m = slice(u * P, (u + 1) * P)
                            for c in range(C):
                                last = three_pass(bank[:, :], exp_h[:, c, m], exp_l[:, c, m], xt_h[:, c, :],
                                                  xt_l[:, c, :], c == 0, c == C - 1)
                            close_bank(key, last)
                            key = (step, "RANK", u)
                            bank = open_bank(key)
                            last = pe.matmul(bank[:, :], sel_picks[:, u, :], picks_t[:, :], start=True, stop=True)
                            close_bank(key, last)
                            spread(("EX", u), u)
                            if u == EC - 1:
                                spread("OVER", EC + 1)
                        elif u < MLP_UNITS:
                            m = slice((u - EC) * P, (u - EC + 1) * P)
                            for w, name in enumerate("AB"):
                                key = (step, name, u)
                                bank = open_bank(key)
                                for c in range(C):
                                    last = three_pass(bank[:, :], up_h[:, w, c, m], up_l[:, w, c, m], xt_h[:, c, :],
                                                      xt_l[:, c, :], c == 0, c == C - 1)
                                close_bank(key, last)
                            if u == MLP_UNITS - 1:
                                last_xt_read[SPLIT_ORDER[("mlp_in", g)]] = key
                        if u >= 1:
                            if u == 1 and g > 0:
                                pe.wait_ge(acc_free, 2 * 2 * g)
                            down(g, u - 1, w_down[:, u - 1, :], u == 1, u == MLP_UNITS)
                elif kind == "attn_in":
                    transpose_xn(step)
                elif kind == "attn":
                    for c in range(C):
                        freed(pe, (("attn_in", g), "T", c))
                    for c in range(C):
                        key = (step, "Q", c)
                        bank = open_bank(key)
                        m = slice(c * P, (c + 1) * P)
                        for k in range(C):
                            last = three_pass(bank[:, :], qg_h[:, k, m], qg_l[:, k, m], xt_h[:, k, :], xt_l[:, k, :],
                                              k == 0, k == C - 1)
                        close_bank(key, last)
                    for p in range(2):
                        key = (step, "G", p)
                        bank = open_bank(key)
                        for t in range(2):
                            o = bank[:, t * D:(t + 1) * D]
                            tok = slice((2 * p + t) * P, (2 * p + t + 1) * P)
                            pe.matmul(o, ones_row[:, :], bg[:, :], start=True, stop=False, skip_group_check=True)
                            for k in range(C):
                                last = three_pass(o, xt_h[:, k, tok], xt_l[:, k, tok], qg_h[:, k, D:], qg_l[:, k, D:],
                                                  False, k == C - 1)
                        close_bank(key, last)
                    last_xt_read[SPLIT_ORDER[("attn_in", g)]] = key
                    pe.wait_ge(qf_ready, C * (g + 1))
                    for t, b in enumerate(main_seqs(g)):
                        key = (step, "AT", t)
                        bank = open_bank(key)
                        for c in range(C):
                            last = pe.matmul(bank[:, c * KVW:(c + 1) * KVW], fs[0][:, c, t * P:(t + 1) * P],
                                             kv_sum[:, b, c * KVW:(c + 1) * KVW], start=True, stop=True)
                        close_bank(key, last)
                    transpose_xn(step)
                    for c in range(C):
                        freed(pe, (step, "T", c))
                    for p in range(2):
                        key = (step, "O", p)
                        bank = open_bank(key)
                        for t in range(2):
                            tok = slice((2 * p + t) * P, (2 * p + t + 1) * P)
                            for c in range(C):
                                last = pe.matmul(bank[:, t * D:(t + 1) * D], fs[2][:, c, tok], wo[:, c, :],
                                                 start=(c == 0), stop=(c == C - 1))
                        close_bank(key, last)
                elif kind == "moe_in":
                    transpose_xn(step)
                elif kind == "moe":
                    for c in range(C):
                        freed(pe, (("moe_in", g), "T", c))
                    key = (step, "S")
                    bank = open_bank(key)
                    for t in range(GT):
                        tok = slice(t * P, (t + 1) * P)
                        for k in range(C):
                            e = slice(k * NE, (k + 1) * NE)
                            last = three_pass(bank[:, t * NE:(t + 1) * NE], xt_h[:, k, tok], xt_l[:, k, tok],
                                              gw_h[:, e], gw_l[:, e], k == 0, k == C - 1)
                    close_bank(key, last)
                    for u in range(MOE_UNITS + 1):
                        if u < MOE_UNITS:
                            j = moe_job(g, u)
                            pe.wait_ge(wsplit_l, j + 1)
                            n = (j - SETUP_JOBS) % 2
                            if u > 0:
                                pe.wait_ge(scores_ready, g + 1)
                                key = (step, "W", u)
                                bank = open_bank(key)
                                for t in range(GT):
                                    lhs = s_e[:, t, u - 1:u].broadcast_to([P, P])
                                    last = pe.transpose(bank[:, t * P:(t + 1) * P], lhs, ident[:, :])
                                close_bank(key, last)
                            for w, name in enumerate("AB"):
                                key = (step, name, u)
                                bank = open_bank(key)
                                for c in range(C):
                                    last = three_pass(bank[:, :], ws_h[n][:, c, w, :], ws_l[n][:, c, w, :],
                                                      xt_h[:, c, :], xt_l[:, c, :], c == 0, c == C - 1)
                                close_bank(key, last)
                            if u == MOE_UNITS - 1:
                                last_xt_read[SPLIT_ORDER[("moe_in", g)]] = key
                        if u >= 1:
                            if u == 1:
                                pe.wait_ge(acc_free, 2 * (2 * g + 1))
                            m = g * MOE_UNITS + u - 1
                            pe.wait_ge(w2_loaded[m % 2], 16 * (m // 2 + 1))
                            down(g, MLP_UNITS + u - 1, w2s[m % 2][:, :], u == 1, u == MOE_UNITS)

        @block.scalar
        def _(act):
            links = [0]

            def link(ins):
                links[0] += 1
                ins.then_inc(act_link, 1)
                act.wait_ge(act_link, links[0])

            def split_high(j):
                _, h, _, cols = jobs[j]
                act.wait_ge(stage_loaded[j % 2], 16 * (j // 2 + 1))
                if j >= SETUP_JOBS + 2:
                    m = j - SETUP_JOBS - 2
                    act.wait_ge(down_done, unit_of(m // MOE_UNITS, MLP_UNITS + m % MOE_UNITS) + 1)
                act.activation(h, stage[j % 2][:, 0:cols], ACT.Copy).then_inc(wsplit_h, 1)

            act.wait_ge(consts_loaded, 16 * len(CONSTS))
            act.activation(gates[:, :], gates[:, :], ACT.Tanh).then_inc(act_setup, 1)
            link(act.activation(ew[:, :], td[:, :], ACT.Exp))
            act.activation(ew[:, :], ew[:, :], ACT.Exp, scale=-1.0).then_inc(act_setup, 1)
            act.wait_ge(dve_setup, 1)
            for step in SCHED:
                kind, g = step
                if kind == "wkv_in":
                    if g > 0:
                        full(act, (("route", g - 1), "Q"))
                    for c in range(C):
                        bank = full(act, (step, "T", c))
                        act.activation(ee_b[c][:, 1, :], bank[:, :], ACT.Exp, bias=bias_b[:, c:c + 1])
                        act.activation(ee_a[c][:, 1, :].rearrange("p (t s) -> p t s", t=GT)[:, :, 1:],
                                       bank[:, :].rearrange("p (t s) -> p t s", t=GT), ACT.Exp,
                                       bias=bias_a[:, c:c + 1]).then_inc(free_sem((step, "T", c)), 1)
                elif kind == "kv":
                    for t in range(GT):
                        n = g * GT + t
                        bank = full(act, (step, "K", t))
                        if n >= 2:
                            prev = divmod(n - 2, GT)
                            full(act, (("kv", prev[0]), "V", prev[1]))
                        act.activation(k_e[n % 2][:, :], bank[:, 0:D], ACT.Exp)
                        act.activation(k_r[n % 2][:, :], bank[:, 0:D], ACT.Relu)
                        act.activation(v_x[n % 2][:, :, 0:P], bank[:, D:].rearrange("p (c m) -> p c m", c=C),
                                       ACT.Copy).then_inc(free_sem((step, "K", t)), 1)
                elif kind == "split":
                    for j in range(*SPLIT_STEPS[g]):
                        split_high(j)
                elif kind == "route_in":
                    for c in range(C):
                        bank = full(act, (step, "T", c))
                        act.activation(ee_b[c][:, 1, :], bank[:, :], ACT.Copy).then_inc(free_sem((step, "T", c)), 1)
                elif kind == "route":
                    bank = full(act, (step, "Q"))
                    if g > 0:
                        act.wait_ge(routes_ready, g)
                    act.activation(q_t, bank[:, :], ACT.Copy).then_inc(free_sem((step, "Q")), 1)
                    bank = full(act, (step, "R"))
                    act.activation(logits[:, :, :].rearrange("p a b -> p (a b)"), bank[:, :],
                                   ACT.Copy).then_inc(free_sem((step, "R")), 1)
                    act.wait_ge(diff_ready, g + 1)
                    act.activation(pair_d[:, :, :], pair_d[:, :, :], ACT.Exp)
                    act.activation(exps[:, g, :, 0:TOPK + NK], exps[:, g, :, 0:TOPK + NK], ACT.Exp).then_inc(exp_ready, 1)
                elif kind in ("mlp_in", "attn_in", "moe_in"):
                    n = SPLIT_ORDER[step]
                    xt_wait(act, n)
                    for c in range(C):
                        bank = full(act, (step, "T", c))
                        act.activation(xt_h[:, c, :], bank[:, :], ACT.Copy).then_inc(high_ready, 1)
                elif kind == "mlp":
                    bank = full(act, (step, "PT"))
                    act.activation(picks_t[:, :], bank[0:TOPK + NK, 0:GN // 2].bitcast(BF16),
                                   ACT.Copy).then_inc(free_sem((step, "PT")), 1)
                    bank = full(act, (step, "ET"))
                    act.activation(exps_t_h, bank[0:TOPK + NK + 1, :], ACT.Copy).then_inc(exps_high, 1)
                    bank = full(act, (step, "EY"))
                    if g > 0:
                        act.wait_ge(h_ready, unit_of(g, 0))
                    act.activation(fs[0][:, 0, :], bank[:, :], ACT.Copy).then_inc(free_sem((step, "EY")), 1)
                    for u in range(MLP_UNITS):
                        n = unit_of(g, u)
                        bank = full(act, (step, "A", u))
                        if n >= 2:
                            act.wait_ge(h_ready, n - 1)
                        act.activation(act_s[n % 2][:, :], bank[:, :], ACT.Silu).then_inc(free_sem((step, "A", u)), 1)
                elif kind == "attn":
                    for c in range(C):
                        bank = full(act, (step, "Q", c))
                        if c > 0 or g > 0:
                            act.wait_ge(qf_ready, C * g + c)
                        act.activation(fs[2][:, 0, :], bank[:, :], ACT.Exp)
                        act.activation(fs[2][:, 1, :], bank[:, :], ACT.Relu).then_inc(free_sem((step, "Q", c)), 1)
                    for p in range(2):
                        bank = full(act, (step, "G", p))
                        act.activation(fs[1][:, p, :], bank[:, :], ACT.Tanh,
                                       scale=0.5).then_inc(free_sem((step, "G", p)), 1)
                    for c in range(C):
                        bank = full(act, (step, "T", c))
                        act.activation(fs[2][:, c, :], bank[:, :], ACT.Copy).then_inc(free_sem((step, "T", c)), 1)
                    split_high(moe_job(g, 0))
                    split_high(moe_job(g, 1))
                elif kind == "moe":
                    bank = full(act, (step, "S"))
                    act.activation(s_e[:, :, :], bank[:, 0:GT * NE].rearrange("p (t e) -> p t e", t=GT), ACT.Exp,
                                   scale=-1.0).then_inc(free_sem((step, "S")), 1)
                    for u in range(MOE_UNITS):
                        n = unit_of(g, MLP_UNITS + u)
                        if u == 0:
                            bank = full(act, (step, "A", u))
                            act.wait_ge(h_ready, n - 1)
                            act.activation(act_s[n % 2][:, :], bank[:, :],
                                           ACT.Silu).then_inc(free_sem((step, "A", u)), 1)
                        if u + 1 < MOE_UNITS:
                            bank = full(act, (step, "W", u + 1))
                            act.wait_ge(h_ready, n)
                            act.activation(fs[0][:, (u + 1) % 2, :], bank[:, :],
                                           ACT.Copy).then_inc(free_sem((step, "W", u + 1)), 1)
                        if u > 0:
                            freed(act, (step, "A", u))
                            act.activation(act_s[n % 2][:, :], act_s[n % 2][:, :], ACT.Silu).then_inc(expert_silu, 1)
                        if u + 2 < MOE_UNITS:
                            split_high(moe_job(g, u + 2))

        @block.vector
        def _(dve):
            links = [0]

            def link(ins):
                links[0] += 1
                ins.then_inc(dve_link, 1)
                dve.wait_ge(dve_link, links[0])

            def layernorm(step, seqs):
                n = XN_ORDER[step]
                fresh = step in STATS_ORDER
                keep = step[0] == "route_in"
                if fresh:
                    for t, b in enumerate(seqs):
                        last = dve.bn_stats(stats[:, t, :], x_nat[:, b, :])
                    link(last)
                    for t, b in enumerate(seqs):
                        out = mean_rstd[:, b, :] if keep else mv[:, t, :]
                        last = dve.bn_aggr(out, stats[:, t, :])
                    link(last)
                    for p in range(2):
                        b = seqs[2 * p]
                        var = mean_rstd[:, b:b + 2, 1] if keep else mv[:, 2 * p:2 * p + 2, 1]
                        last = dve.tensor_scalar(var_eps[:, 2 * p:2 * p + 2], var, LN_EPS, None, ALU.add)
                    last.then_inc(var_ready, 1)
                if n >= 2:
                    prev = [s for s, k in XN_ORDER.items() if k == n - 2][0]
                    full(dve, (prev, "T", C - 1))
                if fresh:
                    dve.wait_ge(rstd_ready, STATS_ORDER[step] + 1)
                if keep:
                    for p in range(2):
                        b = seqs[2 * p]
                        last = dve.tensor_copy(rstd2[:, b:b + 2], rstd[:, 2 * p:2 * p + 2])
                    link(last)
                for t, b in enumerate(seqs):
                    m, r = mv[:, t, 0:1], rstd[:, t:t + 1]
                    if keep or not fresh:
                        m, r = mean_rstd[:, b, 0:1], rstd2[:, b:b + 1]
                    last = dve.tensor_scalar(xn[n % 2][:, t, :], x_nat[:, b, :], m, r, ALU.subtract, ALU.mult)
                last.then_inc(xn_ready, 1)

            def residual(out, bank, gate, signal):
                return dve.scalar_tensor_tensor(out, bank, gates[:, gate:gate + 1], out, ALU.mult,
                                                ALU.add).then_inc(signal, 1)

            dve.wait_ge(consts_loaded, 16 * len(CONSTS))
            dve.tensor_copy(key_iota[:, :, :].rearrange("p a b -> p (a b)"), key_iota_f)
            dve.tensor_copy(rank_w[:, :], rank_w_f)
            dve.tensor_copy(sel_picks[:, :, :].rearrange("k c p -> k (c p)"), sel_picks_f)
            dve.tensor_copy(sel_exps[:, :, :].rearrange("k c p -> k (c p)"), sel_exps_f)
            dve.memset(minus_half[:, :], -0.5)
            dve.memset(ones_row[:, :], 1.0)
            for k in range(2):
                dve.memset(v_x[k][:, :, P:], 1.0)
            dve.tensor_copy(identb[:, :], ident[:, :]).then_inc(identb_ready, 1)
            link(dve.tensor_scalar(bias_a[:, :], tf[:, :], 0.0, -1.0, ALU.max, ALU.mult))
            link(dve.tensor_scalar(bias_b[:, :], tf[:, :], U_LEAST, None, ALU.max))
            link(dve.tensor_tensor(bias_b[:, :], bias_b[:, :], bias_a[:, :], ALU.add))
            for c in range(C):
                last = dve.memset(ee_a[c][:, :, :], 0.0)
            last.then_inc(dve_setup, 1)
            dve.wait_ge(act_setup, 2)
            for c in range(C):
                last = dve.tensor_scalar(decay[:, c, :], first_mask, ew[:, c:c + 1], None, ALU.mult)
            link(last)

            for step in SCHED:
                kind, g = step
                if kind == "wkv_in":
                    dve.wait_ge(x_loaded[g], 32)
                    layernorm(step, prep_seqs(g))
                elif kind == "wkv_out":
                    for c in range(C):
                        dve.wait_ge(ev_ready, C * g + c + 1)
                        for s in range(2):
                            a = ee_a[c][:, s, :]
                            last = dve.tensor_tensor_scan(a, decay[:, c, :], a, 0.0, ALU.mult, ALU.add)
                        link(last)
                        past = ee_a[c][:, :, :].rearrange("p s (t j) -> p s t j", t=GT)[:, :, :, 0:P]
                        both = ee_b[c][:, :, :].rearrange("p s (t j) -> p s t j", t=GT)
                        link(dve.tensor_tensor(both, past, both, ALU.add))
                        link(dve.reciprocal(ee_b[c][:, 1, :], ee_b[c][:, 1, :]))
                        dve.tensor_tensor(ee_b[c][:, 0, :], ee_b[c][:, 0, :], ee_b[c][:, 1, :],
                                          ALU.mult).then_inc(y_ready, 1)
                    for p in range(2):
                        bank = full(dve, (step, "Y", p))
                        b = prep_seqs(g)[2 * p]
                        residual(x_nat[:, b:b + 2, :].rearrange("p t d -> p (t d)"), bank[:, :], 0,
                                 free_sem((step, "Y", p)))
                elif kind == "kv":
                    for t, b in enumerate(prep_seqs(g)):
                        n = g * GT + t
                        freed(dve, (step, "K", t))
                        dve.scalar_tensor_tensor(k_e[n % 2][:, :], k_e[n % 2][:, :], 1.0, k_r[n % 2][:, :], ALU.min,
                                                 ALU.add).then_inc(k_ready, 1)
                        bank = full(dve, (step, "V", t))
                        dve.tensor_tensor(kv_sum[:, b, :], bank[:, 0:C * KVW], head_mask[:, :],
                                          ALU.mult).then_inc(free_sem((step, "V", t)), 1)
                elif kind == "route_in":
                    for p in range(2):
                        freed(dve, (("wkv_out", g), "Y", p))
                    layernorm(step, prep_seqs(g))
                elif kind == "route":
                    freed(dve, (step, "R"))
                    for r in range(8):
                        last = dve.max(top_v[:, r, :], logits[:, r, :])
                    link(last)
                    for r in range(8):
                        last = dve.max_index(top_i[:, r, :], top_v[:, r, :], logits[:, r, :])
                    pr = pairs[:, :, :].rearrange("p r (i j) -> p r i j", i=TOPK)
                    link(dve.tensor_tensor(pr, top_v[:, 0:4, :].unsqueeze(3).broadcast_to([P, 4, TOPK, TOPK]),
                                           top_v[:, 4:8, :].unsqueeze(2).broadcast_to([P, 4, TOPK, TOPK]), ALU.add))
                    for r in range(4):
                        last = dve.max(pair_top[:, r, :], pairs[:, r, :])
                    link(last)
                    for r in range(4):
                        dve.match_replace(pair_rep[:, r, :], pair_top[:, r, :], pairs[:, r, :], LOWEST)
                    dve.tensor_tensor(pair_d[:, :, :], pairs[:, :, :],
                                      pair_top[:, :, 0:1].broadcast_to([P, 4, TOPK * TOPK]), ALU.subtract)
                    dve.tensor_tensor(exps[:, g, :, 0:TOPK], logits[:, 0:4, 0:TOPK],
                                      top_v[:, 0:4, 0:1].broadcast_to([P, 4, TOPK]), ALU.subtract)
                    dve.tensor_tensor(exps[:, g, :, TOPK:TOPK + NK], logits[:, 4:8, :],
                                      top_v[:, 4:8, 0:1].broadcast_to([P, 4, NK]), ALU.subtract).then_inc(diff_ready, 1)
                    dve.wait_ge(diff_ready, g + 1)
                    dve.tensor_copy(ix_f[:, :, :], top_i[:, 0:4, :])
                    dve.tensor_copy(iy_b[:, :, :], top_i[:, 4:8, :])
                    link(dve.tensor_tensor(pair_rep[:, :, :], pairs[:, :, :], pair_rep[:, :, :], ALU.not_equal))
                    pm = pair_rep[:, :, :].rearrange("p r (i j) -> p r i j", i=TOPK)
                    link(dve.tensor_reduce(r_cnt[:, :, :], pm, AX_X, ALU.add))
                    hot = pairs[:, :, :].rearrange("p r (i j) -> p r i j", i=TOPK)
                    table = iota8[:, :, :].unsqueeze(1).broadcast_to([P, 4, TOPK, TOPK])
                    link(dve.tensor_tensor(hot, ix_f[:, :, :].unsqueeze(2).broadcast_to([P, 4, TOPK, TOPK]), table,
                                           ALU.is_equal))
                    link(dve.tensor_tensor(hot, hot, r_cnt[:, :, :].unsqueeze(2).broadcast_to([P, 4, TOPK, TOPK]),
                                           ALU.mult))
                    with nc.allow_low_precision("counts up to 8 are exact in bfloat16"):
                        dve.tensor_reduce(picks[:, g, :, 0:TOPK], hot, AX_X, ALU.add)
                    for a in range(2):
                        oh = onehot[:, :, :, :].rearrange("p h k j -> p (h k) j")
                        for h in range(2):
                            iy = iy_b[:, 2 * a + h, :].unsqueeze(1).broadcast_to([P, NK, TOPK])
                            last = dve.tensor_tensor(onehot[:, h, :, :], iy, key_iota[:, :, :], ALU.is_equal)
                        link(last)
                        rw = rank_w[:, :].unsqueeze(1).broadcast_to([P, 2 * NK, TOPK])
                        link(dve.tensor_tensor(oh, oh, rw, ALU.mult))
                        ry = picks[:, g, 2 * a:2 * a + 2, TOPK:]
                        with nc.allow_low_precision("ranks up to 8 are exact in bfloat16"):
                            link(dve.tensor_reduce(ry, onehot[:, :, :, :], AX_X, ALU.add))
                    dve.wait_ge(exp_ready, g + 1)
                    link(dve.tensor_tensor(pair_d[:, :, :], pair_d[:, :, :], pair_rep[:, :, :], ALU.mult))
                    pd = pair_d[:, :, :].rearrange("p r (i j) -> p r i j", i=TOPK)
                    link(dve.tensor_reduce(r_sum[:, :, :], pd, AX_X, ALU.add))
                    link(dve.tensor_reduce(r_z[:, :], r_sum[:, :, :], AX_X, ALU.add))
                    link(dve.reciprocal(r_z[:, :], r_z[:, :]))
                    zb = r_z[:, :].unsqueeze(2).broadcast_to([P, 4, TOPK])
                    dve.tensor_tensor(exps[:, g, :, 0:TOPK], exps[:, g, :, 0:TOPK], zb, ALU.mult)
                    link(dve.tensor_tensor(r_sum[:, :, :], r_sum[:, :, :], zb, ALU.mult))
                    link(dve.scalar_tensor_tensor(r_sum[:, :, :], ix_f[:, :, :], float(NEXP // NK), r_sum[:, :, :],
                                                  ALU.is_ge, ALU.mult))
                    dve.tensor_reduce(exps[:, g, :, TOPK + NK], r_sum[:, :, :], AX_X, ALU.add).then_inc(routes_ready, 1)
                elif kind in ("mlp_in", "attn_in", "moe_in"):
                    if kind == "attn_in":
                        dve.wait_ge(acc_free, 2 * (2 * g + 1))
                    if kind == "moe_in":
                        for p in range(2):
                            freed(dve, (("attn", g), "O", p))
                    layernorm(step, main_seqs(g))
                    n = SPLIT_ORDER[step]
                    for c in range(C):
                        dve.wait_ge(high_ready, C * n + c + 1)
                        bank = full(dve, (step, "T", c))
                        dve.tensor_tensor(xt_l[:, c, :], bank[:, :], xt_h[:, c, :].bitcast(F32),
                                          ALU.subtract).then_inc(free_sem((step, "T", c)), 1)
                elif kind == "mlp":
                    dve.wait_ge(exps_high, g + 1)
                    bank = full(dve, (step, "ET"))
                    dve.tensor_tensor(exps_t_l, bank[0:TOPK + NK + 1, :], exps_t_h.bitcast(F32),
                                      ALU.subtract).then_inc(free_sem((step, "ET")), 1)
                    freed(dve, (step, "EY"))
                    for u in range(MLP_UNITS):
                        n = unit_of(g, u)
                        if u < EC:
                            w = fs[0][:, 1, :]
                            bank = full(dve, (step, "RANK", u))
                            k = place[(step, "RANK", u)]
                            dve.scalar_tensor_tensor(w, bank[:, :], float(TOPK), fs[0][:, 0, :], ALU.is_gt,
                                                     ALU.mult).then_inc(bank_free[k[0]], 1)
                            dve.wait_ge(bank_free[k[0]], k[1])
                            bank = full(dve, (step, ("EX", u)))
                            k = place[(step, ("EX", u))]
                            dve.tensor_tensor(w, w, bank[:, :], ALU.mult).then_inc(bank_free[k[0]], 1)
                            dve.wait_ge(bank_free[k[0]], k[1])
                            if u == EC - 1:
                                bank = full(dve, (step, "OVER"))
                                k = place[(step, "OVER")]
                                dve.tensor_tensor(w, w, bank[:, :], ALU.add).then_inc(bank_free[k[0]], 1)
                                dve.wait_ge(bank_free[k[0]], k[1])
                            freed(dve, (step, "A", u))
                            if n >= 2:
                                dve.wait_ge(down_done, n - 1)
                            for a in range(2):
                                s = slice(a * 2 * P, (a + 1) * 2 * P)
                                last = dve.tensor_tensor(hid[n % 2][:, s].rearrange("p (j h) -> p h j", h=2),
                                                         act_s[n % 2][:, s].rearrange("p (j h) -> p h j", h=2),
                                                         w[:, s].rearrange("p (h j) -> p h j", h=2), ALU.mult)
                            last.then_inc(h_ready, 1)
                            dve.wait_ge(h_ready, n + 1)
                        else:
                            freed(dve, (step, "A", u))
                            bank = full(dve, (step, "B", u))
                            dve.wait_ge(down_done, n - 1)
                            dve.tensor_tensor(hid[n % 2][:, :], bank[:, :], act_s[n % 2][:, :],
                                              ALU.mult).then_inc(free_sem((step, "B", u)), 1)
                            freed(dve, (step, "B", u))
                            dve.engine_nop().then_inc(h_ready, 1)
                elif kind == "mlp_out":
                    dve.wait_ge(down_done, unit_of(g, MLP_UNITS))
                    for p in range(2):
                        b = main_seqs(g)[2 * p]
                        residual(x_nat[:, b:b + 2, :], acc[p][:, :, :], 1, acc_free)
                elif kind == "attn":
                    for c in range(C):
                        freed(dve, (step, "Q", c))
                        dve.scalar_tensor_tensor(fs[0][:, c, :], fs[2][:, 0, :], 1.0, fs[2][:, 1, :], ALU.min,
                                                 ALU.add).then_inc(qf_ready, 1)
                    nx = XN_ORDER[step]
                    prev = [s for s, k in XN_ORDER.items() if k == nx - 2][0]
                    full(dve, (prev, "T", C - 1))
                    for p in range(2):
                        freed(dve, (step, "G", p))
                    for t in range(GT):
                        bank = full(dve, (step, "AT", t))
                        sums = bank[:, 0:C * KVW].rearrange("p (c m) -> p c m", c=C)
                        z = z_den[:, :].rearrange("p (c m) -> p c m", c=C)
                        link(dve.tensor_scalar(z, sums[:, :, P:], Z_EPS, 2.0, ALU.add, ALU.mult))
                        link(dve.reciprocal(z_den[:, :], z_den[:, :]))
                        o = xn[nx % 2][:, t, :]
                        for c in range(C):
                            last = dve.tensor_tensor(
                                o[:, c * P:(c + 1) * P].rearrange("p (h d) -> p h d", h=HC),
                                bank[:, c * KVW:c * KVW + P].rearrange("p (h d) -> p h d", h=HC),
                                z_den[:, c * HC:(c + 1) * HC].unsqueeze(2).broadcast_to([P, HC, HD]), ALU.mult)
                        last.then_inc(free_sem((step, "AT", t)), 1)
                        freed(dve, (step, "AT", t))
                        gate = fs[1][:, t // 2, (t % 2) * D:(t % 2 + 1) * D]
                        last = dve.scalar_tensor_tensor(o, gate, 1.0, o, ALU.add, ALU.mult)
                    last.then_inc(xn_ready, 1)
                    for p in range(2):
                        bank = full(dve, (step, "O", p))
                        b = main_seqs(g)[2 * p]
                        residual(x_nat[:, b:b + 2, :].rearrange("p t d -> p (t d)"), bank[:, :], 2,
                                 free_sem((step, "O", p)))
                elif kind == "moe":
                    freed(dve, (step, "S"))
                    link(dve.tensor_scalar(s_b[:, :, :], s_e[:, :, :], 1.0, None, ALU.add))
                    link(dve.reciprocal(s_b[:, :, :], s_b[:, :, :]))
                    link(dve.tensor_tensor(s_m[:, :, :], s_b[:, :, :],
                                           e_bias[:, :].unsqueeze(1).broadcast_to([P, GT, NE]), ALU.add))
                    for t in range(GT):
                        last = dve.max(s_top[:, t, :], s_m[:, t, :])
                    link(last)
                    for t in range(GT):
                        last = dve.max_index(s_idx[:, t, :], s_top[:, t, :], s_m[:, t, :])
                    link(last)
                    link(dve.tensor_copy(s_if[:, :, :], s_idx[:, :, 0:2]))
                    tab = iota_e[:, :].unsqueeze(1).broadcast_to([P, GT, NE])
                    dve.tensor_tensor(s_m[:, :, :], tab, s_if[:, :, 0:1].broadcast_to([P, GT, NE]), ALU.is_equal)
                    link(dve.tensor_tensor(s_e[:, :, :], tab, s_if[:, :, 1:2].broadcast_to([P, GT, NE]),
                                           ALU.is_equal))
                    link(dve.tensor_tensor(s_m[:, :, :], s_m[:, :, :], s_e[:, :, :], ALU.add))
                    dve.tensor_tensor(s_e[:, :, :], s_m[:, :, :], s_b[:, :, :], ALU.mult).then_inc(scores_ready, 1)
                    for u in range(MOE_UNITS):
                        n = unit_of(g, MLP_UNITS + u)
                        if u == 0:
                            freed(dve, (step, "A", u))
                            bank = full(dve, (step, "B", u))
                            dve.wait_ge(down_done, n - 1)
                            dve.tensor_tensor(hid[n % 2][:, :], bank[:, :], act_s[n % 2][:, :],
                                              ALU.mult).then_inc(free_sem((step, "B", u)), 1)
                            freed(dve, (step, "B", u))
                            dve.engine_nop().then_inc(h_ready, 1)
                        else:
                            freed(dve, (step, "W", u))
                            s = fs[0][:, u % 2, :]
                            bank = full(dve, (step, "A", u))
                            dve.tensor_tensor(act_s[n % 2][:, :], bank[:, :], s,
                                              ALU.mult).then_inc(free_sem((step, "A", u)), 1)
                            bank = full(dve, (step, "B", u))
                            dve.wait_ge(down_done, n - 1)
                            dve.tensor_tensor(hid[n % 2][:, :], bank[:, :], s,
                                              ALU.mult).then_inc(free_sem((step, "B", u)), 1)
                            freed(dve, (step, "B", u))
                            dve.wait_ge(expert_silu, g * NE + u)
                            dve.tensor_tensor(hid[n % 2][:, :], hid[n % 2][:, :], act_s[n % 2][:, :],
                                              ALU.mult).then_inc(h_ready, 1)
                    dve.wait_ge(down_done, unit_of(g, UNITS))
                    for p in range(2):
                        b = main_seqs(g)[2 * p]
                        residual(x_nat[:, b:b + 2, :], acc[p][:, :, :], 3, acc_free)

        @block.gpsimd
        def _(pool):
            pool.wait_ge(identb_ready, 1)
            for step in SCHED:
                kind, g = step
                if step in STATS_ORDER:
                    pool.wait_ge(var_ready, STATS_ORDER[step] + 1)
                    pool.tensor_tensor(rstd[:, :], var_eps[:, :], minus_half[:, :], ALU.pow).then_inc(rstd_ready, 1)
                if kind == "wkv_in":
                    pool.wait_ge(ctx_loaded, 16 * (g + 1))
                    for c in range(C):
                        freed(pool, (step, "T", c))
                        pool.tensor_tensor(ee_b[c][:, 0, :], ee_b[c][:, 1, :], v_t[:, c, :], ALU.mult)
                        va = ee_a[c][:, :, :].rearrange("p s (t j) -> p s t j", t=GT)[:, :, :, 1:]
                        pool.tensor_tensor(va[:, 0], va[:, 1], v_t[:, c, :].rearrange("p (t j) -> p t j", t=GT),
                                           ALU.mult).then_inc(ev_ready, 1)
                if kind == "split":
                    todo = range(*SPLIT_STEPS[g])
                elif kind == "attn":
                    todo = [moe_job(g, 0), moe_job(g, 1)]
                elif kind == "moe":
                    todo = [moe_job(g, u) for u in range(2, MOE_UNITS)]
                else:
                    todo = []
                for j in todo:
                    _, h, l, cols = jobs[j]
                    pool.wait_ge(wsplit_h, j + 1)
                    pool.tensor_tensor(l, stage[j % 2][:, 0:cols], h.bitcast(F32), ALU.subtract).then_inc(wsplit_l, 1)

        @block.sync
        def _(sp):
            def load_x(g):
                for p in range(2):
                    b = prep_seqs(g)[2 * p]
                    sp.dma_start(x_nat[:, b:b + 2, :],
                                 io["x"][b:b + 2].rearrange("b p d -> p b d")).then_inc(x_loaded[g], 16)

            def load_job(j):
                src, _, _, cols = jobs[j]
                if j >= 2:
                    sp.wait_ge(wsplit_l, j - 1)
                sp.dma_start(stage[j % 2][:, 0:cols], src).then_inc(stage_loaded[j % 2], 16)

            def load_w2(f, u):
                n = f * MOE_UNITS + u
                if n >= 2:
                    m = n - 2
                    sp.wait_ge(down_done, unit_of(m // MOE_UNITS, MLP_UNITS + m % MOE_UNITS) + 1)
                sp.dma_start(w2s[n % 2][:, :], io["w2_t"][u]).then_inc(w2_loaded[n % 2], 16)

            load_x(0)
            dst = {"ident": ident[:, :], "head_mask": head_mask[:, :], "iota8": iota8[:, :, :], "iota_e": iota_e[:, :],
                   "key_iota_f": key_iota_f, "rank_w_f": rank_w_f, "sel_picks_f": sel_picks_f,
                   "sel_exps_f": sel_exps_f, "first_mask": first_mask, "td": td[:, :],
                   "tf": tf[:, :], "gates": gates[:, :], "e_bias": e_bias[:, :],
                   "bg": bg[:, :], "wq0": wq0[:, :, :], "keys_bd": keys_bd[:, :, :], "wkv": wkv[:, :, :]}
            for name in CONSTS:
                sp.dma_start(dst[name], io[name]).then_inc(consts_loaded, 16)
            sp.dma_start(v_t[:, :, :], io["ctx_t"][0]).then_inc(ctx_loaded, 16)
            load_job(0)
            load_job(1)
            for g in range(1, NG):
                load_x(g)
            sp.dma_start(w_down[:, 0:EC, :], io["up_embed"]).then_inc(down_loaded, 16)
            sp.dma_start(w_down[:, EC:, :], io["down_w"]).then_inc(down_loaded, 16)
            sp.dma_start(wo[:, :, :], io["wo_t"]).then_inc(down_loaded, 16)
            stores = 0
            for step in SCHED:
                kind, g = step
                if kind == "kv" and g + 1 < NG:
                    sp.wait_ge(ev_ready, C * (g + 1))
                    full(sp, (step, "K", GT - 1))
                    sp.dma_start(v_t[:, :, :], io["ctx_t"][g + 1]).then_inc(ctx_loaded, 16)
                elif kind == "split":
                    for j in range(*SPLIT_STEPS[g]):
                        if j + 2 < SETUP_JOBS + 2:
                            load_job(j + 2)
                elif kind == "attn":
                    if g > 0:
                        load_job(moe_job(g, 0))
                        load_job(moe_job(g, 1))
                    load_w2(g, 0)
                    load_w2(g, 1)
                elif kind == "moe":
                    for u in range(2, MOE_UNITS):
                        load_job(moe_job(g, u))
                        load_w2(g, u)
                    sp.wait_ge(acc_free, 2 * (2 * g + 2))
                    for p in range(2):
                        b = main_seqs(g)[2 * p]
                        sp.dma_start(io["out"][b:b + 2].rearrange("b p d -> p b d"),
                                     x_nat[:, b:b + 2, :]).then_inc(out_stored, 16)
                        stores += 1
            sp.wait_ge(out_stored, 16 * stores)


def kernel(**inputs):
    import numpy as np
    import concourse.bacc as bacc
    from concourse.bass_utils import run_bass_kernel_spmd

    a = {k: np.asarray(v) for k, v in inputs.items()}

    def chunked(w):
        return np.ascontiguousarray(w.reshape(-1, P, w.shape[-1]).transpose(1, 0, 2))

    def everywhere(v):
        return np.ascontiguousarray(np.broadcast_to(v, (P,) + v.shape))

    ctx_t = a["ctx_2048"].transpose(2, 0, 1)
    ctx_g = np.stack([ctx_t[:, prep_seqs(g), :].reshape(C, P, GN).transpose(1, 0, 2) for g in range(NG)])
    keys = a["L0_ffn_keys"]
    keys_bd = np.zeros((P, 2, 2 * NK), keys.dtype)
    for h in range(2):
        keys_bd[h * NK:(h + 1) * NK, :, h * NK:(h + 1) * NK] = keys.transpose(1, 0, 2)
    w1 = np.concatenate([a["L1_ffn_sw1"][None], a["L1_ffn_w1"]])
    w3 = np.concatenate([a["L1_ffn_sw3"][None], a["L1_ffn_w3"]])
    w2 = np.concatenate([a["L1_ffn_sw2"][None], a["L1_ffn_w2"]])
    w13 = np.stack([w1, w3], 1).transpose(0, 3, 1, 2)
    w13 = w13.reshape(MOE_UNITS, C, P, 2 * P).transpose(0, 2, 1, 3).reshape(MOE_UNITS, P, 2 * D)
    head = np.arange(P) // HD
    mask = np.concatenate([head[:, None] == head[None, :], head[:, None] == np.arange(HC)[None, :]], 1)
    first = np.ones((GT, PAD), np.float32)
    first[:, 0] = 0
    f32 = np.float32
    sel_picks = np.zeros((TOPK + NK, EC, P), f32)
    sel_exps = np.zeros((TOPK + NK + 1, EC + 2, P), f32)
    for p in range(P):
        for c in range(EC):
            sel_picks[c * P // NK + p // NK, c, p] = sel_exps[c * P // NK + p // NK, c, p] = 1
            sel_picks[TOPK + p % NK, c, p] = 1
        sel_exps[TOPK + p % NK, EC, p] = 1
    sel_exps[TOPK + NK, EC + 1, P - 1] = 1
    arrays = {
        "x": a["x"],
        "ctx_t": ctx_g,
        "ident": np.eye(P, dtype=f32),
        "head_mask": np.concatenate([mask, mask], 1).astype(f32),
        "iota8": everywhere(np.repeat(np.arange(TOPK, dtype=f32)[:, None], TOPK, 1)),
        "iota_e": everywhere(np.arange(NE, dtype=f32)),
        "key_iota_f": everywhere(np.repeat(np.arange(NK, dtype=f32), TOPK)),
        "rank_w_f": everywhere(TOPK - np.arange(TOPK, dtype=f32)),
        "sel_picks_f": sel_picks.reshape(TOPK + NK, -1),
        "sel_exps_f": sel_exps.reshape(TOPK + NK + 1, -1),
        "first_mask": everywhere(first.reshape(-1)),
        "td": a["L0_xattn_time_decay"].reshape(C, P).T,
        "tf": a["L0_xattn_time_first"].reshape(C, P).T,
        "gates": everywhere(np.stack([a["g_xattn"], a["g_ffn"]], 1).reshape(-1)),
        "e_bias": everywhere(a["L1_ffn_expert_bias"]),
        "bg": a["L1_xattn_bg"][None],
        "wq0": chunked(a["L0_ffn_W_q"]),
        "keys_bd": keys_bd,
        "wkv": chunked(a["L1_xattn_Wkv"].T),
        "wo_t": chunked(a["L1_xattn_Wo"].T),
        "up_embed": chunked(a["L0_ffn_up_embed"]),
        "down_w": chunked(a["L0_ffn_down_w"]),
        "gate_up": a["L0_ffn_gate_w"],
        "up_up": a["L0_ffn_up_w"],
        "down_embed_t": a["L0_ffn_down_embed"].T,
        "wqg_t": np.concatenate([a["L1_xattn_Wq"].T, a["L1_xattn_Wg"].T], 1),
        "gw_t": chunked(a["L1_ffn_gate_w"].T).reshape(P, C * NE),
        "w13_t": w13,
        "w2_t": w2.transpose(0, 2, 1),
    }
    nc = bacc.Bacc("TRN2", target_bir_lowering=False, num_devices=1)
    io, feeds = {}, {}
    for name, v in arrays.items():
        v = np.ascontiguousarray(v)
        feeds[f"in_{name}"] = v
        io[name] = nc.dram_tensor(f"in_{name}", v.shape, mybir.dt.from_np(v.dtype), kind="ExternalInput").ap()
    io["out"] = nc.dram_tensor("out_x", (NSEQ, P, D), F32, kind="ExternalOutput").ap()
    build(nc, io)
    r = run_bass_kernel_spmd(nc, [feeds], core_ids=[0])
    return r.results[0]["out_x"]
```

```python
from contextlib import ExitStack

import concourse.bass as bass
from concourse import mybir

ALU = mybir.AluOpType
ACT = mybir.ActivationFunctionType
F32 = mybir.dt.float32
F32R = mybir.dt.float32r
BF16 = mybir.dt.bfloat16
U32 = mybir.dt.uint32
AX_X = mybir.AxisListType.X

P = 128
NSEQ = 16
D = 256
C = D // P
GT = 4
GN = GT * P
NG = NSEQ // GT
NK = 64
TOPK = 8
NEXP = 512
EC = NEXP // P
HEADS = 16
HD = D // HEADS
HC = HEADS // C
KVW = P + HC
INTER = 1024
IC = INTER // P
NE = 8
LN_EPS = 1e-5
Z_EPS = 1e-6
U_LEAST = -60.0
LOWEST = -3.0e38
BANKS = 6
LATER = KVW + TOPK * TOPK + 2 * NE + TOPK + C * P + 4 * NK
PAD = P + 1

MAIN_FIRST = [0, 8, 4, 12]
MLP_UNITS = IC + EC
MOE_UNITS = 1 + NE
LAG = 2
RING = LAG + 1
SETUP_JOBS = 2 * C * 2 + C + 1


HOSTS = [("mlp", 0), ("mlp", 1), ("moe", 0), ("mlp", 2), ("mlp", 3), ("moe", 1), ("moe", 2), ("moe", 3)]


def host_units(kind):
    return MLP_UNITS if kind == "mlp" else MOE_UNITS


def steps(text):
    out = []
    for item in text.split(","):
        kind, g, *which = item.split()
        out += [(kind, int(g), int(part)) for part in which]
    return out


START = """wkv_in 0 0, wkv_in 1 0, wkv_in 0 1 2, wkv_in 1 1 2, kv 0 0, split 0 0 1,
    wkv_out 0 0, kv 0 1, wkv_out 0 1, kv 0 2, wkv_out 0 2, split 0 2, wkv_out 0 3, kv 0 3, wkv_out 0 4, kv 0 4,
    wkv_out 0 5, split 0 3, wkv_out 1 0, kv 1 0, wkv_out 1 1, wkv_out 0 6, wkv_out 0 7, kv 1 1, wkv_out 1 2,
    split 0 4, route_in 0 0, kv 1 2, wkv_out 1 3, kv 1 3, route_in 0 1, wkv_out 1 4, kv 1 4, route_in 0 2, wkv_out 1 5,
    split 0 5, route 0 0, kv 2 0, route 0 1, kv 2 1, wkv_out 1 6, wkv_out 1 7, kv 2 2, route_in 1 0, kv 2 3,
    route_in 1 1, kv 2 4, split 0 6, split 0 7, mlp_in 0 0, route_in 1 2, mlp_in 0 1, mlp_in 0 2, route 1 0, route 1 1"""

PLAN = {
    ("mlp", 0): {1: "split 0 8, route 0 2", 2: "split 0 9, route 0 3", 3: "split 0 10, route 0 4, wkv_in 2 0",
                 4: "wkv_in 2 1, route 0 5", 5: "wkv_in 2 2, route 0 6", 6: "route 0 7, wkv_out 2 0", 7: "route 0 8, wkv_out 2 1",
                 8: "wkv_out 2 2 3, peer_in 0 0", 9: "wkv_out 2 4", 10: "wkv_out 2 5", 11: "wkv_out 2 6 7, mlp_in 1 0",
                 12: "mlp_in 1 1, route_in 2 0", 13: "mlp_in 1 2", 14: "route_in 2 1"},
    ("mlp", 1): {1: "mlp_out 0 0, attn_in 0 0, route_in 2 2", 2: "attn_in 0 1, route 2 0", 3: "attn_in 0 2, route 2 1, attn 0 0",
                 4: "attn 0 1 2, route 2 2", 5: "attn 0 3 4, route 2 3 4", 6: "attn 0 5 6, route 2 5",
                 7: "attn 0 7, route 2 6", 8: "attn 0 8, route 2 7 8, peer_in 1 0", 9: "attn 0 9", 10: "attn 0 10",
                 11: "moe_in 0 0 1", 12: "moe_in 0 2, weights 0 0, moe_in 0 3"},
    ("moe", 0): {1: "mlp_out 1 0, wkv_in 3 0", 2: "wkv_in 3 1, kv 3 0", 3: "wkv_in 3 2, kv 3 1",
                 4: "kv 3 2, wkv_out 3 0 1", 5: "kv 3 3, wkv_out 3 2 3", 6: "kv 3 4, wkv_out 3 4", 7: "wkv_out 3 5",
                 8: "wkv_out 3 6 7, route_in 3 0", 9: "route_in 3 1, mlp_in 2 0, mlp_in 2 1, mlp_in 2 2", 10: "route_in 3 2"},
    ("mlp", 2): {1: "moe_out 0 0, attn_in 1 0, route 3 0", 2: "attn_in 1 1, route 1 2, route 3 1", 3: "attn_in 1 2, attn 1 0, route 1 3",
                 4: "attn 1 1 2, route 1 4", 5: "attn 1 3 4, route 1 5", 6: "attn 1 5 6, route 1 6",
                 7: "attn 1 7, route 1 7", 8: "attn 1 8, route 1 8, peer_in 2 0", 9: "attn 1 9", 10: "attn 1 10",
                 11: "mlp_in 3 0", 12: "mlp_in 3 1", 13: "mlp_in 3 2"},
    ("mlp", 3): {1: "mlp_out 2 0, attn_in 2 0", 2: "attn_in 2 1, route 3 2", 3: "attn_in 2 2, attn 2 0, route 3 3",
                 4: "attn 2 1 2, route 3 4", 5: "attn 2 3 4, route 3 5", 6: "attn 2 5 6, route 3 6",
                 7: "attn 2 7, route 3 7", 8: "attn 2 8, route 3 8, peer_in 3 0", 9: "attn 2 9", 10: "attn 2 10",
                 11: "moe_in 1 0 1", 12: "moe_in 1 2, weights 1 0, moe_in 1 3"},
    ("moe", 1): {1: "mlp_out 3 0, attn_in 3 0", 2: "attn_in 3 1", 3: "attn_in 3 2, attn 3 0", 4: "attn 3 1 2", 5: "attn 3 3 4",
                 6: "attn 3 5 6", 7: "attn 3 7", 8: "attn 3 8, moe_in 2 0 1", 9: "attn 3 9, moe_in 2 2, weights 2 0, moe_in 2 3", 10: "attn 3 10"},
    ("moe", 2): {1: "moe_out 1 0", 7: "moe_in 3 0", 8: "moe_in 3 1", 9: "moe_in 3 2, weights 3 0, moe_in 3 3"},
    ("moe", 3): {1: "moe_out 2 0", MOE_UNITS + LAG: "moe_out 3 0"},
}

SCHED = steps(START)
for kind, f in HOSTS:
    for part in range(kind == "mlp", 1 + host_units(kind) + LAG):
        SCHED.append((kind, f, part))
        if part in PLAN[(kind, f)]:
            SCHED += steps(PLAN[(kind, f)][part])

APPLY = {"wkv_in": 1, "route_in": 1, "attn_in": 1, "moe_in": 1, "mlp_in": 0}
TRANSPOSE = {kind: part + 1 for kind, part in APPLY.items()}
XN_ORDER = {s[:2]: n for n, s in enumerate(s for s in SCHED if APPLY.get(s[0]) == s[2])}
SPLIT_ORDER = {s: n for n, s in enumerate(s for s in XN_ORDER if s[0] in ("mlp_in", "moe_in"))}
STATS_ORDER = {s[:2]: n for n, s in enumerate(s for s in SCHED if s[0] in APPLY and s[0] != "mlp_in" and s[2] == 0)}
FIRST_UNIT = {h: sum(host_units(k) for k, _ in HOSTS[:n]) for n, h in enumerate(HOSTS)}
ALL_UNITS = [(kind, f, u) for kind, f in HOSTS for u in range(host_units(kind))]

ROUTE_TURN = {s[1]: n for n, s in enumerate(s for s in SCHED if s[0] == "route" and s[2] == 2)}

TANHS = {s: n + 1 for n, s in enumerate(s for s in ALL_UNITS if s[0] == "mlp" or s[2] == 0)}


def prep_seqs(g):
    return [2 * g, 2 * g + 1, 2 * g + 8, 2 * g + 9]


def main_seqs(f):
    return [MAIN_FIRST[f] + t for t in range(GT)]


def build(nc, io):
    with ExitStack() as ctx:
        def sb(name, shape, dt=F32):
            return ctx.enter_context(nc.sbuf_tensor(name, shape, dt))

        def sem(name):
            return ctx.enter_context(nc.semaphore(name))

        ring = [ctx.enter_context(nc.psum_tensor(f"ring{k}", [P, GN], F32)) for k in range(BANKS)]
        acc = [ctx.enter_context(nc.psum_tensor(f"acc{k}", [P, 2, D], F32)) for k in range(2)]

        x_nat = sb("x_nat", [P, NSEQ, D])
        kv_sum = sb("kv_sum", [P, NSEQ, C * KVW])
        small = sb("small", [P, P + 2 * C + 4])
        ident = small[:, 0:P]
        td = small[:, P:P + C]
        tf = small[:, P + C:P + 2 * C]
        gates = small[:, P + 2 * C:]
        identb = sb("identb", [P, P], BF16)
        later = sb("later", [P, LATER])
        at = [0]

        def const(width):
            at[0] += width
            return later[:, at[0] - width:at[0]]

        head_mask = const(KVW)
        iota8 = const(TOPK * TOPK).rearrange("p (r c) -> p r c", r=TOPK)
        iota_e = const(NE)
        e_bias = const(NE)
        rank_f = const(TOPK)
        wq0 = const(C * P).rearrange("p (c m) -> p c m", c=C)
        keys_bd = const(4 * NK).rearrange("p (a m) -> p a m", a=2)
        key_iota = sb("key_iota", [P, NK, TOPK], BF16)
        rank_w = sb("rank_w", [P, TOPK], BF16)
        decay = sb("decay", [P, C, GT * PAD])
        ew = sb("ew", [P, C])
        bias_a = sb("bias_a", [P, C])
        bias_b = sb("bias_b", [P, C])
        minus_half = sb("minus_half", [P, GT])
        ones_row = sb("ones_row", [1, P])
        bg = sb("bg", [1, D])
        wkv = sb("wkv", [P, C, 2 * D])
        wo = sb("wo", [P, C, D])
        up_h = sb("up_h", [P, 2, C, INTER], F32R)
        up_l = sb("up_l", [P, 2, C, INTER], F32R)
        exp_h = sb("exp_h", [P, C, NEXP], F32R)
        exp_l = sb("exp_l", [P, C, NEXP], F32R)
        wqg = sb("wqg", [P, C, 2 * D])
        gw_h = sb("gw_h", [P, C * NE], F32R)
        gw_l = sb("gw_l", [P, C * NE], F32R)
        picks = sb("picks", [P, NG, 4, TOPK + NK], BF16)
        exps = sb("exps", [P, NG, 4, TOPK + NK + 1])
        sel_picks = sb("sel_picks", [TOPK + NK, EC, P], BF16)
        sel_exps = sb("sel_exps", [TOPK + NK + 1, EC + 2, P], F32R)
        picks_t = sb("picks_t", [TOPK + NK, GN], BF16)
        mean_rstd = sb("mean_rstd", [P, NSEQ, 2])
        rstd2 = sb("rstd2", [P, NSEQ])

        xn = [sb(f"xn{k}", [P, GT, D]) for k in range(2)]
        stats = sb("stats", [P, 2, GT, 6])
        mv = sb("mv", [P, 2, GT, 2])
        var_eps = sb("var_eps", [P, 2, GT])
        rstd = sb("rstd", [P, 2, GT])
        v_t = [sb(f"v_t{c}", [P, GN]) for c in range(C)]
        main_a = [sb(f"main_a{c}", [P, 2, GT * PAD]) for c in range(C)]
        main_b = [sb(f"main_b{c}", [P, 2, GN]) for c in range(C)]
        logits_of = [sb(f"logits{k}", [P, 2 * GT, NK]) for k in range(2)]
        top_v = sb("top_v", [P, 8, TOPK])
        top_i = sb("top_i", [P, 8, TOPK], U32)
        pairs = sb("pairs", [P, 4, TOPK * TOPK])
        pair_top = sb("pair_top", [P, 4, TOPK])
        pair_rep = sb("pair_rep", [P, 4, TOPK * TOPK])
        pair_d = sb("pair_d", [P, 4, TOPK * TOPK])
        ix_f = sb("ix_f", [P, 4, TOPK])
        iy_b = sb("iy_b", [P, 4, TOPK], BF16)
        r_cnt = sb("r_cnt", [P, 4, TOPK])
        r_sum = sb("r_sum", [P, 4, TOPK])
        r_z = sb("r_z", [P, 4])
        onehot = sb("onehot", [P, 2, NK, TOPK], BF16)
        k_e = [sb(f"k_e{k}", [P, D]) for k in range(2)]
        k_r = [sb(f"k_r{k}", [P, D]) for k in range(2)]
        v_x = [sb(f"v_x{k}", [P, C, KVW]) for k in range(2)]
        xt_h = sb("xt_h", [P, C, GN], F32R)
        xt_l = sb("xt_l", [P, C, GN], F32R)
        xt_f_pad = sb("xt_f_pad", [P, 2 * GT * PAD])
        xt_f = xt_f_pad[:, 0:C * GN].rearrange("p (c n) -> p c n", c=C)
        act_s = [sb(f"act_s{k}", [P, GN]) for k in range(RING)]
        hid = [sb(f"hid{k}", [P, GN]) for k in range(RING)]
        w_down = [sb(f"w_down{k}", [P, D]) for k in range(RING)]
        host_s = sb("host_s", [P, 2, GN])
        q_f = sb("q_f", [P, C, GN])
        gate_s = sb("gate_s", [P, 2, 2 * D])
        er_pad = sb("er_pad", [P, 2 * GT * PAD])
        er_s = er_pad[:, 0:C * GN].rearrange("p (c n) -> p c n", c=C)
        pads = [pad[:, :].rearrange("p (s n) -> p s n", s=2) for pad in (xt_f_pad, er_pad)]
        ee_a_of = [pads if g == 1 else main_a for g in range(NG)]
        ee_b_of = [[q_f, gate_s] if g == 1 else main_b for g in range(NG)]
        v_of = [[act_s[1], act_s[2]] if g == 1 else v_t for g in range(NG)]
        att = [sb(f"att{k}", [P, D]) for k in range(2)]
        z_den = sb("z_den", [P, HEADS])
        s_e = sb("s_e", [P, GT, NE])
        s_b = sb("s_b", [P, GT, NE])
        s_top = sb("s_top", [P, GT, TOPK])
        s_idx = sb("s_idx", [P, GT, TOPK], U32)
        s_if = sb("s_if", [P, GT, 2])
        s_m = sb("s_m", [P, GT, NE])
        stage = [sb(f"stage{k}", [P, 2 * D]) for k in range(2)]
        ws_h = [sb(f"ws_h{k}", [P, C, 2, P], F32R) for k in range(2)]
        ws_l = [sb(f"ws_l{k}", [P, C, 2, P], F32R) for k in range(2)]

        bank_full = [sem(f"bank_full{k}") for k in range(BANKS)]
        bank_free = [sem(f"bank_free{k}") for k in range(BANKS)]
        small_loaded = sem("small_loaded")
        later_loaded = sem("later_loaded")
        wkv_loaded = sem("wkv_loaded")
        attn_loaded = sem("attn_loaded")
        sel_loaded = sem("sel_loaded")
        ctx_loaded = [sem(f"ctx_loaded{g}") for g in range(NG)]
        out_stored = sem("out_stored")
        casts_ready = sem("casts_ready")
        pool_setup = sem("pool_setup")
        dve_setup = sem("dve_setup")
        act_setup = sem("act_setup")
        var_ready = sem("var_ready")
        rstd_ready = sem("rstd_ready")
        xn_ready = sem("xn_ready")
        high_ready = sem("high_ready")
        ev_ready = sem("ev_ready")
        recip_ready = sem("recip_ready")
        y_ready = sem("y_ready")
        k_ready = sem("k_ready")
        diff_ready = sem("diff_ready")
        exp_ready = sem("exp_ready")
        routes_ready = sem("routes_ready")
        exps_high = sem("exps_high")
        peer_ready = sem("peer_ready")
        expert_tanh = sem("expert_tanh")
        tanh_ready = sem("tanh_ready")
        expert_ready = sem("expert_ready")
        down_done = sem("down_done")
        acc_free = sem("acc_free")
        scores_ready = sem("scores_ready")
        qf_ready = sem("qf_ready")
        gated_ready = sem("gated_ready")
        wsplit_h = sem("wsplit_h")
        wsplit_l = sem("wsplit_l")
        dve_link = sem("dve_link")
        act_link = sem("act_link")
        x_loaded = [sem(f"x_loaded{g}") for g in range(NG)]
        stage_loaded = [sem(f"stage_loaded{k}") for k in range(2)]
        down_loaded = [sem(f"down_loaded{k}") for k in range(RING)]

        jobs = []
        for half in range(2):
            for w, name in enumerate(("gate_up", "up_up")):
                for c in range(C):
                    s = slice(half * GN, (half + 1) * GN)
                    jobs.append((io[name][c * P:(c + 1) * P, s], up_h[:, w, c, s], up_l[:, w, c, s], GN))
        for c in range(C):
            jobs.append((io["down_embed_t"][c * P:(c + 1) * P, :], exp_h[:, c, :], exp_l[:, c, :], NEXP))
        jobs.append((io["gw_t"], gw_h[:, :], gw_l[:, :], C * NE))
        assert len(jobs) == SETUP_JOBS
        for f in range(NG):
            for e in range(MOE_UNITS):
                n = len(jobs) - SETUP_JOBS
                h, l = ws_h[n % 2], ws_l[n % 2]
                jobs.append((io["w13_t"][e], h[:, :, :, :].rearrange("p c w m -> p (c w m)"),
                             l[:, :, :, :].rearrange("p c w m -> p (c w m)"), 2 * D))

        def moe_job(f, e):
            return SETUP_JOBS + f * MOE_UNITS + e

        place = {}
        last_xt_read = {}

        def full(eng, key):
            k, n = place[key]
            eng.wait_ge(bank_full[k], n)
            return ring[k]

        def freed(eng, key):
            k, n = place[key]
            eng.wait_ge(bank_free[k], n)

        def free_sem(key):
            return bank_free[place[key][0]]

        def unit_of(kind, f, u):
            return FIRST_UNIT[(kind, f)] + u

        def hidden(eng, n):
            kind, f, u = ALL_UNITS[n]
            if kind == "mlp" and u >= IC:
                eng.wait_ge(peer_ready, EC * f + u - IC + 1)
            elif kind == "mlp" or u == 0:
                freed(eng, ((kind, f), "B", u))
            else:
                eng.wait_ge(expert_ready, NE * f + u)

        def xt_wait(eng, n):
            if n > 0:
                k, turn = place[last_xt_read[n - 1]]
                eng.wait_ge(bank_full[k], turn)

        def ws_wait(eng, j):
            if j >= SETUP_JOBS + 2:
                f, u = divmod(j - 2 - SETUP_JOBS, MOE_UNITS)
                full(eng, (("moe", f), "B", u))
            f, u = divmod(j - SETUP_JOBS, MOE_UNITS)
            if u < 2:
                before = [h for h in HOSTS[:HOSTS.index(("moe", f))] if h[0] == "mlp"][-1]
                full(eng, (before, "OVER"))

        exps_t_h = ws_h[0][0:TOPK + NK + 1, :, :, :].rearrange("p c w m -> p (c w m)")
        exps_t_l = ws_l[0][0:TOPK + NK + 1, :, :, :].rearrange("p c w m -> p (c w m)")

        key_iota_f = hid[0][:, :]
        sel_picks_f = hid[1][0:TOPK + NK, :]
        sel_exps_f = host_s[:, :, :].rearrange("p a b -> p (a b)")[0:TOPK + NK + 1, 0:(EC + 2) * P]

        block = ctx.enter_context(nc.Block())

        @block.tensor
        def _(pe):
            uses = [0]

            def open_bank(key):
                k, n = uses[0] % BANKS, uses[0] // BANKS + 1
                uses[0] += 1
                place[key] = (k, n)
                if n > 1:
                    pe.wait_ge(bank_free[k], n - 1)
                return ring[k]

            def close_bank(key, last):
                last.then_inc(bank_full[place[key][0]], 1)

            def transpose_xn(step):
                n = XN_ORDER[step]
                pe.wait_ge(xn_ready, n + 1)
                for c in range(C):
                    key = (step, "T", c)
                    bank = open_bank(key)
                    for t in range(GT):
                        last = pe.transpose(bank[:, t * P:(t + 1) * P], xn[n % 2][:, t, c * P:(c + 1) * P], ident)
                    close_bank(key, last)

            def three_pass(out, wh, wl, xh, xl, first, final):
                pe.matmul(out, wl, xh, start=first, stop=False, skip_group_check=True)
                pe.matmul(out, wh, xl, start=False, stop=False, skip_group_check=True)
                return pe.matmul(out, wh, xh, start=False, stop=final, skip_group_check=True)

            def up(step, name, u, wh, wl):
                key = (step, name, u)
                bank = open_bank(key)
                for c in range(C):
                    last = three_pass(bank[:, :], wh(c), wl(c), xt_h[:, c, :], xt_l[:, c, :], c == 0, c == C - 1)
                close_bank(key, last)
                return key

            def down(kind, f, u):
                n = unit_of(kind, f, u)
                if u == 0 and n > 0:
                    pe.wait_ge(acc_free, 2 * HOSTS.index((kind, f)))
                pe.wait_ge(down_loaded[n % RING], 16 * (n // RING + 1))
                hidden(pe, n)
                final = u == host_units(kind) - 1
                for t in range(GT):
                    last = pe.matmul(acc[t // 2][:, t % 2, :], hid[n % RING][:, t * P:(t + 1) * P], w_down[n % RING][:, :],
                                     start=u == 0 and t % 2 == 0, stop=final, skip_group_check=True)
                last.then_inc(down_done, 1)

            def spread(step, name, k):
                key = (step, name)
                bank = open_bank(key)
                pe.matmul(bank[:, :], sel_exps[:, k, :], exps_t_l, start=True, stop=False)
                last = pe.matmul(bank[:, :], sel_exps[:, k, :], exps_t_h, start=False, stop=True)
                close_bank(key, last)

            pe.wait_ge(small_loaded, 16)
            first_use = set()

            def once(name, sem, n):
                if name not in first_use:
                    first_use.add(name)
                    pe.wait_ge(sem, n)

            for kind, g, part in SCHED:
                step = (kind, g)
                if TRANSPOSE.get(kind) == part:
                    transpose_xn(step)
                elif kind == "wkv_out" and part >= 6:
                    p = part - 6
                    ee_b = ee_b_of[g]
                    pe.wait_ge(y_ready, C * (g + 1))
                    key = (step, "Y", p)
                    bank = open_bank(key)
                    for t in range(2):
                        for c in range(C):
                            last = pe.transpose(bank[:, (t * C + c) * P:(t * C + c + 1) * P],
                                                ee_b[c][:, 0, (2 * p + t) * P:(2 * p + t + 1) * P], ident)
                    close_bank(key, last)
                elif kind == "kv":
                    t = part
                    v = v_of[g]
                    once("wkv", wkv_loaded, 16)
                    once("pool_setup", pool_setup, 1)
                    if t == 0:
                        pe.wait_ge(ctx_loaded[g], 16 * C)
                    if t < GT:
                        key = (step, "K", t)
                        bank = open_bank(key)
                        for c in range(C):
                            last = pe.matmul(bank[:, :], v[c][:, t * P:(t + 1) * P], wkv[:, c, :],
                                             start=(c == 0), stop=(c == C - 1))
                        close_bank(key, last)
                    if t >= 1:
                        n = g * GT + t - 1
                        pe.wait_ge(k_ready, n + 1)
                        key = (step, "V", t - 1)
                        bank = open_bank(key)
                        for c in range(C):
                            last = pe.matmul(bank[:, c * KVW:(c + 1) * KVW], k_e[n % 2][:, c * P:(c + 1) * P],
                                             v_x[n % 2][:, c, :], start=True, stop=True)
                        close_bank(key, last)
                elif kind == "route" and part == 0:
                    ee_b = ee_b_of[g]
                    once("later", later_loaded, 16)
                    for c in range(C):
                        freed(pe, (("route_in", g), "T", c))
                    key = (step, "Q")
                    bank = open_bank(key)
                    for c in range(C):
                        last = pe.matmul(bank[:, :], wq0[:, c, :], ee_b[c][:, 1, :], start=(c == 0), stop=(c == C - 1))
                    close_bank(key, last)
                elif kind == "route" and part == 1:
                    freed(pe, (step, "Q"))
                    key = (step, "R")
                    bank = open_bank(key)
                    q_t = logits_of[g == 1][:, :, :].rearrange("p a b -> p (a b)")
                    for t in range(GT):
                        last = pe.matmul(bank[:, t * P:(t + 1) * P], q_t[:, t * P:(t + 1) * P],
                                         keys_bd[:, t // 2, :], start=True, stop=True)
                    close_bank(key, last)
                elif kind == "peer_in":
                    rg = MAIN_FIRST[g] // GT
                    once("casts", casts_ready, 1)
                    pe.wait_ge(routes_ready, ROUTE_TURN[rg] + 1)
                    key = (("peer_in", g), "PT")
                    bank = open_bank(key)
                    half_words = bank[0:TOPK + NK, 0:GN // 2].bitcast(BF16)
                    for r in range(4):
                        last = pe.transpose(half_words[:, r * P:(r + 1) * P], picks[:, rg, r, :], identb[:, :])
                    close_bank(key, last)
                    key = (("peer_in", g), "ET")
                    bank = open_bank(key)
                    for r in range(4):
                        last = pe.transpose(bank[0:TOPK + NK + 1, r * P:(r + 1) * P], exps[:, rg, r, :], ident)
                    close_bank(key, last)
                elif kind == "mlp" and part > 0:
                    u = part - 1
                    if u == 0:
                        for c in range(C):
                            freed(pe, (("mlp_in", g), "T", c))
                    once(("split", u // 4), wsplit_l, min(u // 4 + 1, 3) * 4 - (u >= IC) * (4 - C))
                    if IC <= u < MLP_UNITS:
                        e = u - IC
                        m = slice(e * P, (e + 1) * P)
                        up(step, "A", u, lambda c: exp_h[:, c, m], lambda c: exp_l[:, c, m])
                        if e == 0:
                            freed(pe, (("peer_in", g), "PT"))
                            freed(pe, (("peer_in", g), "ET"))
                            spread(step, "EY", EC)
                        key = (step, "RANK", u)
                        bank = open_bank(key)
                        last = pe.matmul(bank[:, :], sel_picks[:, e, :], picks_t[:, :], start=True, stop=True)
                        close_bank(key, last)
                        spread(step, ("EX", u), e)
                        if u == MLP_UNITS - 1:
                            last_xt_read[SPLIT_ORDER[("mlp_in", g)]] = (step, "A", u)
                            spread(step, "OVER", EC + 1)
                    elif u < IC:
                        m = slice(u * P, (u + 1) * P)
                        up(step, "A", u, lambda c: up_h[:, 0, c, m], lambda c: up_l[:, 0, c, m])
                        up(step, "B", u, lambda c: up_h[:, 1, c, m], lambda c: up_l[:, 1, c, m])
                    if u >= LAG:
                        down(kind, g, u - LAG)
                elif kind == "attn":
                    if part == 0:
                        once("attn", attn_loaded, 48)
                        for c in range(C):
                            freed(pe, (("attn_in", g), "T", c))
                    if part < 2:
                        c = part
                        key = (step, "Q", c)
                        bank = open_bank(key)
                        for k in range(C):
                            last = pe.matmul(bank[:, :], wqg[:, k, c * P:(c + 1) * P], xt_f[:, k, :],
                                             start=(k == 0), stop=(k == C - 1))
                        close_bank(key, last)
                    elif part < 4:
                        p = part - 2
                        key = (step, "G", p)
                        bank = open_bank(key)
                        for t in range(2):
                            o = bank[:, t * D:(t + 1) * D]
                            tok = slice((2 * p + t) * P, (2 * p + t + 1) * P)
                            pe.matmul(o, ones_row[:, :], bg[:, :], start=True, stop=False)
                            for k in range(C):
                                last = pe.matmul(o, xt_f[:, k, tok], wqg[:, k, D:], start=False, stop=(k == C - 1))
                        close_bank(key, last)
                    elif part < 8:
                        t = part - 4
                        if t == 0:
                            pe.wait_ge(qf_ready, C * (g + 1))
                        b = main_seqs(g)[t]
                        key = (step, "AT", t)
                        bank = open_bank(key)
                        for c in range(C):
                            last = pe.matmul(bank[:, c * KVW:(c + 1) * KVW], q_f[:, c, t * P:(t + 1) * P],
                                             kv_sum[:, b, c * KVW:(c + 1) * KVW], start=True, stop=True)
                        close_bank(key, last)
                    elif part == 8:
                        pe.wait_ge(gated_ready, GT * (g + 1))
                        for c in range(C):
                            key = (step, "T", c)
                            bank = open_bank(key)
                            for t in range(GT):
                                src = gate_s[:, t // 2, (t % 2) * D + c * P:(t % 2) * D + (c + 1) * P]
                                last = pe.transpose(bank[:, t * P:(t + 1) * P], src, ident)
                            close_bank(key, last)
                    else:
                        p = part - 9
                        if p == 0:
                            for c in range(C):
                                freed(pe, (step, "T", c))
                        key = (step, "O", p)
                        bank = open_bank(key)
                        for t in range(2):
                            tok = slice((2 * p + t) * P, (2 * p + t + 1) * P)
                            for c in range(C):
                                last = pe.matmul(bank[:, t * D:(t + 1) * D], er_s[:, c, tok], wo[:, c, :],
                                                 start=(c == 0), stop=(c == C - 1))
                        close_bank(key, last)
                elif kind == "moe" and part == 0:
                    for c in range(C):
                        freed(pe, (("moe_in", g), "T", c))
                    once("gate", wsplit_l, SETUP_JOBS)
                    key = (step, "S")
                    bank = open_bank(key)
                    for t in range(GT):
                        tok = slice(t * P, (t + 1) * P)
                        for k in range(C):
                            e = slice(k * NE, (k + 1) * NE)
                            last = three_pass(bank[:, t * NE:(t + 1) * NE], xt_h[:, k, tok], xt_l[:, k, tok],
                                              gw_h[:, e], gw_l[:, e], k == 0, k == C - 1)
                    close_bank(key, last)
                elif kind == "moe":
                    u = part - 1
                    if u < MOE_UNITS:
                        j = moe_job(g, u)
                        pe.wait_ge(wsplit_l, j + 1)
                        n = (j - SETUP_JOBS) % 2
                        if u > 0:
                            pe.wait_ge(scores_ready, g + 1)
                            key = (step, "W", u)
                            bank = open_bank(key)
                            for t in range(GT):
                                lhs = s_e[:, t, u - 1:u].broadcast_to([P, P])
                                last = pe.transpose(bank[:, t * P:(t + 1) * P], lhs, ident)
                            close_bank(key, last)
                        for w, name in enumerate("AB"):
                            key = up(step, name, u, lambda c: ws_h[n][:, c, w, :], lambda c: ws_l[n][:, c, w, :])
                        if u == MOE_UNITS - 1:
                            last_xt_read[SPLIT_ORDER[("moe_in", g)]] = key
                    if u >= LAG:
                        down(kind, g, u - LAG)

        @block.scalar
        def _(act):
            def split_high(j):
                _, h, _, cols = jobs[j]
                act.wait_ge(stage_loaded[j % 2], 16 * (j // 2 + 1))
                if j >= SETUP_JOBS:
                    ws_wait(act, j)
                act.activation(h, stage[j % 2][:, 0:cols], ACT.Copy).then_inc(wsplit_h, 1)

            def score_rows(step, g, u):
                bank = full(act, (step, "W", u))
                if u > 2:
                    freed(act, (step, "B", u - 2))
                elif u == 1:
                    hidden(act, unit_of("moe", g, 0) - 1)
                act.activation(host_s[:, u % 2, :], bank[:, :], ACT.Copy).then_inc(free_sem((step, "W", u)), 1)

            def cast_consts():
                act.wait_ge(later_loaded, 16)
                act.wait_ge(sel_loaded, 48)
                act.activation(key_iota[:, :, :].rearrange("p a b -> p (a b)"), key_iota_f, ACT.Copy)
                act.activation(rank_w[:, :], rank_f, ACT.Copy)
                act.activation(identb[:, :], ident, ACT.Copy)
                act.activation(sel_picks[:, :, :].rearrange("k c p -> k (c p)"), sel_picks_f, ACT.Copy)
                act.activation(sel_exps[:, :, :].rearrange("k c p -> k (c p)"), sel_exps_f,
                               ACT.Copy).then_inc(casts_ready, 1)

            act.wait_ge(small_loaded, 16)
            act.activation(gates, gates, ACT.Tanh).then_inc(act_setup, 1)
            act.activation(ew[:, :], td, ACT.Exp).then_inc(act_link, 1)
            act.wait_ge(act_link, 1)
            act.activation(ew[:, :], ew[:, :], ACT.Exp, scale=-1.0).then_inc(act_setup, 1)
            act.wait_ge(dve_setup, 1)
            for kind, g, part in SCHED:
                step = (kind, g)
                ee_a, ee_b = ee_a_of[g], ee_b_of[g]
                if kind == "wkv_in" and part == 2:
                    if g > 1:
                        full(act, (("route", 0 if g == 2 else 2), "Q"))
                    for c in range(C):
                        bank = full(act, (step, "T", c))
                        act.activation(ee_b[c][:, 1, :], bank[:, :], ACT.Exp, bias=bias_b[:, c:c + 1])
                        act.activation(ee_a[c][:, 1, :].rearrange("p (t s) -> p t s", t=GT)[:, :, 1:],
                                       bank[:, :].rearrange("p (t s) -> p t s", t=GT), ACT.Exp,
                                       bias=bias_a[:, c:c + 1]).then_inc(free_sem((step, "T", c)), 1)
                elif kind == "kv" and part < GT:
                    t = part
                    n = g * GT + t
                    bank = full(act, (step, "K", t))
                    if n >= 2:
                        prev = divmod(n - 2, GT)
                        full(act, (("kv", prev[0]), "V", prev[1]))
                    act.activation(k_e[n % 2][:, :], bank[:, 0:D], ACT.Exp)
                    act.activation(k_r[n % 2][:, :], bank[:, 0:D], ACT.Relu)
                    act.activation(v_x[n % 2][:, :, 0:P], bank[:, D:].rearrange("p (c m) -> p c m", c=C),
                                   ACT.Copy).then_inc(free_sem((step, "K", t)), 1)
                elif kind == "split":
                    split_high(part)
                    if part == 5:
                        cast_consts()
                elif kind == "route_in" and part == 2:
                    for c in range(C):
                        bank = full(act, (step, "T", c))
                        act.activation(ee_b[c][:, 1, :], bank[:, :], ACT.Copy).then_inc(free_sem((step, "T", c)), 1)
                elif kind == "route" and part == 0:
                    bank = full(act, (step, "Q"))
                    if g > 1:
                        act.wait_ge(routes_ready, ROUTE_TURN[0 if g == 2 else 2] + 1)
                    act.activation(logits_of[g == 1][:, :, :].rearrange("p a b -> p (a b)"), bank[:, :], ACT.Copy).then_inc(free_sem((step, "Q")), 1)
                elif kind == "route" and part == 1:
                    bank = full(act, (step, "R"))
                    act.activation(logits_of[g == 1][:, :, :].rearrange("p a b -> p (a b)"), bank[:, :],
                                   ACT.Copy).then_inc(free_sem((step, "R")), 1)
                elif kind == "route" and part == 4:
                    act.wait_ge(diff_ready, ROUTE_TURN[g] + 1)
                    act.activation(pair_d[:, :, :], pair_d[:, :, :], ACT.Exp)
                    act.activation(exps[:, g, :, 0:TOPK + NK], exps[:, g, :, 0:TOPK + NK], ACT.Exp).then_inc(exp_ready, 1)
                elif kind == "mlp_in" and part == 2 or kind == "moe_in" and part == 3:
                    xt_wait(act, SPLIT_ORDER[step])
                    for c in range(C):
                        bank = full(act, (step, "T", c))
                        act.activation(xt_h[:, c, :], bank[:, :], ACT.Copy).then_inc(high_ready, 1)
                elif kind == "attn_in" and part == 2:
                    for c in range(C):
                        bank = full(act, (step, "T", c))
                        act.activation(xt_f[:, c, :], bank[:, :], ACT.Copy).then_inc(free_sem((step, "T", c)), 1)
                elif kind == "attn" and part < 2:
                    c = part
                    bank = full(act, (step, "Q", c))
                    if c > 0 or g > 0:
                        act.wait_ge(qf_ready, C * g + c)
                    act.activation(er_s[:, 0, :], bank[:, :], ACT.Exp)
                    act.activation(er_s[:, 1, :], bank[:, :], ACT.Relu).then_inc(free_sem((step, "Q", c)), 1)
                elif kind == "attn" and part < 4:
                    p = part - 2
                    bank = full(act, (step, "G", p))
                    act.activation(gate_s[:, p, :], bank[:, :], ACT.Tanh,
                                   scale=0.5).then_inc(free_sem((step, "G", p)), 1)
                elif kind == "attn" and part == 8:
                    for c in range(C):
                        bank = full(act, (step, "T", c))
                        act.activation(er_s[:, c, :], bank[:, :], ACT.Copy).then_inc(free_sem((step, "T", c)), 1)
                elif kind == "moe" and part == 0:
                    bank = full(act, (step, "S"))
                    act.activation(s_e[:, :, :], bank[:, 0:GT * NE].rearrange("p (t e) -> p t e", t=GT), ACT.Exp,
                                   scale=-1.0).then_inc(free_sem((step, "S")), 1)
                elif kind == "weights":
                    split_high(moe_job(g, 0))
                    split_high(moe_job(g, 1))
                elif kind == "peer_in":
                    bank = full(act, (("peer_in", g), "PT"))
                    act.activation(picks_t[:, :], bank[0:TOPK + NK, 0:GN // 2].bitcast(BF16),
                                   ACT.Copy).then_inc(free_sem((("peer_in", g), "PT")), 1)
                    bank = full(act, (("peer_in", g), "ET"))
                    act.activation(exps_t_h, bank[0:TOPK + NK + 1, :], ACT.Copy).then_inc(exps_high, 1)
                elif kind in ("mlp", "moe") and 1 <= part <= host_units(kind):
                    u = part - 1
                    n = unit_of(kind, g, u)
                    if kind == "mlp" and u == IC:
                        hidden(act, n - 1)
                    if kind == "mlp" or u == 0:
                        bank = full(act, (step, "A", u))
                        if n >= RING:
                            hidden(act, n - RING)
                        act.activation(act_s[n % RING][:, :], bank[:, :], ACT.Tanh, scale=0.5).then_inc(tanh_ready, 1)
                    if kind == "mlp" and u == IC:
                        bank = full(act, (step, "EY"))
                        act.activation(host_s[:, 0, :], bank[:, :], ACT.Copy).then_inc(free_sem((step, "EY")), 1)
                    if kind == "moe":
                        if u > 0:
                            score_rows(step, g, u)
                            freed(act, (step, "A", u))
                            act.wait_ge(down_done, n - RING + 1)
                            act.activation(hid[n % RING][:, :], act_s[n % RING][:, :], ACT.Tanh,
                                           scale=0.5).then_inc(expert_tanh, 1)
                        if u + 2 < MOE_UNITS:
                            split_high(moe_job(g, u + 2))

        @block.vector
        def _(dve):
            links = [0]

            def link(ins):
                links[0] += 1
                ins.then_inc(dve_link, 1)
                dve.wait_ge(dve_link, links[0])

            def free(key, ins):
                ins.then_inc(free_sem(key), 1)
                freed(dve, key)

            def moments(step, seqs):
                n = STATS_ORDER[step] % 2
                keep = step[0] == "route_in"
                for t, b in enumerate(seqs):
                    last = dve.bn_stats(stats[:, n, t, :], x_nat[:, b, :])
                link(last)
                for t, b in enumerate(seqs):
                    out = mean_rstd[:, b, :] if keep else mv[:, n, t, :]
                    last = dve.bn_aggr(out, stats[:, n, t, :])
                link(last)
                for p in range(2):
                    b = seqs[2 * p]
                    var = mean_rstd[:, b:b + 2, 1] if keep else mv[:, n, 2 * p:2 * p + 2, 1]
                    last = dve.tensor_scalar(var_eps[:, n, 2 * p:2 * p + 2], var, LN_EPS, None, ALU.add)
                last.then_inc(var_ready, 1)

            def normalize(step, seqs):
                n = XN_ORDER[step]
                if n >= 2:
                    prev = [s for s, k in XN_ORDER.items() if k == n - 2][0]
                    full(dve, (prev, "T", C - 1))
                if step in STATS_ORDER:
                    o = STATS_ORDER[step]
                    dve.wait_ge(rstd_ready, o + 1)
                if step[0] == "route_in":
                    for p in range(2):
                        b = seqs[2 * p]
                        last = dve.tensor_copy(rstd2[:, b:b + 2], rstd[:, o % 2, 2 * p:2 * p + 2])
                    link(last)
                for t, b in enumerate(seqs):
                    if step[0] in ("route_in", "mlp_in"):
                        m, r = mean_rstd[:, b, 0:1], rstd2[:, b:b + 1]
                    else:
                        m, r = mv[:, o % 2, t, 0:1], rstd[:, o % 2, t:t + 1]
                    last = dve.tensor_scalar(xn[n % 2][:, t, :], x_nat[:, b, :], m, r, ALU.subtract, ALU.mult)
                last.then_inc(xn_ready, 1)

            def residual(out, bank, gate):
                return dve.scalar_tensor_tensor(out, bank, gates[:, gate:gate + 1], out, ALU.mult, ALU.add)

            def scale_expert(step, g, u):
                n = unit_of("moe", g, u)
                if n >= RING:
                    hidden(dve, n - RING)
                freed(dve, (step, "W", u))
                bank = full(dve, (step, "A", u))
                dve.tensor_tensor(act_s[n % RING][:, :], bank[:, :], host_s[:, u % 2, :],
                                  ALU.mult).then_inc(free_sem((step, "A", u)), 1)

            dve.wait_ge(small_loaded, 16)
            link(dve.tensor_scalar(bias_a[:, :], tf, 0.0, -1.0, ALU.max, ALU.mult))
            link(dve.tensor_scalar(bias_b[:, :], tf, U_LEAST, None, ALU.max))
            dve.tensor_tensor(bias_b[:, :], bias_b[:, :], bias_a[:, :], ALU.add).then_inc(dve_setup, 1)
            dve.wait_ge(act_setup, 2)
            dve.wait_ge(pool_setup, 1)
            dve.tensor_scalar(gates[:, 1::2], gates[:, 1::2], 0.5, None, ALU.mult)
            for c in range(C):
                last = dve.tensor_copy(decay[:, c, :].rearrange("p (t j) -> p t j", t=GT)[:, :, 1:],
                                       ew[:, c:c + 1].unsqueeze(2).broadcast_to([P, GT, P]))
            link(last)

            for kind, g, part in SCHED:
                step = (kind, g)
                ee_a, ee_b, logits = ee_a_of[g], ee_b_of[g], logits_of[g == 1]
                seqs = main_seqs(g) if kind in ("mlp_in", "attn_in", "moe_in") else prep_seqs(g)
                if step in STATS_ORDER and part == 0:
                    if kind == "wkv_in":
                        dve.wait_ge(x_loaded[g], 32)
                    moments(step, seqs)
                elif APPLY.get(kind) == part:
                    normalize(step, seqs)
                elif kind == "wkv_out" and part < 6:
                    c, stage_of = divmod(part, 3)
                    half = GN // 2
                    if stage_of == 0:
                        dve.wait_ge(ev_ready, C * g + c + 1)
                        for s in range(2):
                            a = ee_a[c][:, s, :]
                            last = dve.tensor_tensor_scan(a, decay[:, c, :], a, 0.0, ALU.mult, ALU.add)
                        link(last)
                    elif stage_of == 1:
                        past = ee_a[c][:, :, :].rearrange("p s (t j) -> p s t j", t=GT)[:, :, :, 0:P]
                        both = ee_b[c][:, :, :].rearrange("p s (t j) -> p s t j", t=GT)
                        link(dve.tensor_tensor(both, past, both, ALU.add))
                        link(dve.reciprocal(ee_b[c][:, 1, 0:half], ee_b[c][:, 1, 0:half]))
                    else:
                        dve.reciprocal(ee_b[c][:, 1, half:], ee_b[c][:, 1, half:]).then_inc(recip_ready, 1)
                elif kind == "wkv_out":
                    p = part - 6
                    bank = full(dve, (step, "Y", p))
                    b = seqs[2 * p]
                    free((step, "Y", p), residual(x_nat[:, b:b + 2, :].rearrange("p t d -> p (t d)"), bank[:, :], 0))
                elif kind == "kv":
                    t = part
                    if t < GT:
                        n = g * GT + t
                        freed(dve, (step, "K", t))
                        dve.scalar_tensor_tensor(k_e[n % 2][:, :], k_e[n % 2][:, :], 1.0, k_r[n % 2][:, :], ALU.min,
                                                 ALU.add).then_inc(k_ready, 1)
                    if t > 0:
                        bank = full(dve, (step, "V", t - 1))
                        if g == 0:
                            dve.wait_ge(later_loaded, 16)
                        free((step, "V", t - 1), dve.tensor_tensor(
                            kv_sum[:, seqs[t - 1], :].rearrange("p (c m) -> p c m", c=C),
                            bank[:, 0:C * KVW].rearrange("p (c m) -> p c m", c=C),
                            head_mask.unsqueeze(1).broadcast_to([P, C, KVW]), ALU.mult))
                elif kind == "route" and part == 2:
                    freed(dve, (step, "R"))
                    for r in range(8):
                        last = dve.max(top_v[:, r, :], logits[:, r, :])
                    link(last)
                elif kind == "route" and part == 3:
                    for r in range(8):
                        last = dve.max_index(top_i[:, r, :], top_v[:, r, :], logits[:, r, :])
                    pr = pairs[:, :, :].rearrange("p r (i j) -> p r i j", i=TOPK)
                    link(dve.tensor_tensor(pr, top_v[:, 0:4, :].unsqueeze(3).broadcast_to([P, 4, TOPK, TOPK]),
                                           top_v[:, 4:8, :].unsqueeze(2).broadcast_to([P, 4, TOPK, TOPK]), ALU.add))
                    for r in range(4):
                        last = dve.max(pair_top[:, r, :], pairs[:, r, :])
                    link(last)
                elif kind == "route" and part == 4:
                    for r in range(4):
                        dve.match_replace(pair_rep[:, r, :], pair_top[:, r, :], pairs[:, r, :], LOWEST)
                    dve.tensor_tensor(pair_d[:, :, :], pairs[:, :, :],
                                      pair_top[:, :, 0:1].broadcast_to([P, 4, TOPK * TOPK]), ALU.subtract)
                    dve.tensor_tensor(exps[:, g, :, 0:TOPK], logits[:, 0:4, 0:TOPK],
                                      top_v[:, 0:4, 0:1].broadcast_to([P, 4, TOPK]), ALU.subtract)
                    dve.tensor_tensor(exps[:, g, :, TOPK:TOPK + NK], logits[:, 4:8, :],
                                      top_v[:, 4:8, 0:1].broadcast_to([P, 4, NK]), ALU.subtract).then_inc(diff_ready, 1)
                    dve.wait_ge(diff_ready, ROUTE_TURN[g] + 1)
                elif kind == "route" and part == 5:
                    dve.tensor_copy(ix_f[:, :, :], top_i[:, 0:4, :])
                    dve.tensor_copy(iy_b[:, :, :], top_i[:, 4:8, :])
                    link(dve.tensor_tensor(pair_rep[:, :, :], pairs[:, :, :], pair_rep[:, :, :], ALU.not_equal))
                    pm = pair_rep[:, :, :].rearrange("p r (i j) -> p r i j", i=TOPK)
                    link(dve.tensor_reduce(r_cnt[:, :, :], pm, AX_X, ALU.add))
                    hot = pairs[:, :, :].rearrange("p r (i j) -> p r i j", i=TOPK)
                    table = iota8.unsqueeze(1).broadcast_to([P, 4, TOPK, TOPK])
                    link(dve.tensor_tensor(hot, ix_f[:, :, :].unsqueeze(2).broadcast_to([P, 4, TOPK, TOPK]), table,
                                           ALU.is_equal))
                    link(dve.tensor_tensor(hot, hot, r_cnt[:, :, :].unsqueeze(2).broadcast_to([P, 4, TOPK, TOPK]),
                                           ALU.mult))
                    with nc.allow_low_precision("counts up to 8 are exact in bfloat16"):
                        link(dve.tensor_reduce(picks[:, g, :, 0:TOPK], hot, AX_X, ALU.add))
                elif kind == "route" and part in (6, 7):
                    dve.wait_ge(casts_ready, 1)
                    a = part - 6
                    oh = onehot[:, :, :, :].rearrange("p h k j -> p (h k) j")
                    for h in range(2):
                        iy = iy_b[:, 2 * a + h, :].unsqueeze(1).broadcast_to([P, NK, TOPK])
                        last = dve.tensor_tensor(onehot[:, h, :, :], iy, key_iota[:, :, :], ALU.is_equal)
                    link(last)
                    rw = rank_w[:, :].unsqueeze(1).broadcast_to([P, 2 * NK, TOPK])
                    link(dve.tensor_tensor(oh, oh, rw, ALU.mult))
                    with nc.allow_low_precision("ranks up to 8 are exact in bfloat16"):
                        link(dve.tensor_reduce(picks[:, g, 2 * a:2 * a + 2, TOPK:], onehot[:, :, :, :], AX_X, ALU.add))
                elif kind == "route" and part == 8:
                    dve.wait_ge(exp_ready, ROUTE_TURN[g] + 1)
                    link(dve.tensor_tensor(pair_d[:, :, :], pair_d[:, :, :], pair_rep[:, :, :], ALU.mult))
                    pd = pair_d[:, :, :].rearrange("p r (i j) -> p r i j", i=TOPK)
                    link(dve.tensor_reduce(r_sum[:, :, :], pd, AX_X, ALU.add))
                    link(dve.tensor_reduce(r_z[:, :], r_sum[:, :, :], AX_X, ALU.add))
                    link(dve.reciprocal(r_z[:, :], r_z[:, :]))
                    zb = r_z[:, :].unsqueeze(2).broadcast_to([P, 4, TOPK])
                    dve.tensor_tensor(exps[:, g, :, 0:TOPK], exps[:, g, :, 0:TOPK], zb, ALU.mult)
                    link(dve.tensor_tensor(r_sum[:, :, :], r_sum[:, :, :], zb, ALU.mult))
                    link(dve.scalar_tensor_tensor(r_sum[:, :, :], ix_f[:, :, :], float(NEXP // NK), r_sum[:, :, :],
                                                  ALU.is_ge, ALU.mult))
                    dve.tensor_reduce(exps[:, g, :, TOPK + NK], r_sum[:, :, :], AX_X, ALU.add).then_inc(routes_ready, 1)
                    dve.wait_ge(routes_ready, ROUTE_TURN[g] + 1)
                elif kind == "mlp_in" and part == 2 or kind == "moe_in" and part == 3:
                    n = SPLIT_ORDER[step]
                    for c in range(C):
                        dve.wait_ge(high_ready, C * n + c + 1)
                        bank = full(dve, (step, "T", c))
                        dve.tensor_tensor(xt_l[:, c, :], bank[:, :], xt_h[:, c, :].bitcast(F32),
                                          ALU.subtract).then_inc(free_sem((step, "T", c)), 1)
                elif kind == "peer_in":
                    dve.wait_ge(exps_high, g + 1)
                    bank = full(dve, (("peer_in", g), "ET"))
                    dve.tensor_tensor(exps_t_l, bank[0:TOPK + NK + 1, :], exps_t_h.bitcast(F32),
                                      ALU.subtract).then_inc(free_sem((("peer_in", g), "ET")), 1)
                elif kind == "mlp" and 1 <= part <= MLP_UNITS:
                    u = part - 1
                    n = unit_of(kind, g, u)
                    s = act_s[n % RING]
                    dve.wait_ge(tanh_ready, TANHS[(kind, g, u)])
                    bank = full(dve, (step, "A", u))
                    free((step, "A", u), dve.scalar_tensor_tensor(s[:, :], s[:, :], 1.0, bank[:, :], ALU.add, ALU.mult))
                    if u >= IC:
                        if u == IC:
                            freed(dve, (step, "EY"))
                        w = host_s[:, 1, :]
                        bank = full(dve, (step, "RANK", u))
                        free((step, "RANK", u), dve.scalar_tensor_tensor(w, bank[:, :], float(TOPK), host_s[:, 0, :],
                                                                         ALU.is_gt, ALU.mult))
                        bank = full(dve, (step, ("EX", u)))
                        free((step, ("EX", u)), dve.tensor_tensor(w, w, bank[:, :], ALU.mult))
                        if u == MLP_UNITS - 1:
                            bank = full(dve, (step, "OVER"))
                            free((step, "OVER"), dve.tensor_tensor(w, w, bank[:, :], ALU.add))
                        dve.wait_ge(down_done, n - RING + 1)
                        for a in range(2):
                            r = slice(a * 2 * P, (a + 1) * 2 * P)
                            last = dve.tensor_tensor(hid[n % RING][:, r].rearrange("p (j h) -> p h j", h=2),
                                                     s[:, r].rearrange("p (j h) -> p h j", h=2),
                                                     w[:, r].rearrange("p (h j) -> p h j", h=2), ALU.mult)
                        last.then_inc(peer_ready, 1)
                        dve.wait_ge(peer_ready, EC * g + u - IC + 1)
                    else:
                        bank = full(dve, (step, "B", u))
                        if n >= RING:
                            dve.wait_ge(down_done, n - RING + 1)
                        elif n == 0:
                            dve.wait_ge(casts_ready, 1)
                        free((step, "B", u), dve.tensor_tensor(hid[n % RING][:, :], bank[:, :], s[:, :], ALU.mult))
                elif kind in ("mlp_out", "moe_out"):
                    host = HOSTS.index((kind[:3], g))
                    dve.wait_ge(down_done, unit_of(kind[:3], g, host_units(kind[:3])))
                    for p in range(2):
                        b = main_seqs(g)[2 * p]
                        residual(x_nat[:, b:b + 2, :], acc[p][:, :, :], 1 if kind == "mlp_out" else 3).then_inc(acc_free, 1)
                    dve.wait_ge(acc_free, 2 * (host + 1))
                elif kind == "attn" and part < 2:
                    c = part
                    freed(dve, (step, "Q", c))
                    dve.scalar_tensor_tensor(q_f[:, c, :], er_s[:, 0, :], 1.0, er_s[:, 1, :], ALU.min,
                                             ALU.add).then_inc(qf_ready, 1)
                elif kind == "attn" and 4 <= part < 8:
                    t = part - 4
                    freed(dve, (step, "G", t // 2))
                    bank = full(dve, (step, "AT", t))
                    sums = bank[:, 0:C * KVW].rearrange("p (c m) -> p c m", c=C)
                    z = z_den[:, :].rearrange("p (c m) -> p c m", c=C)
                    link(dve.tensor_scalar(z, sums[:, :, P:], Z_EPS, 2.0, ALU.add, ALU.mult))
                    link(dve.reciprocal(z_den[:, :], z_den[:, :]))
                    for c in range(C):
                        last = dve.tensor_tensor(
                            att[t % 2][:, c * P:(c + 1) * P].rearrange("p (h d) -> p h d", h=HC),
                            bank[:, c * KVW:c * KVW + P].rearrange("p (h d) -> p h d", h=HC),
                            z_den[:, c * HC:(c + 1) * HC].unsqueeze(2).broadcast_to([P, HC, HD]), ALU.mult)
                    free((step, "AT", t), last)
                    gate = gate_s[:, t // 2, (t % 2) * D:(t % 2 + 1) * D]
                    dve.scalar_tensor_tensor(gate, gate, 1.0, att[t % 2][:, :], ALU.add, ALU.mult).then_inc(gated_ready, 1)
                elif kind == "attn" and part > 8:
                    p = part - 9
                    bank = full(dve, (step, "O", p))
                    b = main_seqs(g)[2 * p]
                    free((step, "O", p), residual(x_nat[:, b:b + 2, :].rearrange("p t d -> p (t d)"), bank[:, :], 2))
                elif kind == "moe" and part == 0:
                    freed(dve, (step, "S"))
                    link(dve.tensor_scalar(s_b[:, :, :], s_e[:, :, :], 1.0, None, ALU.add))
                    link(dve.reciprocal(s_b[:, :, :], s_b[:, :, :]))
                    link(dve.tensor_tensor(s_m[:, :, :], s_b[:, :, :],
                                           e_bias.unsqueeze(1).broadcast_to([P, GT, NE]), ALU.add))
                    for t in range(GT):
                        last = dve.max(s_top[:, t, :], s_m[:, t, :])
                    link(last)
                    for t in range(GT):
                        last = dve.max_index(s_idx[:, t, :], s_top[:, t, :], s_m[:, t, :])
                    link(last)
                    link(dve.tensor_copy(s_if[:, :, :], s_idx[:, :, 0:2]))
                    tab = iota_e.unsqueeze(1).broadcast_to([P, GT, NE])
                    dve.tensor_tensor(s_m[:, :, :], tab, s_if[:, :, 0:1].broadcast_to([P, GT, NE]), ALU.is_equal)
                    link(dve.tensor_tensor(s_e[:, :, :], tab, s_if[:, :, 1:2].broadcast_to([P, GT, NE]),
                                           ALU.is_equal))
                    link(dve.tensor_tensor(s_m[:, :, :], s_m[:, :, :], s_e[:, :, :], ALU.add))
                    dve.tensor_tensor(s_e[:, :, :], s_m[:, :, :], s_b[:, :, :], ALU.mult).then_inc(scores_ready, 1)
                    dve.wait_ge(scores_ready, g + 1)
                elif kind == "moe" and part <= MOE_UNITS + 1:
                    u = part - 1
                    if u == 0:
                        n = unit_of(kind, g, u)
                        a, h = act_s[n % RING], hid[n % RING]
                        dve.wait_ge(tanh_ready, TANHS[(kind, g, u)])
                        bank = full(dve, (step, "A", u))
                        free((step, "A", u), dve.scalar_tensor_tensor(a[:, :], a[:, :], 1.0, bank[:, :], ALU.add,
                                                                      ALU.mult))
                        bank = full(dve, (step, "B", u))
                        dve.wait_ge(down_done, n - RING + 1)
                        free((step, "B", u), dve.tensor_tensor(h[:, :], bank[:, :], a[:, :], ALU.mult))
                    if u > 1:
                        u -= 1
                        n = unit_of(kind, g, u)
                        a, h = act_s[n % RING], hid[n % RING]
                        dve.wait_ge(expert_tanh, NE * g + u)
                        link(dve.scalar_tensor_tensor(a[:, :], h[:, :], 1.0, a[:, :], ALU.add, ALU.mult))
                        bank = full(dve, (step, "B", u))
                        free((step, "B", u), dve.tensor_tensor(h[:, :], bank[:, :], host_s[:, u % 2, :], ALU.mult))
                    if 0 < part - 1 < MOE_UNITS:
                        scale_expert(step, g, part - 1)

        @block.gpsimd
        def _(pool):
            pool.memset(minus_half[:, :], -0.5)
            pool.memset(ones_row[:, :], 1.0)
            for k in range(2):
                pool.memset(v_x[k][:, :, P:], 1.0)
            for c in range(C):
                pool.memset(decay[:, c, :].rearrange("p (t j) -> p t j", t=GT)[:, :, 0:1], 0.0)
                for ee_a in (main_a, pads):
                    last = pool.memset(ee_a[c][:, :, :].rearrange("p s (t j) -> p s t j", t=GT)[:, :, :, 0:1], 0.0)
            last.then_inc(pool_setup, 1)
            pool.wait_ge(pool_setup, 1)
            for kind, g, part in SCHED:
                step = (kind, g)
                todo = []
                ee_a, ee_b, v = ee_a_of[g], ee_b_of[g], v_of[g]
                if step in STATS_ORDER and part == 0:
                    n = STATS_ORDER[step]
                    pool.wait_ge(var_ready, n + 1)
                    pool.tensor_tensor(rstd[:, n % 2, :], var_eps[:, n % 2, :], minus_half[:, :],
                                       ALU.pow).then_inc(rstd_ready, 1)
                elif kind == "wkv_in" and part == 2:
                    pool.wait_ge(ctx_loaded[g], 16 * C)
                    for c in range(C):
                        freed(pool, (step, "T", c))
                        pool.tensor_tensor(ee_b[c][:, 0, :], ee_b[c][:, 1, :], v[c][:, :], ALU.mult)
                        va = ee_a[c][:, :, :].rearrange("p s (t j) -> p s t j", t=GT)[:, :, :, 1:]
                        pool.tensor_tensor(va[:, 0], va[:, 1], v[c][:, :].rearrange("p (t j) -> p t j", t=GT),
                                           ALU.mult).then_inc(ev_ready, 1)
                elif kind == "wkv_out" and part in (2, 5):
                    c = part // 3
                    pool.wait_ge(recip_ready, C * g + c + 1)
                    pool.tensor_tensor(ee_b[c][:, 0, :], ee_b[c][:, 0, :], ee_b[c][:, 1, :],
                                       ALU.mult).then_inc(y_ready, 1)
                elif kind == "split":
                    todo = [part]
                elif kind == "weights":
                    todo = [moe_job(g, 0), moe_job(g, 1)]
                elif kind == "moe" and 1 <= part <= MOE_UNITS + 1:
                    u = part - 1
                    if u > 1:
                        n = unit_of(kind, g, u - 1)
                        freed(pool, (step, "B", u - 1))
                        pool.tensor_tensor(hid[n % RING][:, :], hid[n % RING][:, :], act_s[n % RING][:, :],
                                           ALU.mult).then_inc(expert_ready, 1)
                    if u + 2 < MOE_UNITS:
                        todo = [moe_job(g, u + 2)]
                for j in todo:
                    _, h, l, cols = jobs[j]
                    pool.wait_ge(wsplit_h, j + 1)
                    pool.tensor_tensor(l, stage[j % 2][:, 0:cols], h.bitcast(F32), ALU.subtract).then_inc(wsplit_l, 1)

        @block.sync
        def _(sp):
            def load_x(g):
                for p in range(2):
                    b = prep_seqs(g)[2 * p]
                    sp.dma_start(x_nat[:, b:b + 2, :],
                                 io["x"][b:b + 2].rearrange("b p d -> p b d")).then_inc(x_loaded[g], 16)

            def load_job(j):
                src, _, _, cols = jobs[j]
                if j >= 2:
                    sp.wait_ge(wsplit_l, j - 1)
                sp.dma_start(stage[j % 2][:, 0:cols], src).then_inc(stage_loaded[j % 2], 16)

            def load_down(n):
                if n >= len(ALL_UNITS):
                    return
                kind, f, u = ALL_UNITS[n]
                if n >= RING:
                    sp.wait_ge(down_done, n - RING + 1)
                sp.dma_start(w_down[n % RING][:, :], io["down_" + kind][u]).then_inc(down_loaded[n % RING], 16)

            def load_ctx(g):
                for c in range(C):
                    sp.dma_start(v_of[g][c][:, :], io["ctx_t"][g, :, c, :]).then_inc(ctx_loaded[g], 16)

            load_x(0)
            sp.dma_start(small[:, :], io["small"]).then_inc(small_loaded, 16)
            load_x(1)
            load_ctx(0)
            sp.dma_start(wkv[:, :, :], io["wkv"]).then_inc(wkv_loaded, 16)
            load_ctx(1)
            load_job(0)
            load_job(1)
            sp.dma_start(later[:, :], io["later"]).then_inc(later_loaded, 16)
            for dst, name in ((key_iota_f, "key_iota"), (sel_picks_f, "sel_picks"), (sel_exps_f, "sel_exps")):
                sp.dma_start(dst, io[name]).then_inc(sel_loaded, 16)
            sp.dma_start(bg[:, :], io["bg"]).then_inc(attn_loaded, 16)
            stores = 0
            for kind, g, part in SCHED:
                step = (kind, g)
                if step == ("kv", 0) and part == GT:
                    sp.wait_ge(ev_ready, C)
                    full(sp, (step, "K", GT - 1))
                    load_ctx(2)
                    load_x(2)
                    load_x(3)
                elif step == ("wkv_out", 2) and part == 0:
                    sp.wait_ge(ev_ready, C * 3)
                    full(sp, (("kv", 2), "K", GT - 1))
                    load_ctx(3)
                elif step == ("kv", 1) and part == GT:
                    for n in range(RING):
                        load_down(n)
                    sp.dma_start(wqg[:, :, :], io["wqg"]).then_inc(attn_loaded, 16)
                    sp.dma_start(wo[:, :, :], io["wo"]).then_inc(attn_loaded, 16)
                elif kind == "split":
                    load_job(part + 2)
                elif kind in ("mlp", "moe") and part >= 1:
                    u = part - 1
                    if kind == "moe" and u < MOE_UNITS and moe_job(g, u) + 2 < len(jobs):
                        load_job(moe_job(g, u) + 2)
                    if u >= LAG:
                        load_down(unit_of(kind, g, u - LAG) + RING)
                if kind == "moe_out":
                    sp.wait_ge(acc_free, 2 * (HOSTS.index(("moe", g)) + 1))
                    for p in range(2):
                        b = main_seqs(g)[2 * p]
                        sp.dma_start(io["out"][b:b + 2].rearrange("b p d -> p b d"),
                                     x_nat[:, b:b + 2, :]).then_inc(out_stored, 16)
                        stores += 1
            sp.wait_ge(out_stored, 16 * stores)


def kernel(**inputs):
    import numpy as np
    import concourse.bacc as bacc
    from concourse.bass_utils import run_bass_kernel_spmd

    a = {k: np.asarray(v) for k, v in inputs.items()}

    def chunked(w):
        return np.ascontiguousarray(w.reshape(-1, P, w.shape[-1]).transpose(1, 0, 2))

    def everywhere(v):
        return np.ascontiguousarray(np.broadcast_to(v, (P,) + v.shape))

    ctx_t = a["ctx_2048"].transpose(2, 0, 1)
    ctx_g = np.stack([ctx_t[:, prep_seqs(g), :].reshape(C, P, GN).transpose(1, 0, 2) for g in range(NG)])
    keys = a["L0_ffn_keys"]
    keys_bd = np.zeros((P, 2, 2 * NK), keys.dtype)
    for h in range(2):
        keys_bd[h * NK:(h + 1) * NK, :, h * NK:(h + 1) * NK] = keys.transpose(1, 0, 2)
    w1 = np.concatenate([a["L1_ffn_sw1"][None], a["L1_ffn_w1"]])
    w3 = np.concatenate([a["L1_ffn_sw3"][None], a["L1_ffn_w3"]])
    w2 = np.concatenate([a["L1_ffn_sw2"][None], a["L1_ffn_w2"]])
    w13 = np.stack([w1, w3], 1).transpose(0, 3, 1, 2)
    w13 = w13.reshape(MOE_UNITS, C, P, 2 * P).transpose(0, 2, 1, 3).reshape(MOE_UNITS, P, 2 * D)
    head = np.arange(P) // HD
    mask = np.concatenate([head[:, None] == head[None, :], head[:, None] == np.arange(HC)[None, :]], 1)
    f32 = np.float32
    sel_picks = np.zeros((TOPK + NK, EC, P), f32)
    sel_exps = np.zeros((TOPK + NK + 1, EC + 2, P), f32)
    for p in range(P):
        for c in range(EC):
            sel_picks[c * P // NK + p // NK, c, p] = sel_exps[c * P // NK + p // NK, c, p] = 1
            sel_picks[TOPK + p % NK, c, p] = 1
        sel_exps[TOPK + p % NK, EC, p] = 1
    sel_exps[TOPK + NK, EC + 1, P - 1] = 1
    arrays = {
        "x": a["x"],
        "ctx_t": ctx_g,
        "small": np.concatenate([
            np.eye(P, dtype=f32), a["L0_xattn_time_decay"].reshape(C, P).T, a["L0_xattn_time_first"].reshape(C, P).T,
            everywhere(np.stack([a["g_xattn"], a["g_ffn"]], 1).reshape(-1))], 1),
        "later": np.concatenate([
            mask.astype(f32), everywhere(np.repeat(np.arange(TOPK, dtype=f32), TOPK)),
            everywhere(np.arange(NE, dtype=f32)), everywhere(a["L1_ffn_expert_bias"]),
            everywhere(TOPK - np.arange(TOPK, dtype=f32)), chunked(a["L0_ffn_W_q"]).reshape(P, -1),
            keys_bd.reshape(P, -1)], 1),
        "key_iota": everywhere(np.repeat(np.arange(NK, dtype=f32), TOPK)),
        "sel_picks": sel_picks.reshape(TOPK + NK, -1),
        "sel_exps": sel_exps.reshape(TOPK + NK + 1, -1),
        "bg": a["L1_xattn_bg"][None],
        "wkv": chunked(a["L1_xattn_Wkv"].T),
        "wo": chunked(a["L1_xattn_Wo"].T),
        "down_mlp": np.concatenate([a["L0_ffn_down_w"], a["L0_ffn_up_embed"]]).reshape(MLP_UNITS, P, D),
        "gate_up": a["L0_ffn_gate_w"],
        "up_up": a["L0_ffn_up_w"],
        "down_embed_t": a["L0_ffn_down_embed"].T,
        "wqg": chunked(np.concatenate([a["L1_xattn_Wq"].T, a["L1_xattn_Wg"].T], 1)),
        "gw_t": chunked(a["L1_ffn_gate_w"].T).reshape(P, C * NE),
        "w13_t": w13,
        "down_moe": w2.transpose(0, 2, 1),
    }
    nc = bacc.Bacc("TRN2", target_bir_lowering=False, num_devices=1)
    io, feeds = {}, {}
    for name, v in arrays.items():
        v = np.ascontiguousarray(v)
        feeds[f"in_{name}"] = v
        io[name] = nc.dram_tensor(f"in_{name}", v.shape, mybir.dt.from_np(v.dtype), kind="ExternalInput").ap()
    io["out"] = nc.dram_tensor("out_x", (NSEQ, P, D), F32, kind="ExternalOutput").ap()
    build(nc, io)
    r = run_bass_kernel_spmd(nc, [feeds], core_ids=[0])
    return r.results[0]["out_x"]
```

```python
from contextlib import ExitStack

import concourse.bass as bass
from concourse import mybir

ALU = mybir.AluOpType
ACT = mybir.ActivationFunctionType
F32 = mybir.dt.float32
F32R = mybir.dt.float32r
BF16 = mybir.dt.bfloat16
U32 = mybir.dt.uint32
AX_X = mybir.AxisListType.X

P = 128
NSEQ = 16
D = 256
C = D // P
GT = 4
GN = GT * P
NG = NSEQ // GT
NK = 64
TOPK = 8
NEXP = 512
EC = NEXP // P
HEADS = 16
HD = D // HEADS
HC = HEADS // C
KVW = P + HC
IC = 1024 // P
NE = 8
LN_EPS = 1e-5
Z_EPS = 1e-6
U_LEAST = -60.0
LOWEST = -3.0e38
BANKS = 6
LATER = KVW + TOPK * TOPK + (3 + C) * NE + TOPK + C * P + 4 * NK
BG_ROW = 32
PAD = P + 1

MAIN_FIRST = [0, 8, 4, 12]
MLP_UNITS = IC + EC
MOE_UNITS = 1 + NE
LAG = 3
RING = LAG + 1
SLOTS = 5
UP = 2 * D
PEER_UP = D


HOSTS = [("mlp", 0), ("mlp", 1), ("moe", 0), ("mlp", 2), ("mlp", 3), ("moe", 1), ("moe", 2), ("moe", 3)]


BEHIND = {"mlp": 1, "moe": 2}


def host_units(kind):
    return MLP_UNITS if kind == "mlp" else MOE_UNITS


def steps(text):
    out = []
    for item in text.split(","):
        kind, g, *which = item.split()
        out += [(kind, int(g), int(part)) for part in which]
    return out


START = """wkv_in 0 0 1, wkv_in 1 0, setup 0 0, wkv_in 1 1, split 0 0, wkv_in 0 2, wkv_out 0 0, wkv_in 1 2,
    split 0 1, kv 0 0, wkv_out 0 1, casts 0 0, kv 0 1, wkv_out 0 2 3, casts 0 1, wkv_out 0 4 5, kv 0 2 3,
    wkv_out 1 0 1, wkv_out 0 6, wkv_out 1 2, wkv_out 0 7, wkv_out 1 3, kv 0 4, kv 1 0, route_in 0 0,
    kv 1 1, wkv_out 1 4, route_in 0 1, kv 1 2 3, route_in 0 2, wkv_out 1 5, kv 2 0, route 0 0,
    wkv_out 1 6 7, route_in 1 0, kv 2 1, route_in 1 1, kv 1 4, mlp_in 0 0, kv 2 2 3, mlp_in 0 1 2,
    kv 2 4"""

PLAN = {
    ("mlp", 0): {
        1: "route 0 1 2 3, route_in 1 2",
        2: "route 1 0",
        3: "route 1 1, wkv_in 2 0",
        4: "wkv_in 2 1, route 0 4",
        5: "route 0 5 6, wkv_in 2 2",
        7: "route 0 7 8",
        8: "wkv_out 2 0, peer_in 0 0, wkv_out 2 1 2 3",
        9: "wkv_out 2 4 5",
        10: "mlp_in 1 0",
        11: "wkv_out 2 6 7",
        13: "mlp_in 1 1 2, mlp 0 14 15, route_in 2 0 1",
    },
    ("mlp", 1): {
        1: "mlp_out 0 0, route_in 2 2, attn_in 0 0",
        2: "route 2 0, attn_in 0 1",
        3: "attn_in 0 2, route 2 1, attn 0 0 1 2 3, route 2 2 3 4",
        5: "attn 0 4",
        6: "attn 0 5, route 2 5, attn 0 6 7",
        7: "route 2 6 7, attn 0 8, route 2 8",
        8: "attn 0 9, peer_in 1 0",
        10: "attn 0 10, moe_in 0 0",
        11: "moe_in 0 1",
        13: "mlp 1 14, wkv_in 3 0, moe_in 0 2 3, mlp 1 15",
    },
    ("moe", 0): {
        2: "wkv_in 3 1, kv 3 0 1",
        3: "wkv_in 3 2, mlp_out 1 0",
        4: "kv 3 2",
        5: "wkv_out 3 0 1 2 3, kv 3 3",
        6: "kv 3 4",
        7: "wkv_out 3 4 5",
        8: "wkv_out 3 6 7, route_in 3 0",
        9: "route_in 3 1",
        10: "route_in 3 2",
        11: "mlp_in 2 0 1, moe 0 12, mlp_in 2 2",
    },
    ("mlp", 2): {
        1: "attn_in 1 0, route 3 0",
        2: "attn_in 1 1, route 1 2, moe_out 0 0, route 3 1",
        3: "attn_in 1 2",
        4: "route 1 3 4",
        5: "attn 1 0 1 2 3 4 5 6",
        6: "attn 1 7, route 1 5, attn 1 8, route 1 6 7",
        7: "route 1 8",
        8: "attn 1 9 10, peer_in 2 0",
        11: "mlp_in 3 0",
        12: "mlp_in 3 1 2",
        13: "mlp 2 14 15, mlp_out 2 0, attn_in 2 0",
    },
    ("mlp", 3): {
        2: "attn_in 2 1, route 3 2 3",
        3: "attn_in 2 2",
        4: "attn 2 0 1 2, route 3 4 5",
        5: "attn 2 3 4 5 6 7",
        7: "attn 2 8, route 3 6 7 8, attn 2 9",
        8: "peer_in 3 0",
        9: "moe_in 1 0",
        10: "attn 2 10",
        11: "moe_in 1 1",
        13: "mlp 3 14, moe_in 1 2 3, mlp 3 15",
    },
    ("moe", 1): {
        0: "mlp_out 3 0, attn_in 3 0",
        3: "attn_in 3 1 2",
        4: "attn 3 0 1 2",
        5: "attn 3 3 4, moe_in 2 0",
        6: "attn 3 5 6",
        7: "attn 3 7",
        8: "moe_in 2 1",
        9: "moe_in 2 2, attn 3 8 9",
        10: "moe_in 2 3",
        11: "attn 3 10",
    },
    ("moe", 2): {
        3: "moe 1 12, moe_out 1 0",
        7: "moe_in 3 0",
        9: "moe_in 3 1 2 3",
    },
    ("moe", 3): {
        2: "moe 2 12",
        3: "moe_out 2 0",
        11: "moe 3 12, moe_out 3 0",
    },
}

SCHED = steps(START)
for kind, f in HOSTS:
    for part in range(kind == "mlp", 1 + host_units(kind) + BEHIND[kind]):
        SCHED.append((kind, f, part))
        if part in PLAN[(kind, f)]:
            SCHED += steps(PLAN[(kind, f)][part])

APPLY = {"wkv_in": 1, "route_in": 1, "attn_in": 1, "moe_in": 1, "mlp_in": 0}
TRANSPOSE = {kind: part + 1 for kind, part in APPLY.items()}
XN_ORDER = {s[:2]: n for n, s in enumerate(s for s in SCHED if APPLY.get(s[0]) == s[2])}
SPLIT_ORDER = {s: n for n, s in enumerate(s for s in XN_ORDER if s[0] in ("mlp_in", "moe_in"))}
STATS_ORDER = {s[:2]: n for n, s in enumerate(s for s in SCHED if s[0] in APPLY and s[0] != "mlp_in" and s[2] == 0)}
FIRST_UNIT = {h: sum(host_units(k) for k, _ in HOSTS[:n]) for n, h in enumerate(HOSTS)}
ALL_UNITS = [(kind, f, u) for kind, f in HOSTS for u in range(host_units(kind))]

ROUTE_TURN = {s[1]: n for n, s in enumerate(s for s in SCHED if s[0] == "route" and s[2] == 2)}

TANHS = {s: n + 1 for n, s in enumerate(s for s in ALL_UNITS if s[0] == "mlp" or s[2] == 0)}


HID_TURN = {s: n + 1 for n, s in enumerate(s for s in ALL_UNITS if (s[2] >= IC if s[0] == "mlp" else s[2] > 0))}


def prep_seqs(g):
    return [2 * g, 2 * g + 1, 2 * g + 8, 2 * g + 9]


def main_seqs(f):
    return [MAIN_FIRST[f] + t for t in range(GT)]


def build(nc, io):
    with ExitStack() as ctx:
        def sb(name, shape, dt=F32):
            return ctx.enter_context(nc.sbuf_tensor(name, shape, dt))

        def sem(name):
            return ctx.enter_context(nc.semaphore(name))

        ring = [ctx.enter_context(nc.psum_tensor(f"ring{k}", [P, GN], F32)) for k in range(BANKS)]
        acc = [ctx.enter_context(nc.psum_tensor(f"acc{k}", [P, 2, D], F32)) for k in range(2)]

        x_nat = sb("x_nat", [P, NSEQ, D])
        kv_sum = sb("kv_sum", [P, NSEQ, C * KVW])
        small = sb("small", [P, P + 2 * C + 4])
        ident = small[:, 0:P]
        td = small[:, P:P + C]
        tf = small[:, P + C:P + 2 * C]
        gates = small[:, P + 2 * C:]
        identb = sb("identb", [P, P], BF16)
        later = sb("later", [P, LATER])
        at = [0]

        def const(width):
            at[0] += width
            return later[:, at[0] - width:at[0]]

        head_mask = const(KVW)
        iota8 = const(TOPK * TOPK).rearrange("p (r c) -> p r c", r=TOPK)
        iota_e = const(NE)
        e_bias = const(NE)
        rank_f = const(TOPK)
        row_sel_f = const(NE)
        gw_f = const(C * NE)
        wq0 = const(C * P).rearrange("p (c m) -> p c m", c=C)
        keys_bd = const(4 * NK).rearrange("p (a m) -> p a m", a=2)
        key_iota = sb("key_iota", [P, NK, TOPK], BF16)
        rank_w = sb("rank_w", [P, TOPK], BF16)
        decay = sb("decay", [P, C, GT * PAD])
        ew = sb("ew", [P, C])
        bias_a = sb("bias_a", [P, C])
        bias_b = sb("bias_b", [P, C])
        minus_half = sb("minus_half", [P, GT])
        wkv = sb("wkv", [P, C, 2 * D])
        wo = sb("wo", [P, C, D])
        exps_t_h = sb("exps_t_h", [TOPK + NK + 1, GN], F32R)
        exps_t_l = sb("exps_t_l", [TOPK + NK + 1, GN], F32R)
        wqg = sb("wqg", [P, C, 2 * D])
        gw_h = sb("gw_h", [P, C * NE], F32R)
        gw_l = sb("gw_l", [P, C * NE], F32R)
        picks = sb("picks", [P, NG, 4, TOPK + NK], BF16)
        exps = sb("exps", [P, NG, 4, TOPK + NK + 1])
        sel_picks = sb("sel_picks", [TOPK + NK, EC, P], BF16)
        sel_exps = sb("sel_exps", [TOPK + NK + 1, EC + 2, P], F32R)
        picks_t = sb("picks_t", [TOPK + NK, GN], BF16)
        mean_rstd = sb("mean_rstd", [P, NSEQ, 2])
        rstd2 = sb("rstd2", [P, NSEQ])

        xn = [sb(f"xn{k}", [P, GT, D]) for k in range(2)]
        stats = sb("stats", [P, 2, GT, 6])
        mv = sb("mv", [P, 2, GT, 2])
        var_eps = sb("var_eps", [P, 2, GT])
        rstd = sb("rstd", [P, 2, GT])
        v_t = [sb(f"v_t{c}", [P, GN]) for c in range(C)]
        main_a = [sb(f"main_a{c}", [P, 2, GT * PAD]) for c in range(C)]
        main_b = [sb(f"main_b{c}", [P, 2, GN]) for c in range(C)]
        logits_of = [sb(f"logits{k}", [P, 2 * GT, NK]) for k in range(2)]
        top_v = sb("top_v", [P, 8, TOPK])
        top_i = sb("top_i", [P, 8, TOPK], U32)
        pairs = sb("pairs", [P, 4, TOPK * TOPK])
        pair_top = sb("pair_top", [P, 4, TOPK])
        pair_rep = sb("pair_rep", [P, 4, TOPK * TOPK])
        pair_d = sb("pair_d", [P, 4, TOPK * TOPK])
        ix_f = sb("ix_f", [P, 4, TOPK])
        iy_b = sb("iy_b", [P, 4, TOPK], BF16)
        r_cnt = sb("r_cnt", [P, 4, TOPK])
        r_sum = sb("r_sum", [P, 4, TOPK])
        r_z = sb("r_z", [P, 4])
        onehot = sb("onehot", [P, 2, NK, TOPK], BF16)
        k_e = [sb(f"k_e{k}", [P, D]) for k in range(2)]
        k_r = [sb(f"k_r{k}", [P, D]) for k in range(2)]
        v_x = [sb(f"v_x{k}", [P, C, KVW]) for k in range(2)]
        xt_h = sb("xt_h", [P, C, GN], F32R)
        xt_l = sb("xt_l", [P, C, GN], F32R)
        xt_f_pad = sb("xt_f_pad", [P, 2 * GT * PAD])
        xt_f = xt_f_pad[:, 0:C * GN].rearrange("p (c n) -> p c n", c=C)
        act_s = [sb(f"act_s{k}", [P, GN]) for k in range(RING)]
        hid_h = [sb(f"hid_h{k}", [P, GN], F32R) for k in range(RING)]
        hid_l = [sb(f"hid_l{k}", [P, GN], F32R) for k in range(RING)]
        th = [sb(f"th{k}", [P, GN]) for k in range(2)]
        host_s = sb("host_s", [P, 2, GN])
        q_f = sb("q_f", [P, C, GN])
        gate_s = sb("gate_s", [P, 2, 2 * D])
        er_pad = sb("er_pad", [P, 2 * GT * PAD])
        er_s = er_pad[:, 0:C * GN].rearrange("p (c n) -> p c n", c=C)
        pads = [pad[:, :].rearrange("p (s n) -> p s n", s=2) for pad in (xt_f_pad, er_pad)]
        ee_a_of = [pads if g == 1 else main_a for g in range(NG)]
        ee_b_of = [[q_f, gate_s] if g == 1 else main_b for g in range(NG)]
        v_of = [[act_s[1], act_s[2]] if g == 1 else v_t for g in range(NG)]
        att = k_e
        z_den = sb("z_den", [P, HEADS])
        s_e = sb("s_e", [P, GT, NE])
        s_b = sb("s_b", [P, GT, NE])
        s_top = sb("s_top", [P, GT, TOPK])
        s_idx = sb("s_idx", [P, GT, TOPK], U32)
        s_if = sb("s_if", [P, GT, 2])
        s_m = sb("s_m", [P, GT, NE])
        s_split = sb("s_split", [P, GT, 2 * NE], F32R)
        row_data = sb("row_data", [BG_ROW + 1, GN], F32R)
        score_t = row_data[0:2 * NE, :]
        bg_h = row_data[BG_ROW:, 0:D].unsqueeze(1)
        bg_l = row_data[BG_ROW:, D:].unsqueeze(1)
        row_sel = sb("row_sel", [BG_ROW + 1, NE], F32R)
        sel_score = row_sel[0:2 * NE, :]
        one = row_sel[BG_ROW:, 0:1]
        stage = [sb(f"stage{k}", [P, UP + D]) for k in range(2)]
        ws_h = [sb(f"ws_h{k}", [P, UP + D], F32R) for k in range(SLOTS)]
        ws_l = [sb(f"ws_l{k}", [P, UP + D], F32R) for k in range(SLOTS)]

        bank_full = [sem(f"bank_full{k}") for k in range(BANKS)]
        bank_free = [sem(f"bank_free{k}") for k in range(BANKS)]
        small_loaded = sem("small_loaded")
        later_loaded = sem("later_loaded")
        wkv_loaded = sem("wkv_loaded")
        attn_loaded = sem("attn_loaded")
        sel_loaded = sem("sel_loaded")
        ctx_loaded = [sem(f"ctx_loaded{g}") for g in range(NG)]
        out_stored = sem("out_stored")
        casts_ready = sem("casts_ready")
        bg_ready = sem("bg_ready")
        pool_setup = sem("pool_setup")
        dve_setup = sem("dve_setup")
        act_setup = sem("act_setup")
        var_ready = sem("var_ready")
        rstd_ready = sem("rstd_ready")
        xn_ready = sem("xn_ready")
        high_ready = sem("high_ready")
        ev_ready = sem("ev_ready")
        first_values = sem("first_values")
        scanned = sem("scanned")
        past_added = sem("past_added")
        recip_ready = sem("recip_ready")
        y_ready = sem("y_ready")
        k_ready = sem("k_ready")
        diff_ready = sem("diff_ready")
        exp_ready = sem("exp_ready")
        routes_ready = sem("routes_ready")
        exps_high = sem("exps_high")
        expert_tanh = sem("expert_tanh")
        tanh_ready = sem("tanh_ready")
        hid_ready = sem("hid_ready")
        hid_high = sem("hid_high")
        hid_low = sem("hid_low")
        down_done = sem("down_done")
        acc_free = sem("acc_free")
        scores_ready = sem("scores_ready")
        qf_ready = sem("qf_ready")
        gated_ready = sem("gated_ready")
        wsplit_h = sem("wsplit_h")
        wsplit_l = sem("wsplit_l")
        dve_link = sem("dve_link")
        act_link = sem("act_link")
        x_loaded = [sem(f"x_loaded{g}") for g in range(NG)]
        stage_loaded = [sem(f"stage_loaded{k}") for k in range(2)]

        def block_cols(n):
            kind, _, u = ALL_UNITS[n]
            return (PEER_UP if kind == "mlp" and u >= IC else UP) + D

        def block_source(n):
            kind, _, u = ALL_UNITS[n]
            if kind == "moe":
                return io["w_moe"][u]
            return io["w_mlp"][u] if u < IC else io["w_peer"][u - IC]

        place = {}
        last_xt_read = {}

        def full(eng, key):
            k, n = place[key]
            eng.wait_ge(bank_full[k], n)
            return ring[k]

        def freed(eng, key):
            k, n = place[key]
            eng.wait_ge(bank_free[k], n)

        def weigh_values(eng, g, c):
            ee_a, ee_b, v = ee_a_of[g], ee_b_of[g], v_of[g]
            eng.wait_ge(ctx_loaded[g], 16 * C)
            freed(eng, (("wkv_in", g), "T", c))
            eng.tensor_tensor(ee_b[c][:, 0, :], ee_b[c][:, 1, :], v[c][:, :], ALU.mult)
            va = ee_a[c][:, :, :].rearrange("p s (t j) -> p s t j", t=GT)[:, :, :, 1:]
            return eng.tensor_tensor(va[:, 0], va[:, 1], v[c][:, :].rearrange("p (t j) -> p t j", t=GT), ALU.mult)

        def free_sem(key):
            return bank_free[place[key][0]]

        def unit_of(kind, f, u):
            return FIRST_UNIT[(kind, f)] + u

        def hidden_made(eng, n):
            kind, f, u = ALL_UNITS[n]
            if ALL_UNITS[n] in HID_TURN:
                eng.wait_ge(hid_ready, HID_TURN[ALL_UNITS[n]])
            else:
                freed(eng, ((kind, f), "B", u))

        def xt_wait(eng, n):
            if n > 0:
                k, turn = place[last_xt_read[n - 1]]
                eng.wait_ge(bank_full[k], turn)

        key_iota_f = th[0][:, :]
        bg_f = act_s[0][BG_ROW:BG_ROW + 1, 0:D].unsqueeze(1)
        sel_picks_f = th[1][0:TOPK + NK, :]
        sel_exps_f = host_s[:, :, :].rearrange("p a b -> p (a b)")[0:TOPK + NK + 1, 0:(EC + 2) * P]

        block = ctx.enter_context(nc.Block())

        @block.tensor
        def _(pe):
            uses = [0]

            def open_bank(key):
                k, n = uses[0] % BANKS, uses[0] // BANKS + 1
                uses[0] += 1
                place[key] = (k, n)
                if n > 1:
                    pe.wait_ge(bank_free[k], n - 1)
                return ring[k]

            def close_bank(key, last):
                last.then_inc(bank_full[place[key][0]], 1)

            def transpose_xn(step):
                n = XN_ORDER[step]
                pe.wait_ge(xn_ready, n + 1)
                for c in range(C):
                    key = (step, "T", c)
                    bank = open_bank(key)
                    for t in range(GT):
                        last = pe.transpose(bank[:, t * P:(t + 1) * P], xn[n % 2][:, t, c * P:(c + 1) * P], ident)
                    close_bank(key, last)

            def three_pass(out, wh, wl, xh, xl, first, final):
                pe.matmul(out, wl, xh, start=first, stop=False, skip_group_check=True)
                pe.matmul(out, wh, xl, start=False, stop=False, skip_group_check=True)
                return pe.matmul(out, wh, xh, start=False, stop=final, skip_group_check=True)

            def block_up(step, name, u, slot, place_of):
                key = (step, name, u)
                bank = open_bank(key)
                for c in range(C):
                    cols = slice(place_of(c) * P, (place_of(c) + 1) * P)
                    last = three_pass(bank[:, :], ws_h[slot][:, cols], ws_l[slot][:, cols], xt_h[:, c, :], xt_l[:, c, :],
                                      c == 0, c == C - 1)
                close_bank(key, last)
                return key

            def down(kind, f, u):
                n = unit_of(kind, f, u)
                if u == 0 and n > 0:
                    pe.wait_ge(acc_free, 2 * HOSTS.index((kind, f)))
                pe.wait_ge(hid_low, n + 1)
                final = u == host_units(kind) - 1
                k, slot, cols = n % RING, n % SLOTS, slice(block_cols(n) - D, block_cols(n))
                for t in range(GT):
                    tok = slice(t * P, (t + 1) * P)
                    last = three_pass(acc[t // 2][:, t % 2, :], hid_h[k][:, tok], hid_l[k][:, tok], ws_h[slot][:, cols],
                                      ws_l[slot][:, cols], u == 0 and t % 2 == 0, final)
                last.then_inc(down_done, 1)

            def spread(step, name, k):
                key = (step, name)
                bank = open_bank(key)
                pe.matmul(bank[:, :], sel_exps[:, k, :], exps_t_l[:, :], start=True, stop=False)
                last = pe.matmul(bank[:, :], sel_exps[:, k, :], exps_t_h[:, :], start=False, stop=True)
                close_bank(key, last)

            def weigh(step, u):
                key = (step, "W", u)
                bank = open_bank(key)
                lhs = sel_score[:, u - 1:u].broadcast_to([2 * NE, P])
                close_bank(key, pe.matmul(bank[:, :], lhs, score_t, start=True, stop=True))

            pe.wait_ge(small_loaded, 16)
            first_use = set()

            def once(name, sem, n):
                if name not in first_use:
                    first_use.add(name)
                    pe.wait_ge(sem, n)

            for kind, g, part in SCHED:
                step = (kind, g)
                if TRANSPOSE.get(kind) == part:
                    transpose_xn(step)
                elif kind == "wkv_out" and part >= 6:
                    p = part - 6
                    ee_b = ee_b_of[g]
                    pe.wait_ge(y_ready, C * (g + 1))
                    key = (step, "Y", p)
                    bank = open_bank(key)
                    for t in range(2):
                        for c in range(C):
                            last = pe.transpose(bank[:, (t * C + c) * P:(t * C + c + 1) * P],
                                                ee_b[c][:, 0, (2 * p + t) * P:(2 * p + t + 1) * P], ident)
                    close_bank(key, last)
                elif kind == "kv":
                    t = part
                    v = v_of[g]
                    once("wkv", wkv_loaded, 16)
                    once("pool_setup", pool_setup, 1)
                    if t == 0:
                        pe.wait_ge(ctx_loaded[g], 16 * C)
                    if t < GT:
                        key = (step, "K", t)
                        bank = open_bank(key)
                        for c in range(C):
                            last = pe.matmul(bank[:, :], v[c][:, t * P:(t + 1) * P], wkv[:, c, :],
                                             start=(c == 0), stop=(c == C - 1))
                        close_bank(key, last)
                    if t >= 1:
                        n = g * GT + t - 1
                        pe.wait_ge(k_ready, n + 1)
                        key = (step, "V", t - 1)
                        bank = open_bank(key)
                        for c in range(C):
                            last = pe.matmul(bank[:, c * KVW:(c + 1) * KVW], k_e[n % 2][:, c * P:(c + 1) * P],
                                             v_x[n % 2][:, c, :], start=True, stop=True)
                        close_bank(key, last)
                elif kind == "route" and part == 0:
                    ee_b = ee_b_of[g]
                    once("later", later_loaded, 16)
                    for c in range(C):
                        freed(pe, (("route_in", g), "T", c))
                    key = (step, "Q")
                    bank = open_bank(key)
                    for c in range(C):
                        last = pe.matmul(bank[:, :], wq0[:, c, :], ee_b[c][:, 1, :], start=(c == 0), stop=(c == C - 1))
                    close_bank(key, last)
                elif kind == "route" and part == 1:
                    freed(pe, (step, "Q"))
                    key = (step, "R")
                    bank = open_bank(key)
                    q_t = logits_of[g == 1][:, :, :].rearrange("p a b -> p (a b)")
                    for t in range(GT):
                        last = pe.matmul(bank[:, t * P:(t + 1) * P], q_t[:, t * P:(t + 1) * P],
                                         keys_bd[:, t // 2, :], start=True, stop=True)
                    close_bank(key, last)
                elif kind == "peer_in":
                    rg = MAIN_FIRST[g] // GT
                    once("casts", casts_ready, 1)
                    pe.wait_ge(routes_ready, ROUTE_TURN[rg] + 1)
                    key = (("peer_in", g), "PT")
                    bank = open_bank(key)
                    half_words = bank[0:TOPK + NK, 0:GN // 2].bitcast(BF16)
                    for r in range(4):
                        last = pe.transpose(half_words[:, r * P:(r + 1) * P], picks[:, rg, r, :], identb[:, :])
                    close_bank(key, last)
                    key = (("peer_in", g), "ET")
                    bank = open_bank(key)
                    for r in range(4):
                        last = pe.transpose(bank[0:TOPK + NK + 1, r * P:(r + 1) * P], exps[:, rg, r, :], ident)
                    close_bank(key, last)
                elif kind == "mlp" and part > 0:
                    u = part - 1
                    if u == 0:
                        for c in range(C):
                            freed(pe, (("mlp_in", g), "T", c))
                    if u < MLP_UNITS:
                        n = unit_of(kind, g, u)
                        pe.wait_ge(wsplit_l, n + 1)
                        slot = n % SLOTS
                    if IC <= u < MLP_UNITS:
                        e = u - IC
                        block_up(step, "A", u, slot, lambda c: c)
                        if e == 0:
                            freed(pe, (("peer_in", g), "PT"))
                            freed(pe, (("peer_in", g), "ET"))
                            spread(step, "EY", EC)
                        key = (step, "RANK", u)
                        bank = open_bank(key)
                        last = pe.matmul(bank[:, :], sel_picks[:, e, :], picks_t[:, :], start=True, stop=True)
                        close_bank(key, last)
                        spread(step, ("EX", u), e)
                        if u == MLP_UNITS - 1:
                            last_xt_read[SPLIT_ORDER[("mlp_in", g)]] = (step, "A", u)
                            spread(step, "OVER", EC + 1)
                    elif u < IC:
                        for w, name in enumerate("AB"):
                            block_up(step, name, u, slot, lambda c: 2 * c + w)
                    if u >= LAG:
                        down(kind, g, u - LAG)
                elif kind == "attn":
                    if part == 0:
                        once("attn", attn_loaded, 32)
                        for c in range(C):
                            freed(pe, (("attn_in", g), "T", c))
                    if part < 2:
                        c = part
                        key = (step, "Q", c)
                        bank = open_bank(key)
                        for k in range(C):
                            last = pe.matmul(bank[:, :], wqg[:, k, c * P:(c + 1) * P], xt_f[:, k, :],
                                             start=(k == 0), stop=(k == C - 1))
                        close_bank(key, last)
                    elif part < 4:
                        p = part - 2
                        key = (step, "G", p)
                        bank = open_bank(key)
                        once("bg", bg_ready, 1)
                        both = bank[:, :].rearrange("p (t d) -> p t d", t=2)
                        for n, bias in enumerate((bg_l, bg_h)):
                            pe.matmul(both, one.broadcast_to([1, P]), bias.broadcast_to([1, 2, D]), start=n == 0,
                                      stop=False, skip_group_check=True)
                        for t in range(2):
                            tok = slice((2 * p + t) * P, (2 * p + t + 1) * P)
                            for k in range(C):
                                last = pe.matmul(bank[:, t * D:(t + 1) * D], xt_f[:, k, tok], wqg[:, k, D:], start=False,
                                                 stop=(k == C - 1), skip_group_check=True)
                        close_bank(key, last)
                    elif part < 8:
                        t = part - 4
                        if t == 0:
                            pe.wait_ge(qf_ready, C * (g + 1))
                        b = main_seqs(g)[t]
                        key = (step, "AT", t)
                        bank = open_bank(key)
                        for c in range(C):
                            last = pe.matmul(bank[:, c * KVW:(c + 1) * KVW], q_f[:, c, t * P:(t + 1) * P],
                                             kv_sum[:, b, c * KVW:(c + 1) * KVW], start=True, stop=True)
                        close_bank(key, last)
                    elif part == 8:
                        pe.wait_ge(gated_ready, GT * (g + 1))
                        for c in range(C):
                            key = (step, "T", c)
                            bank = open_bank(key)
                            for t in range(GT):
                                src = gate_s[:, t // 2, (t % 2) * D + c * P:(t % 2) * D + (c + 1) * P]
                                last = pe.transpose(bank[:, t * P:(t + 1) * P], src, ident)
                            close_bank(key, last)
                    else:
                        p = part - 9
                        if p == 0:
                            for c in range(C):
                                freed(pe, (step, "T", c))
                        key = (step, "O", p)
                        bank = open_bank(key)
                        for t in range(2):
                            tok = slice((2 * p + t) * P, (2 * p + t + 1) * P)
                            for c in range(C):
                                last = pe.matmul(bank[:, t * D:(t + 1) * D], er_s[:, c, tok], wo[:, c, :],
                                                 start=(c == 0), stop=(c == C - 1))
                        close_bank(key, last)
                elif kind == "moe" and part == 0:
                    for c in range(C):
                        freed(pe, (("moe_in", g), "T", c))
                    once("gate", bg_ready, 1)
                    key = (step, "S")
                    bank = open_bank(key)
                    for t in range(GT):
                        tok = slice(t * P, (t + 1) * P)
                        for k in range(C):
                            e = slice(k * NE, (k + 1) * NE)
                            last = three_pass(bank[:, t * NE:(t + 1) * NE], xt_h[:, k, tok], xt_l[:, k, tok],
                                              gw_h[:, e], gw_l[:, e], k == 0, k == C - 1)
                    close_bank(key, last)
                elif kind == "moe":
                    u = part - 1
                    if u < MOE_UNITS:
                        n = unit_of(kind, g, u)
                        pe.wait_ge(wsplit_l, n + 1)
                        if u > 1:
                            weigh(step, u)
                        for w, name in enumerate("AB"):
                            key = block_up(step, name, u, n % SLOTS, lambda c: 2 * c + w)
                            if u == 1 and w == 0:
                                pe.wait_ge(scores_ready, g + 1)
                                st = (step, "ST")
                                bank = open_bank(st)
                                for t in range(GT):
                                    last = pe.transpose(bank[0:2 * NE, t * P:(t + 1) * P], s_split[:, t, :].bitcast(F32),
                                                        ident)
                                close_bank(st, last)
                        if u == 1:
                            freed(pe, (step, "ST"))
                            weigh(step, u)
                        if u == MOE_UNITS - 1:
                            last_xt_read[SPLIT_ORDER[("moe_in", g)]] = key
                    if u >= LAG:
                        down(kind, g, u - LAG)

        @block.scalar
        def _(act):
            def split_high(n):
                cols = block_cols(n)
                act.wait_ge(stage_loaded[n % 2], 16 * (n // 2 + 1))
                if n >= SLOTS:
                    act.wait_ge(down_done, n - SLOTS + 1)
                act.activation(ws_h[n % SLOTS][:, 0:cols], stage[n % 2][:, 0:cols], ACT.Copy).then_inc(wsplit_h, 1)

            def hidden_high(n):
                hidden_made(act, n)
                if n >= RING:
                    act.wait_ge(down_done, n - RING + 1)
                act.activation(hid_h[n % RING][:, :], act_s[n % RING][:, :], ACT.Copy).then_inc(hid_high, 1)

            def score_rows(step, g, u):
                bank = full(act, (step, "W", u))
                if u > 2:
                    freed(act, (step, "B", u - 2))
                elif u == 1:
                    hidden_made(act, unit_of("moe", g, 0) - 1)
                act.activation(host_s[:, u % 2, :], bank[:, :], ACT.Copy).then_inc(free_sem((step, "W", u)), 1)

            def cast_consts():
                act.wait_ge(later_loaded, 16)
                act.wait_ge(sel_loaded, 64)
                act.activation(key_iota[:, :, :].rearrange("p a b -> p (a b)"), key_iota_f, ACT.Copy)
                act.activation(rank_w[:, :], rank_f, ACT.Copy)
                act.activation(row_sel[:, :], row_sel_f[0:BG_ROW + 1, :], ACT.Copy)
                act.activation(bg_h, bg_f, ACT.Copy)
                act.activation(gw_h[:, :], gw_f, ACT.Copy)
                act.activation(identb[:, :], ident, ACT.Copy)
                act.activation(sel_picks[:, :, :].rearrange("k c p -> k (c p)"), sel_picks_f, ACT.Copy)
                act.activation(sel_exps[:, :, :].rearrange("k c p -> k (c p)"), sel_exps_f,
                               ACT.Copy).then_inc(casts_ready, 1)

            act.wait_ge(small_loaded, 16)
            act.activation(gates, gates, ACT.Tanh).then_inc(act_setup, 1)
            act.activation(ew[:, :], td, ACT.Exp).then_inc(act_link, 1)
            act.wait_ge(act_link, 1)
            act.activation(ew[:, :], ew[:, :], ACT.Exp, scale=-1.0).then_inc(act_setup, 1)
            for kind, g, part in SCHED:
                step = (kind, g)
                ee_a, ee_b = ee_a_of[g], ee_b_of[g]
                if kind == "wkv_in" and part == 2:
                    if g == 0:
                        act.wait_ge(dve_setup, 1)
                    if g > 1:
                        full(act, (("route", 0 if g == 2 else 2), "Q"))
                    for c in range(C):
                        bank = full(act, (step, "T", c))
                        act.activation(ee_b[c][:, 1, :], bank[:, :], ACT.Exp, bias=bias_b[:, c:c + 1])
                        act.activation(ee_a[c][:, 1, :].rearrange("p (t s) -> p t s", t=GT)[:, :, 1:],
                                       bank[:, :].rearrange("p (t s) -> p t s", t=GT), ACT.Exp,
                                       bias=bias_a[:, c:c + 1]).then_inc(free_sem((step, "T", c)), 1)
                elif kind == "kv" and part < GT:
                    t = part
                    n = g * GT + t
                    bank = full(act, (step, "K", t))
                    if n >= 2:
                        prev = divmod(n - 2, GT)
                        full(act, (("kv", prev[0]), "V", prev[1]))
                    act.activation(k_e[n % 2][:, :], bank[:, 0:D], ACT.Exp)
                    act.activation(k_r[n % 2][:, :], bank[:, 0:D], ACT.Relu)
                    act.activation(v_x[n % 2][:, :, 0:P], bank[:, D:].rearrange("p (c m) -> p c m", c=C),
                                   ACT.Copy).then_inc(free_sem((step, "K", t)), 1)
                elif kind == "split":
                    split_high(part)
                elif kind == "casts" and part == 0:
                    cast_consts()
                elif kind == "route_in" and part == 2:
                    for c in range(C):
                        bank = full(act, (step, "T", c))
                        act.activation(ee_b[c][:, 1, :], bank[:, :], ACT.Copy).then_inc(free_sem((step, "T", c)), 1)
                elif kind == "route" and part == 0:
                    bank = full(act, (step, "Q"))
                    if g > 1:
                        act.wait_ge(routes_ready, ROUTE_TURN[0 if g == 2 else 2] + 1)
                    act.activation(logits_of[g == 1][:, :, :].rearrange("p a b -> p (a b)"), bank[:, :], ACT.Copy).then_inc(free_sem((step, "Q")), 1)
                elif kind == "route" and part == 1:
                    bank = full(act, (step, "R"))
                    act.activation(logits_of[g == 1][:, :, :].rearrange("p a b -> p (a b)"), bank[:, :],
                                   ACT.Copy).then_inc(free_sem((step, "R")), 1)
                elif kind == "route" and part == 4:
                    act.wait_ge(diff_ready, ROUTE_TURN[g] + 1)
                    act.activation(pair_d[:, :, :], pair_d[:, :, :], ACT.Exp)
                    act.activation(exps[:, g, :, 0:TOPK + NK], exps[:, g, :, 0:TOPK + NK], ACT.Exp).then_inc(exp_ready, 1)
                elif kind == "mlp_in" and part == 2 or kind == "moe_in" and part == 3:
                    xt_wait(act, SPLIT_ORDER[step])
                    for c in range(C):
                        bank = full(act, (step, "T", c))
                        act.activation(xt_h[:, c, :], bank[:, :], ACT.Copy).then_inc(high_ready, 1)
                elif kind == "attn_in" and part == 2:
                    for c in range(C):
                        bank = full(act, (step, "T", c))
                        act.activation(xt_f[:, c, :], bank[:, :], ACT.Copy).then_inc(free_sem((step, "T", c)), 1)
                elif kind == "attn" and part < 2:
                    c = part
                    bank = full(act, (step, "Q", c))
                    if c > 0 or g > 0:
                        act.wait_ge(qf_ready, C * g + c)
                    act.activation(er_s[:, 0, :], bank[:, :], ACT.Exp)
                    act.activation(er_s[:, 1, :], bank[:, :], ACT.Relu).then_inc(free_sem((step, "Q", c)), 1)
                elif kind == "attn" and part < 4:
                    p = part - 2
                    bank = full(act, (step, "G", p))
                    act.activation(gate_s[:, p, :], bank[:, :], ACT.Tanh,
                                   scale=0.5).then_inc(free_sem((step, "G", p)), 1)
                elif kind == "attn" and part == 8:
                    for c in range(C):
                        bank = full(act, (step, "T", c))
                        act.activation(er_s[:, c, :], bank[:, :], ACT.Copy).then_inc(free_sem((step, "T", c)), 1)
                elif kind == "moe" and part == 0:
                    bank = full(act, (step, "S"))
                    act.activation(s_e[:, :, :], bank[:, 0:GT * NE].rearrange("p (t e) -> p t e", t=GT), ACT.Exp,
                                   scale=-1.0).then_inc(free_sem((step, "S")), 1)
                elif kind == "peer_in":
                    bank = full(act, (("peer_in", g), "PT"))
                    act.activation(picks_t[:, :], bank[0:TOPK + NK, 0:GN // 2].bitcast(BF16),
                                   ACT.Copy).then_inc(free_sem((("peer_in", g), "PT")), 1)
                    bank = full(act, (("peer_in", g), "ET"))
                    act.activation(exps_t_h[:, :], bank[0:TOPK + NK + 1, :], ACT.Copy).then_inc(exps_high, 1)
                elif kind in ("mlp", "moe") and part > 0:
                    u = part - 1
                    units = host_units(kind)
                    behind = BEHIND[kind]
                    if behind <= u < units + behind:
                        hidden_high(unit_of(kind, g, u - behind))
                    if u < units:
                        n = unit_of(kind, g, u)
                        if kind == "mlp" or u == 0:
                            bank = full(act, (step, "A", u))
                            if n >= RING:
                                act.wait_ge(hid_low, n - RING + 1)
                            elif n == 0:
                                act.wait_ge(bg_ready, 1)
                            act.activation(act_s[n % RING][:, :], bank[:, :], ACT.Tanh, scale=0.5).then_inc(tanh_ready, 1)
                        if kind == "mlp" and u == IC:
                            hidden_made(act, n - 1)
                            bank = full(act, (step, "EY"))
                            act.activation(host_s[:, 0, :], bank[:, :], ACT.Copy).then_inc(free_sem((step, "EY")), 1)
                        if kind == "moe" and u > 0:
                            if u == 1:
                                bank = full(act, (step, "ST"))
                                act.activation(score_t, bank[0:2 * NE, :], ACT.Copy).then_inc(free_sem((step, "ST")), 1)
                            score_rows(step, g, u)
                            freed(act, (step, "A", u))
                            if u > 2:
                                hidden_made(act, n - 2)
                            act.activation(th[n % 2][:, :], act_s[n % RING][:, :], ACT.Tanh,
                                           scale=0.5).then_inc(expert_tanh, 1)
                        if n + 2 < len(ALL_UNITS):
                            split_high(n + 2)

        @block.vector
        def _(dve):
            links = [0]

            def link(ins):
                links[0] += 1
                ins.then_inc(dve_link, 1)
                dve.wait_ge(dve_link, links[0])

            def free(key, ins):
                ins.then_inc(free_sem(key), 1)
                freed(dve, key)

            def moments(step, seqs):
                n = STATS_ORDER[step] % 2
                keep = step[0] == "route_in"
                for t, b in enumerate(seqs):
                    last = dve.bn_stats(stats[:, n, t, :], x_nat[:, b, :])
                link(last)
                for t, b in enumerate(seqs):
                    out = mean_rstd[:, b, :] if keep else mv[:, n, t, :]
                    last = dve.bn_aggr(out, stats[:, n, t, :])
                link(last)
                for p in range(2):
                    b = seqs[2 * p]
                    var = mean_rstd[:, b:b + 2, 1] if keep else mv[:, n, 2 * p:2 * p + 2, 1]
                    last = dve.tensor_scalar(var_eps[:, n, 2 * p:2 * p + 2], var, LN_EPS, None, ALU.add)
                last.then_inc(var_ready, 1)

            def normalize(step, seqs):
                n = XN_ORDER[step]
                if n >= 2:
                    prev = [s for s, k in XN_ORDER.items() if k == n - 2][0]
                    full(dve, (prev, "T", C - 1))
                if step in STATS_ORDER:
                    o = STATS_ORDER[step]
                    dve.wait_ge(rstd_ready, o + 1)
                if step[0] == "route_in":
                    for p in range(2):
                        b = seqs[2 * p]
                        last = dve.tensor_copy(rstd2[:, b:b + 2], rstd[:, o % 2, 2 * p:2 * p + 2])
                    link(last)
                for t, b in enumerate(seqs):
                    if step[0] in ("route_in", "mlp_in"):
                        m, r = mean_rstd[:, b, 0:1], rstd2[:, b:b + 1]
                    else:
                        m, r = mv[:, o % 2, t, 0:1], rstd[:, o % 2, t:t + 1]
                    last = dve.tensor_scalar(xn[n % 2][:, t, :], x_nat[:, b, :], m, r, ALU.subtract, ALU.mult)
                last.then_inc(xn_ready, 1)

            def residual(out, bank, gate):
                return dve.scalar_tensor_tensor(out, bank, gates[:, gate:gate + 1], out, ALU.mult, ALU.add)

            def scale_expert(step, g, u):
                n = unit_of("moe", g, u)
                dve.wait_ge(hid_low, n - RING + 1)
                freed(dve, (step, "W", u))
                bank = full(dve, (step, "A", u))
                dve.tensor_tensor(act_s[n % RING][:, :], bank[:, :], host_s[:, u % 2, :],
                                  ALU.mult).then_inc(free_sem((step, "A", u)), 1)

            for kind, g, part in SCHED:
                step = (kind, g)
                ee_a, ee_b, logits = ee_a_of[g], ee_b_of[g], logits_of[g == 1]
                seqs = main_seqs(g) if kind in ("mlp_in", "attn_in", "moe_in") else prep_seqs(g)
                if kind == "setup":
                    dve.wait_ge(small_loaded, 16)
                    link(dve.tensor_scalar(bias_a[:, :], tf, 0.0, -1.0, ALU.max, ALU.mult))
                    link(dve.tensor_scalar(bias_b[:, :], tf, U_LEAST, None, ALU.max))
                    dve.tensor_tensor(bias_b[:, :], bias_b[:, :], bias_a[:, :], ALU.add).then_inc(dve_setup, 1)
                    dve.wait_ge(act_setup, 2)
                    dve.wait_ge(pool_setup, 1)
                    dve.tensor_scalar(gates[:, 1::2], gates[:, 1::2], 0.5, None, ALU.mult)
                    for c in range(C):
                        last = dve.tensor_copy(decay[:, c, :].rearrange("p (t j) -> p t j", t=GT)[:, :, 1:],
                                               ew[:, c:c + 1].unsqueeze(2).broadcast_to([P, GT, P]))
                    link(last)
                elif step in STATS_ORDER and part == 0:
                    if kind == "wkv_in":
                        dve.wait_ge(x_loaded[g], 32)
                    moments(step, seqs)
                elif APPLY.get(kind) == part:
                    normalize(step, seqs)
                elif kind == "casts" and part == 1:
                    dve.wait_ge(casts_ready, 1)
                    dve.tensor_tensor(gw_l[:, :], gw_f, gw_h[:, :].bitcast(F32), ALU.subtract)
                    dve.tensor_tensor(bg_l, bg_f, bg_h.bitcast(F32), ALU.subtract).then_inc(bg_ready, 1)
                elif kind == "wkv_out" and part < 6:
                    if part < 2:
                        c = part
                        if g > 0 or c > 0:
                            dve.wait_ge(ev_ready, C * g + c)
                        for s in range(2):
                            a = ee_a[c][:, s, :]
                            last = dve.tensor_tensor_scan(a, decay[:, c, :], a, 0.0, ALU.mult, ALU.add)
                        last.then_inc(scanned, 1)
                    else:
                        c, half = divmod(part - 2, 2)
                        den = ee_b[c][:, 1, half * GN // 2:(half + 1) * GN // 2]
                        if half == 0:
                            past = ee_a[c][:, 1, :].rearrange("p (t j) -> p t j", t=GT)[:, :, 0:P]
                            own = ee_b[c][:, 1, :].rearrange("p (t j) -> p t j", t=GT)
                            dve.wait_ge(scanned, C * g + c + 1)
                            link(dve.tensor_tensor(own, past, own, ALU.add))
                        last = dve.reciprocal(den, den)
                        if half:
                            last.then_inc(recip_ready, 1)
                elif step == ("wkv_in", 0) and part == 2:
                    weigh_values(dve, 0, 0).then_inc(first_values, 1)
                    dve.wait_ge(first_values, 1)
                elif kind == "wkv_out":
                    p = part - 6
                    bank = full(dve, (step, "Y", p))
                    b = seqs[2 * p]
                    free((step, "Y", p), residual(x_nat[:, b:b + 2, :].rearrange("p t d -> p (t d)"), bank[:, :], 0))
                elif kind == "kv":
                    t = part
                    if t < GT:
                        n = g * GT + t
                        freed(dve, (step, "K", t))
                        dve.scalar_tensor_tensor(k_e[n % 2][:, :], k_e[n % 2][:, :], 1.0, k_r[n % 2][:, :], ALU.min,
                                                 ALU.add).then_inc(k_ready, 1)
                    if t > 0:
                        bank = full(dve, (step, "V", t - 1))
                        if g == 0:
                            dve.wait_ge(later_loaded, 16)
                        free((step, "V", t - 1), dve.tensor_tensor(
                            kv_sum[:, seqs[t - 1], :].rearrange("p (c m) -> p c m", c=C),
                            bank[:, 0:C * KVW].rearrange("p (c m) -> p c m", c=C),
                            head_mask.unsqueeze(1).broadcast_to([P, C, KVW]), ALU.mult))
                elif kind == "route" and part == 2:
                    freed(dve, (step, "R"))
                    for r in range(8):
                        last = dve.max(top_v[:, r, :], logits[:, r, :])
                    link(last)
                elif kind == "route" and part == 3:
                    for r in range(8):
                        last = dve.max_index(top_i[:, r, :], top_v[:, r, :], logits[:, r, :])
                    pr = pairs[:, :, :].rearrange("p r (i j) -> p r i j", i=TOPK)
                    link(dve.tensor_tensor(pr, top_v[:, 0:4, :].unsqueeze(3).broadcast_to([P, 4, TOPK, TOPK]),
                                           top_v[:, 4:8, :].unsqueeze(2).broadcast_to([P, 4, TOPK, TOPK]), ALU.add))
                    for r in range(4):
                        last = dve.max(pair_top[:, r, :], pairs[:, r, :])
                    link(last)
                elif kind == "route" and part == 4:
                    for r in range(4):
                        dve.match_replace(pair_rep[:, r, :], pair_top[:, r, :], pairs[:, r, :], LOWEST)
                    dve.tensor_tensor(pair_d[:, :, :], pairs[:, :, :],
                                      pair_top[:, :, 0:1].broadcast_to([P, 4, TOPK * TOPK]), ALU.subtract)
                    dve.tensor_tensor(exps[:, g, :, 0:TOPK], logits[:, 0:4, 0:TOPK],
                                      top_v[:, 0:4, 0:1].broadcast_to([P, 4, TOPK]), ALU.subtract)
                    dve.tensor_tensor(exps[:, g, :, TOPK:TOPK + NK], logits[:, 4:8, :],
                                      top_v[:, 4:8, 0:1].broadcast_to([P, 4, NK]), ALU.subtract).then_inc(diff_ready, 1)
                    dve.wait_ge(diff_ready, ROUTE_TURN[g] + 1)
                elif kind == "route" and part == 5:
                    dve.tensor_copy(ix_f[:, :, :], top_i[:, 0:4, :])
                    dve.tensor_copy(iy_b[:, :, :], top_i[:, 4:8, :])
                    link(dve.tensor_tensor(pair_rep[:, :, :], pairs[:, :, :], pair_rep[:, :, :], ALU.not_equal))
                    pm = pair_rep[:, :, :].rearrange("p r (i j) -> p r i j", i=TOPK)
                    link(dve.tensor_reduce(r_cnt[:, :, :], pm, AX_X, ALU.add))
                    hot = pairs[:, :, :].rearrange("p r (i j) -> p r i j", i=TOPK)
                    table = iota8.unsqueeze(1).broadcast_to([P, 4, TOPK, TOPK])
                    link(dve.tensor_tensor(hot, ix_f[:, :, :].unsqueeze(2).broadcast_to([P, 4, TOPK, TOPK]), table,
                                           ALU.is_equal))
                    link(dve.tensor_tensor(hot, hot, r_cnt[:, :, :].unsqueeze(2).broadcast_to([P, 4, TOPK, TOPK]),
                                           ALU.mult))
                    with nc.allow_low_precision("counts up to 8 are exact in bfloat16"):
                        link(dve.tensor_reduce(picks[:, g, :, 0:TOPK], hot, AX_X, ALU.add))
                elif kind == "route" and part in (6, 7):
                    dve.wait_ge(casts_ready, 1)
                    a = part - 6
                    oh = onehot[:, :, :, :].rearrange("p h k j -> p (h k) j")
                    for h in range(2):
                        iy = iy_b[:, 2 * a + h, :].unsqueeze(1).broadcast_to([P, NK, TOPK])
                        last = dve.tensor_tensor(onehot[:, h, :, :], iy, key_iota[:, :, :], ALU.is_equal)
                    link(last)
                    rw = rank_w[:, :].unsqueeze(1).broadcast_to([P, 2 * NK, TOPK])
                    link(dve.tensor_tensor(oh, oh, rw, ALU.mult))
                    with nc.allow_low_precision("ranks up to 8 are exact in bfloat16"):
                        link(dve.tensor_reduce(picks[:, g, 2 * a:2 * a + 2, TOPK:], onehot[:, :, :, :], AX_X, ALU.add))
                elif kind == "route" and part == 8:
                    dve.wait_ge(exp_ready, ROUTE_TURN[g] + 1)
                    link(dve.tensor_tensor(pair_d[:, :, :], pair_d[:, :, :], pair_rep[:, :, :], ALU.mult))
                    pd = pair_d[:, :, :].rearrange("p r (i j) -> p r i j", i=TOPK)
                    link(dve.tensor_reduce(r_sum[:, :, :], pd, AX_X, ALU.add))
                    link(dve.tensor_reduce(r_z[:, :], r_sum[:, :, :], AX_X, ALU.add))
                    link(dve.reciprocal(r_z[:, :], r_z[:, :]))
                    zb = r_z[:, :].unsqueeze(2).broadcast_to([P, 4, TOPK])
                    dve.tensor_tensor(exps[:, g, :, 0:TOPK], exps[:, g, :, 0:TOPK], zb, ALU.mult)
                    link(dve.tensor_tensor(r_sum[:, :, :], r_sum[:, :, :], zb, ALU.mult))
                    link(dve.scalar_tensor_tensor(r_sum[:, :, :], ix_f[:, :, :], float(NEXP // NK), r_sum[:, :, :],
                                                  ALU.is_ge, ALU.mult))
                    dve.tensor_reduce(exps[:, g, :, TOPK + NK], r_sum[:, :, :], AX_X, ALU.add).then_inc(routes_ready, 1)
                    dve.wait_ge(routes_ready, ROUTE_TURN[g] + 1)
                elif kind == "mlp_in" and part == 2 or kind == "moe_in" and part == 3:
                    n = SPLIT_ORDER[step]
                    for c in range(C):
                        dve.wait_ge(high_ready, C * n + c + 1)
                        bank = full(dve, (step, "T", c))
                        dve.tensor_tensor(xt_l[:, c, :], bank[:, :], xt_h[:, c, :].bitcast(F32),
                                          ALU.subtract).then_inc(free_sem((step, "T", c)), 1)
                elif kind == "peer_in":
                    dve.wait_ge(exps_high, g + 1)
                    bank = full(dve, (("peer_in", g), "ET"))
                    dve.tensor_tensor(exps_t_l[:, :], bank[0:TOPK + NK + 1, :], exps_t_h[:, :].bitcast(F32),
                                      ALU.subtract).then_inc(free_sem((("peer_in", g), "ET")), 1)
                elif kind == "mlp" and 1 <= part <= MLP_UNITS:
                    u = part - 1
                    n = unit_of(kind, g, u)
                    s = act_s[n % RING]
                    dve.wait_ge(tanh_ready, TANHS[(kind, g, u)])
                    bank = full(dve, (step, "A", u))
                    free((step, "A", u), dve.scalar_tensor_tensor(s[:, :], s[:, :], 1.0, bank[:, :], ALU.add, ALU.mult))
                    if u >= IC:
                        if u == IC:
                            freed(dve, (step, "EY"))
                        w = host_s[:, 1, :]
                        bank = full(dve, (step, "RANK", u))
                        free((step, "RANK", u), dve.scalar_tensor_tensor(w, bank[:, :], float(TOPK), host_s[:, 0, :],
                                                                         ALU.is_gt, ALU.mult))
                        bank = full(dve, (step, ("EX", u)))
                        free((step, ("EX", u)), dve.tensor_tensor(w, w, bank[:, :], ALU.mult))
                        if u == MLP_UNITS - 1:
                            bank = full(dve, (step, "OVER"))
                            free((step, "OVER"), dve.tensor_tensor(w, w, bank[:, :], ALU.add))
                        for a in range(2):
                            r = slice(a * 2 * P, (a + 1) * 2 * P)
                            last = dve.tensor_tensor(s[:, r].rearrange("p (j h) -> p h j", h=2),
                                                     s[:, r].rearrange("p (j h) -> p h j", h=2),
                                                     w[:, r].rearrange("p (h j) -> p h j", h=2), ALU.mult)
                        last.then_inc(hid_ready, 1)
                    else:
                        bank = full(dve, (step, "B", u))
                        free((step, "B", u), dve.tensor_tensor(s[:, :], bank[:, :], s[:, :], ALU.mult))
                elif kind in ("mlp_out", "moe_out"):
                    host = HOSTS.index((kind[:3], g))
                    dve.wait_ge(down_done, unit_of(kind[:3], g, host_units(kind[:3])))
                    for p in range(2):
                        b = main_seqs(g)[2 * p]
                        residual(x_nat[:, b:b + 2, :], acc[p][:, :, :], 1 if kind == "mlp_out" else 3).then_inc(acc_free, 1)
                    dve.wait_ge(acc_free, 2 * (host + 1))
                elif kind == "attn" and part < 2:
                    c = part
                    freed(dve, (step, "Q", c))
                    dve.scalar_tensor_tensor(q_f[:, c, :], er_s[:, 0, :], 1.0, er_s[:, 1, :], ALU.min,
                                             ALU.add).then_inc(qf_ready, 1)
                elif kind == "attn" and 4 <= part < 8:
                    t = part - 4
                    freed(dve, (step, "G", t // 2))
                    bank = full(dve, (step, "AT", t))
                    sums = bank[:, 0:C * KVW].rearrange("p (c m) -> p c m", c=C)
                    z = z_den[:, :].rearrange("p (c m) -> p c m", c=C)
                    link(dve.tensor_scalar(z, sums[:, :, P:], Z_EPS, 2.0, ALU.add, ALU.mult))
                    link(dve.reciprocal(z_den[:, :], z_den[:, :]))
                    for c in range(C):
                        last = dve.tensor_tensor(
                            att[t % 2][:, c * P:(c + 1) * P].rearrange("p (h d) -> p h d", h=HC),
                            bank[:, c * KVW:c * KVW + P].rearrange("p (h d) -> p h d", h=HC),
                            z_den[:, c * HC:(c + 1) * HC].unsqueeze(2).broadcast_to([P, HC, HD]), ALU.mult)
                    free((step, "AT", t), last)
                    gate = gate_s[:, t // 2, (t % 2) * D:(t % 2 + 1) * D]
                    dve.scalar_tensor_tensor(gate, gate, 1.0, att[t % 2][:, :], ALU.add, ALU.mult).then_inc(gated_ready, 1)
                elif kind == "attn" and part > 8:
                    p = part - 9
                    bank = full(dve, (step, "O", p))
                    b = main_seqs(g)[2 * p]
                    free((step, "O", p), residual(x_nat[:, b:b + 2, :].rearrange("p t d -> p (t d)"), bank[:, :], 2))
                elif kind == "moe" and part == 0:
                    freed(dve, (step, "S"))
                    link(dve.tensor_scalar(s_b[:, :, :], s_e[:, :, :], 1.0, None, ALU.add))
                    link(dve.reciprocal(s_b[:, :, :], s_b[:, :, :]))
                    link(dve.tensor_tensor(s_m[:, :, :], s_b[:, :, :],
                                           e_bias.unsqueeze(1).broadcast_to([P, GT, NE]), ALU.add))
                    for t in range(GT):
                        last = dve.max(s_top[:, t, :], s_m[:, t, :])
                    link(last)
                    for t in range(GT):
                        last = dve.max_index(s_idx[:, t, :], s_top[:, t, :], s_m[:, t, :])
                    link(last)
                    link(dve.tensor_copy(s_if[:, :, :], s_idx[:, :, 0:2]))
                    tab = iota_e.unsqueeze(1).broadcast_to([P, GT, NE])
                    dve.tensor_tensor(s_m[:, :, :], tab, s_if[:, :, 0:1].broadcast_to([P, GT, NE]), ALU.is_equal)
                    link(dve.tensor_tensor(s_e[:, :, :], tab, s_if[:, :, 1:2].broadcast_to([P, GT, NE]),
                                           ALU.is_equal))
                    link(dve.tensor_tensor(s_m[:, :, :], s_m[:, :, :], s_e[:, :, :], ALU.add))
                    link(dve.tensor_tensor(s_e[:, :, :], s_m[:, :, :], s_b[:, :, :], ALU.mult))
                    link(dve.tensor_copy(s_split[:, :, 0:NE], s_e[:, :, :]))
                    dve.tensor_tensor(s_split[:, :, NE:], s_e[:, :, :], s_split[:, :, 0:NE].bitcast(F32),
                                      ALU.subtract).then_inc(scores_ready, 1)
                    dve.wait_ge(scores_ready, g + 1)
                elif kind == "moe" and part <= MOE_UNITS + 1:
                    u = part - 1
                    if u == 0:
                        a = act_s[unit_of(kind, g, u) % RING]
                        dve.wait_ge(tanh_ready, TANHS[(kind, g, u)])
                        bank = full(dve, (step, "A", u))
                        free((step, "A", u), dve.scalar_tensor_tensor(a[:, :], a[:, :], 1.0, bank[:, :], ALU.add,
                                                                      ALU.mult))
                        bank = full(dve, (step, "B", u))
                        free((step, "B", u), dve.tensor_tensor(a[:, :], bank[:, :], a[:, :], ALU.mult))
                    if u > 1:
                        u -= 1
                        n = unit_of(kind, g, u)
                        a, h = act_s[n % RING], th[n % 2]
                        dve.wait_ge(expert_tanh, NE * g + u)
                        link(dve.scalar_tensor_tensor(a[:, :], h[:, :], 1.0, a[:, :], ALU.add, ALU.mult))
                        bank = full(dve, (step, "B", u))
                        free((step, "B", u), dve.tensor_tensor(h[:, :], bank[:, :], host_s[:, u % 2, :], ALU.mult))
                        dve.tensor_tensor(a[:, :], a[:, :], h[:, :], ALU.mult).then_inc(hid_ready, 1)
                    if 0 < part - 1 < MOE_UNITS:
                        scale_expert(step, g, part - 1)

        @block.gpsimd
        def _(pool):
            def split_low(n):
                cols = block_cols(n)
                pool.wait_ge(wsplit_h, n + 1)
                pool.tensor_tensor(ws_l[n % SLOTS][:, 0:cols], stage[n % 2][:, 0:cols],
                                   ws_h[n % SLOTS][:, 0:cols].bitcast(F32), ALU.subtract).then_inc(wsplit_l, 1)

            pool.memset(minus_half[:, :], -0.5)
            for k in range(2):
                pool.memset(v_x[k][:, :, P:], 1.0)
            for c in range(C):
                pool.memset(decay[:, c, :].rearrange("p (t j) -> p t j", t=GT)[:, :, 0:1], 0.0)
                for ee_a in (main_a, pads):
                    last = pool.memset(ee_a[c][:, :, :].rearrange("p s (t j) -> p s t j", t=GT)[:, :, :, 0:1], 0.0)
            last.then_inc(pool_setup, 1)
            pool.wait_ge(pool_setup, 1)
            for kind, g, part in SCHED:
                step = (kind, g)
                ee_a, ee_b, v = ee_a_of[g], ee_b_of[g], v_of[g]
                if step in STATS_ORDER and part == 0:
                    n = STATS_ORDER[step]
                    pool.wait_ge(var_ready, n + 1)
                    pool.tensor_tensor(rstd[:, n % 2, :], var_eps[:, n % 2, :], minus_half[:, :],
                                       ALU.pow).then_inc(rstd_ready, 1)
                elif kind == "wkv_in" and part == 2:
                    for c in range(g == 0, C):
                        weigh_values(pool, g, c).then_inc(ev_ready, 1)
                elif kind == "wkv_out" and part == 1:
                    for c in range(C):
                        past = ee_a[c][:, 0, :].rearrange("p (t j) -> p t j", t=GT)[:, :, 0:P]
                        own = ee_b[c][:, 0, :].rearrange("p (t j) -> p t j", t=GT)
                        pool.wait_ge(scanned, C * g + c + 1)
                        pool.tensor_tensor(own, past, own, ALU.add).then_inc(past_added, 1)
                elif kind == "wkv_out" and part in (3, 5):
                    c = part // 2 - 1
                    pool.wait_ge(past_added, C * g + c + 1)
                    pool.wait_ge(recip_ready, C * g + c + 1)
                    pool.tensor_tensor(ee_b[c][:, 0, :], ee_b[c][:, 0, :], ee_b[c][:, 1, :],
                                       ALU.mult).then_inc(y_ready, 1)
                elif kind == "split":
                    split_low(part)
                elif kind in ("mlp", "moe") and part > 0:
                    u = part - 1
                    units = host_units(kind)
                    behind = BEHIND[kind]
                    if behind <= u < units + behind:
                        n = unit_of(kind, g, u - behind)
                        k = n % RING
                        pool.wait_ge(hid_high, n + 1)
                        pool.tensor_tensor(hid_l[k][:, :], act_s[k][:, :], hid_h[k][:, :].bitcast(F32),
                                           ALU.subtract).then_inc(hid_low, 1)
                    if u < units and unit_of(kind, g, u) + 2 < len(ALL_UNITS):
                        split_low(unit_of(kind, g, u) + 2)

        @block.sync
        def _(sp):
            def load_x(g):
                for p in range(2):
                    b = prep_seqs(g)[2 * p]
                    sp.dma_start(x_nat[:, b:b + 2, :],
                                 io["x"][b:b + 2].rearrange("b p d -> p b d")).then_inc(x_loaded[g], 16)

            def load_block(n):
                if n >= len(ALL_UNITS):
                    return
                if n >= 2:
                    sp.wait_ge(wsplit_l, n - 1)
                sp.dma_start(stage[n % 2][:, 0:block_cols(n)], block_source(n)).then_inc(stage_loaded[n % 2], 16)

            def load_ctx(g):
                for c in range(C):
                    sp.dma_start(v_of[g][c][:, :], io["ctx_t"][g, :, c, :]).then_inc(ctx_loaded[g], 16)

            load_x(0)
            sp.dma_start(small[:, :], io["small"]).then_inc(small_loaded, 16)
            load_ctx(0)
            load_x(1)
            sp.dma_start(wkv[:, :, :], io["wkv"]).then_inc(wkv_loaded, 16)
            load_ctx(1)
            load_block(0)
            load_block(1)
            sp.dma_start(later[:, :], io["later"]).then_inc(later_loaded, 16)
            for dst, name in ((key_iota_f, "key_iota"), (sel_picks_f, "sel_picks"), (sel_exps_f, "sel_exps"),
                              (bg_f, "bg")):
                sp.dma_start(dst, io[name]).then_inc(sel_loaded, 16)
            stores = 0
            for kind, g, part in SCHED:
                step = (kind, g)
                if step == ("kv", 0) and part == GT:
                    sp.wait_ge(first_values, 1)
                    sp.wait_ge(ev_ready, C - 1)
                    full(sp, (step, "K", GT - 1))
                    load_ctx(2)
                    load_x(2)
                    load_x(3)
                elif step == ("wkv_out", 2) and part == 0:
                    sp.wait_ge(ev_ready, C * 3 - 1)
                    full(sp, (("kv", 2), "K", GT - 1))
                    load_ctx(3)
                elif step == ("kv", 1) and part == GT:
                    sp.dma_start(wqg[:, :, :], io["wqg"]).then_inc(attn_loaded, 16)
                    sp.dma_start(wo[:, :, :], io["wo"]).then_inc(attn_loaded, 16)
                elif kind == "split":
                    load_block(part + 2)
                elif kind in ("mlp", "moe") and 1 <= part <= host_units(kind):
                    load_block(unit_of(kind, g, part - 1) + 4)
                if kind == "moe_out":
                    sp.wait_ge(acc_free, 2 * (HOSTS.index(("moe", g)) + 1))
                    for p in range(2):
                        b = main_seqs(g)[2 * p]
                        sp.dma_start(io["out"][b:b + 2].rearrange("b p d -> p b d"),
                                     x_nat[:, b:b + 2, :]).then_inc(out_stored, 16)
                        stores += 1
            sp.wait_ge(out_stored, 16 * stores)


def kernel(**inputs):
    import numpy as np
    import concourse.bacc as bacc
    from concourse.bass_utils import run_bass_kernel_spmd

    a = {k: np.asarray(v) for k, v in inputs.items()}

    def chunked(w):
        return np.ascontiguousarray(w.reshape(-1, P, w.shape[-1]).transpose(1, 0, 2))

    def blocks(ups, down):
        up = np.stack(ups).reshape(len(ups), C, P, -1, P).transpose(3, 2, 1, 0, 4)
        return np.concatenate([up.reshape(-1, P, C * len(ups) * P), down.reshape(-1, P, D)], 2)

    def everywhere(v):
        return np.ascontiguousarray(np.broadcast_to(v, (P,) + v.shape))

    ctx_t = a["ctx_2048"].transpose(2, 0, 1)
    ctx_g = np.stack([ctx_t[:, prep_seqs(g), :].reshape(C, P, GN).transpose(1, 0, 2) for g in range(NG)])
    keys = a["L0_ffn_keys"]
    keys_bd = np.zeros((P, 2, 2 * NK), keys.dtype)
    for h in range(2):
        keys_bd[h * NK:(h + 1) * NK, :, h * NK:(h + 1) * NK] = keys.transpose(1, 0, 2)
    w1 = np.concatenate([a["L1_ffn_sw1"][None], a["L1_ffn_w1"]])
    w3 = np.concatenate([a["L1_ffn_sw3"][None], a["L1_ffn_w3"]])
    w2 = np.concatenate([a["L1_ffn_sw2"][None], a["L1_ffn_w2"]])
    head = np.arange(P) // HD
    mask = np.concatenate([head[:, None] == head[None, :], head[:, None] == np.arange(HC)[None, :]], 1)
    f32 = np.float32
    sel_picks = np.zeros((TOPK + NK, EC, P), f32)
    sel_exps = np.zeros((TOPK + NK + 1, EC + 2, P), f32)
    for p in range(P):
        for c in range(EC):
            sel_picks[c * P // NK + p // NK, c, p] = sel_exps[c * P // NK + p // NK, c, p] = 1
            sel_picks[TOPK + p % NK, c, p] = 1
        sel_exps[TOPK + p % NK, EC, p] = 1
    sel_exps[TOPK + NK, EC + 1, P - 1] = 1
    score_rows = np.zeros((P, NE), f32)
    for p in range(2 * NE):
        score_rows[p, p % NE] = 1
    score_rows[BG_ROW] = 1
    arrays = {
        "x": a["x"],
        "ctx_t": ctx_g,
        "small": np.concatenate([
            np.eye(P, dtype=f32), a["L0_xattn_time_decay"].reshape(C, P).T, a["L0_xattn_time_first"].reshape(C, P).T,
            everywhere(np.stack([a["g_xattn"], a["g_ffn"]], 1).reshape(-1))], 1),
        "later": np.concatenate([
            mask.astype(f32), everywhere(np.repeat(np.arange(TOPK, dtype=f32), TOPK)),
            everywhere(np.arange(NE, dtype=f32)), everywhere(a["L1_ffn_expert_bias"]),
            everywhere(TOPK - np.arange(TOPK, dtype=f32)), score_rows, chunked(a["L1_ffn_gate_w"].T).reshape(P, -1),
            chunked(a["L0_ffn_W_q"]).reshape(P, -1),
            keys_bd.reshape(P, -1)], 1),
        "key_iota": everywhere(np.repeat(np.arange(NK, dtype=f32), TOPK)),
        "sel_picks": sel_picks.reshape(TOPK + NK, -1),
        "sel_exps": sel_exps.reshape(TOPK + NK + 1, -1),
        "bg": a["L1_xattn_bg"][None, None],
        "wkv": chunked(a["L1_xattn_Wkv"].T),
        "wo": chunked(a["L1_xattn_Wo"].T),
        "w_mlp": blocks([a["L0_ffn_gate_w"], a["L0_ffn_up_w"]], a["L0_ffn_down_w"]),
        "w_peer": blocks([a["L0_ffn_down_embed"].T], a["L0_ffn_up_embed"]),
        "wqg": chunked(np.concatenate([a["L1_xattn_Wq"].T, a["L1_xattn_Wg"].T], 1)),
        "w_moe": np.concatenate([blocks([x1.T, x3.T], x2.T) for x1, x3, x2 in zip(w1, w3, w2)]),
    }
    nc = bacc.Bacc("TRN2", target_bir_lowering=False, num_devices=1)
    io, feeds = {}, {}
    for name, v in arrays.items():
        v = np.ascontiguousarray(v)
        feeds[f"in_{name}"] = v
        io[name] = nc.dram_tensor(f"in_{name}", v.shape, mybir.dt.from_np(v.dtype), kind="ExternalInput").ap()
    io["out"] = nc.dram_tensor("out_x", (NSEQ, P, D), F32, kind="ExternalOutput").ap()
    build(nc, io)
    r = run_bass_kernel_spmd(nc, [feeds], core_ids=[0])
    return r.results[0]["out_x"]
```
